# Optimizing a Trainium2 kernel written in Bass

```python
import numpy as np
import jax
import jax.numpy as jnp

def _softmax(x, axis=-1):
    return jax.nn.softmax(x, axis=axis)

def _gelu(x):
    return jax.nn.gelu(x, approximate=True)

def _silu(x):
    return jax.nn.silu(x)

def _sigmoid(x):
    return jax.nn.sigmoid(x)

def _layernorm(x, axis=-1, eps=1e-05):
    m = jnp.mean(x, axis=axis, keepdims=True)
    v = jnp.var(x, axis=axis, keepdims=True)
    return (x - m) / jnp.sqrt(v + eps)

def _scatter_add(tgt, idx, src, axis=0):
    return tgt.at[idx].add(src)

def _segment_sum(src, seg, n):
    return jax.ops.segment_sum(src, seg, n)
kernel_name = 'mk_decoder_postln_d1_seqx_r4_039735'

def setup_inputs(seed: int=0):
    np.random.seed(seed)
    _w = jnp.asarray

    def _rec_inputs():
        import jax
        import jax.numpy as jnp
        _rk = jax.random.key(seed)
        x = -0.0005207 + 1.001 * jax.random.normal(jax.random.fold_in(_rk, 1), (8, 512, 256), jnp.float32)
        _lenS = 512 - jax.random.randint(jax.random.fold_in(_rk, 7), (8,), 0, max(1, 512 // 4) + 1, jnp.int32)
        _lenS2 = 1024 - jax.random.randint(jax.random.fold_in(_rk, 8), (8,), 0, max(1, 1024 // 4) + 1, jnp.int32)
        _ctx_1024P = jax.random.normal(jax.random.fold_in(_rk, 11), (8, 16, 256), jnp.float32)
        _ctx_1024c = jax.random.dirichlet(jax.random.fold_in(_rk, 511), 0.3 * jnp.ones((16,), jnp.float32), (8, 1024))
        _ctx_1024t = jnp.einsum('bsk,bkd->bsd', _ctx_1024c, _ctx_1024P)
        _ctx_1024t = _ctx_1024t * jax.lax.rsqrt(jnp.mean(jnp.square(_ctx_1024t)) + 1e-12) * 0.953939
        ctx_1024 = -1.52775e-05 + 0.999936 * (_ctx_1024t + 0.3 * jax.random.normal(jax.random.fold_in(_rk, 611), (8, 1024, 256), jnp.float32))
        return (x, ctx_1024)
    x, ctx_1024 = _rec_inputs()

    def _L0_attn_setup():
        import jax, jax.numpy as jnp
        import numpy as np
        S, B, D = (512, 2, 256)
        H, HD = (16, 64)
        SCALE = 1.0 / HD ** 0.5
        key = jax.random.key(seed)
        ks = jax.random.split(key, 7)
        std = 1.0 / np.sqrt(D)
        return {'inputs': jax.random.normal(ks[0], (S, B, D), dtype=jnp.float32), 'Wkv': jax.random.uniform(ks[1], (D, 2 * H * HD), jnp.float32, -std, std), 'bkv': jax.random.uniform(ks[2], (2 * H * HD,), jnp.float32, -std, std), 'Wq': jax.random.uniform(ks[3], (D, H * HD), jnp.float32, -std, std), 'bq': jax.random.uniform(ks[4], (H * HD,), jnp.float32, -std, std), 'Wp': jax.random.uniform(ks[5], (H * HD, D), jnp.float32, -std, std), 'bp': jax.random.uniform(ks[6], (D,), jnp.float32, -std, std)}
    _L0_attn_all = _L0_attn_setup()
    _L0_attn_in = {k: v for k, v in _L0_attn_all.items() if k in ('Wkv', 'bkv', 'Wq', 'bq', 'Wp', 'bp')}
    del _L0_attn_all

    def _L0_xattn_setup():
        import jax, jax.numpy as jnp
        import numpy as np
        DIM = 256
        HEADS = 16
        DHEAD = 64
        INNER = HEADS * DHEAD
        EPS = 1e-05

        def layer_norm(x, g, b):
            mu = jnp.mean(x, axis=-1, keepdims=True)
            var = jnp.mean(jnp.square(x - mu), axis=-1, keepdims=True)
            return (x - mu) * jax.lax.rsqrt(var + EPS) * g + b

        def apply_rope(x, cos, sin):
            d2 = x.shape[-1] // 2
            x1, x2 = (x[..., :d2], x[..., d2:])
            return jnp.concatenate([x1 * cos - x2 * sin, x2 * cos + x1 * sin], axis=-1)
        key = jax.random.key(seed)
        ks = jax.random.split(key, 10)
        B, N, S = (8, 64, 1024)
        latents = jax.random.normal(ks[0], (B, N, DIM), dtype=jnp.float32)
        context = jax.random.normal(ks[1], (B, S, DIM), dtype=jnp.float32)
        cos = jax.random.uniform(ks[2], (S, DHEAD // 2), dtype=jnp.float32)
        sin = jax.random.uniform(ks[3], (S, DHEAD // 2), dtype=jnp.float32)
        init = lambda k, shp, fan_in: jax.random.normal(k, shp, dtype=jnp.float32) / np.sqrt(fan_in)
        return {'latents': latents, 'context': context, 'cos': cos, 'sin': sin, 'ln_lat_g': jnp.ones((DIM,), jnp.float32), 'ln_lat_b': jnp.zeros((DIM,), jnp.float32), 'ln_ctx_g': jnp.ones((DIM,), jnp.float32), 'ln_ctx_b': jnp.zeros((DIM,), jnp.float32), 'Wq': init(ks[4], (DIM, INNER), DIM), 'Wkv': init(ks[5], (DIM, 2 * INNER), DIM), 'Wo': init(ks[6], (INNER, DIM), INNER), 'bo': jnp.zeros((DIM,), jnp.float32)}
    _L0_xattn_all = _L0_xattn_setup()
    _L0_xattn_in = {k: v for k, v in _L0_xattn_all.items() if k in ('cos', 'sin', 'ln_lat_g', 'ln_lat_b', 'ln_ctx_g', 'ln_ctx_b', 'Wq', 'Wkv', 'Wo', 'bo')}
    del _L0_xattn_all

    def _L0_ffn_setup():
        import jax, jax.numpy as jnp
        import numpy as np
        B, S, D = (2, 512, 256)
        H = 512
        E = 8
        K = 2
        HS = 512 * 1
        SCALE = 1.0 / float(np.sqrt(D))
        key = jax.random.key(seed)
        ks = jax.random.split(key, 9)
        init = 0.02
        return {'x': jax.random.normal(ks[0], (B, S, D), dtype=jnp.float32), 'Wr': jax.random.normal(ks[1], (D, E), dtype=jnp.float32) * init, 'rb': jnp.zeros((E,), dtype=jnp.float32), 'W1': jax.random.normal(ks[2], (E, D, H), dtype=jnp.float32) * init, 'W2': jax.random.normal(ks[3], (E, H, D), dtype=jnp.float32) * init, 'W3': jax.random.normal(ks[4], (E, D, H), dtype=jnp.float32) * init, 'Ws1': jax.random.normal(ks[5], (D, HS), dtype=jnp.float32) * init, 'Ws2': jax.random.normal(ks[6], (HS, D), dtype=jnp.float32) * init, 'Ws3': jax.random.normal(ks[7], (D, HS), dtype=jnp.float32) * init}
    _L0_ffn_all = _L0_ffn_setup()
    _L0_ffn_in = {k: v for k, v in _L0_ffn_all.items() if k in ('Wr', 'rb', 'W1', 'W2', 'W3', 'Ws1', 'Ws2', 'Ws3')}
    del _L0_ffn_all
    return {'x': x, 'ctx_1024': ctx_1024, 'L0_attn_Wkv': _L0_attn_in['Wkv'], 'L0_attn_bkv': _L0_attn_in['bkv'], 'L0_attn_Wq': _L0_attn_in['Wq'], 'L0_attn_bq': _L0_attn_in['bq'], 'L0_attn_Wp': _L0_attn_in['Wp'], 'L0_attn_bp': _L0_attn_in['bp'], 'L0_xattn_cos': _L0_xattn_in['cos'], 'L0_xattn_sin': _L0_xattn_in['sin'], 'L0_xattn_ln_lat_g': _L0_xattn_in['ln_lat_g'], 'L0_xattn_ln_lat_b': _L0_xattn_in['ln_lat_b'], 'L0_xattn_ln_ctx_g': _L0_xattn_in['ln_ctx_g'], 'L0_xattn_ln_ctx_b': _L0_xattn_in['ln_ctx_b'], 'L0_xattn_Wq': _L0_xattn_in['Wq'], 'L0_xattn_Wkv': _L0_xattn_in['Wkv'], 'L0_xattn_Wo': _L0_xattn_in['Wo'], 'L0_xattn_bo': _L0_xattn_in['bo'], 'L0_ffn_Wr': _L0_ffn_in['Wr'], 'L0_ffn_rb': _L0_ffn_in['rb'], 'L0_ffn_W1': _L0_ffn_in['W1'], 'L0_ffn_W2': _L0_ffn_in['W2'], 'L0_ffn_W3': _L0_ffn_in['W3'], 'L0_ffn_Ws1': _L0_ffn_in['Ws1'], 'L0_ffn_Ws2': _L0_ffn_in['Ws2'], 'L0_ffn_Ws3': _L0_ffn_in['Ws3']}

def reference(x, ctx_1024, L0_attn_Wkv, L0_attn_bkv, L0_attn_Wq, L0_attn_bq, L0_attn_Wp, L0_attn_bp, L0_xattn_cos, L0_xattn_sin, L0_xattn_ln_lat_g, L0_xattn_ln_lat_b, L0_xattn_ln_ctx_g, L0_xattn_ln_ctx_b, L0_xattn_Wq, L0_xattn_Wkv, L0_xattn_Wo, L0_xattn_bo, L0_ffn_Wr, L0_ffn_rb, L0_ffn_W1, L0_ffn_W2, L0_ffn_W3, L0_ffn_Ws1, L0_ffn_Ws2, L0_ffn_Ws3):
    import jax
    import jax.numpy as jnp

    def _L0_attn_ref(inputs, Wkv, bkv, Wq, bq, Wp, bp):
        import jax, jax.numpy as jnp
        import numpy as np
        S, B, D = (512, 2, 256)
        H, HD = (16, 64)
        SCALE = 1.0 / HD ** 0.5
        s, b, _ = inputs.shape
        kv = inputs @ Wkv + bkv
        k, v = jnp.split(kv, 2, axis=-1)
        q = inputs @ Wq + bq
        k = k.reshape(s, b, H, HD)
        q = q.reshape(s, b, H, HD)
        v = v.reshape(s, b, H, HD)
        attn = jnp.einsum('sbhd,tbhd->bhst', q, k) * SCALE
        attn = jax.nn.softmax(attn, axis=-1)
        attn_vec = jnp.einsum('bhst,tbhd->sbhd', attn, v)
        attn_vec = attn_vec.reshape(s, b, H * HD)
        return attn_vec @ Wp + bp

    def _L0_xattn_ref(latents, context, cos, sin, ln_lat_g, ln_lat_b, ln_ctx_g, ln_ctx_b, Wq, Wkv, Wo, bo):
        import jax, jax.numpy as jnp
        import numpy as np
        DIM = 256
        HEADS = 16
        DHEAD = 64
        INNER = HEADS * DHEAD
        EPS = 1e-05

        def layer_norm(x, g, b):
            mu = jnp.mean(x, axis=-1, keepdims=True)
            var = jnp.mean(jnp.square(x - mu), axis=-1, keepdims=True)
            return (x - mu) * jax.lax.rsqrt(var + EPS) * g + b

        def apply_rope(x, cos, sin):
            d2 = x.shape[-1] // 2
            x1, x2 = (x[..., :d2], x[..., d2:])
            return jnp.concatenate([x1 * cos - x2 * sin, x2 * cos + x1 * sin], axis=-1)
        b, n, _ = latents.shape
        s = context.shape[1]
        lat = layer_norm(latents, ln_lat_g, ln_lat_b)
        ctx = layer_norm(context, ln_ctx_g, ln_ctx_b)
        q = (lat @ Wq).reshape(b, n, HEADS, DHEAD).transpose(0, 2, 1, 3)
        kv = ctx @ Wkv
        k, v = jnp.split(kv, 2, axis=-1)
        k = k.reshape(b, s, HEADS, DHEAD).transpose(0, 2, 1, 3)
        v = v.reshape(b, s, HEADS, DHEAD).transpose(0, 2, 1, 3)
        k = apply_rope(k, cos[None, None], sin[None, None])
        scale = DHEAD ** (-0.5)
        attn = jnp.einsum('bhnd,bhsd->bhns', q, k) * scale
        attn = jnp.clip(attn, -11.0, 11.0)
        attn = jax.nn.softmax(attn, axis=-1)
        out = jnp.einsum('bhns,bhsd->bhnd', attn, v)
        out = out.transpose(0, 2, 1, 3).reshape(b, n, INNER)
        return out @ Wo + bo

    def _L0_ffn_ref(x, Wr, rb, W1, W2, W3, Ws1, Ws2, Ws3):
        import jax, jax.numpy as jnp
        import numpy as np
        B, S, D = (2, 512, 256)
        H = 512
        E = 8
        K = 2
        HS = 512 * 1
        SCALE = 1.0 / float(np.sqrt(D))
        logits = jnp.einsum('bsd,de->bse', x, Wr) * SCALE
        _, idx = jax.lax.top_k(logits + rb, K)
        gathered = jnp.take_along_axis(logits, idx, axis=-1)
        w = jax.nn.softmax(gathered, axis=-1)
        w_full = jnp.sum(jax.nn.one_hot(idx, E, dtype=x.dtype) * w[..., None], axis=-2)
        h = jnp.einsum('bsd,edh->bseh', x, W1) * jax.nn.silu(jnp.einsum('bsd,edh->bseh', x, W3))
        expert_out = jnp.einsum('bseh,ehd->bsed', h, W2)
        out = jnp.einsum('bsed,bse->bsd', expert_out, w_full)
        hs = jnp.einsum('bsd,dh->bsh', x, Ws1) * jax.nn.silu(jnp.einsum('bsd,dh->bsh', x, Ws3))
        out = out + jnp.einsum('bsh,hd->bsd', hs, Ws2)
        return out
    x = _layernorm(x + _L0_attn_ref(x, L0_attn_Wkv, L0_attn_bkv, L0_attn_Wq, L0_attn_bq, L0_attn_Wp, L0_attn_bp), axis=-1)
    x = _layernorm(x + _L0_xattn_ref(x, ctx_1024, L0_xattn_cos, L0_xattn_sin, L0_xattn_ln_lat_g, L0_xattn_ln_lat_b, L0_xattn_ln_ctx_g, L0_xattn_ln_ctx_b, L0_xattn_Wq, L0_xattn_Wkv, L0_xattn_Wo, L0_xattn_bo), axis=-1)
    x = _layernorm(x + _L0_ffn_ref(x, L0_ffn_Wr, L0_ffn_rb, L0_ffn_W1, L0_ffn_W2, L0_ffn_W3, L0_ffn_Ws1, L0_ffn_Ws2, L0_ffn_Ws3), axis=-1)
    return x

_drawn_inputs = setup_inputs


def setup_inputs(seed=0):
    import zlib

    import numpy as np

    out = dict(_drawn_inputs(seed))
    spreads = {'L0_xattn_ln_lat_g': (1.0, 0.6),
     'L0_xattn_ln_lat_b': (0.0, 0.65),
     'L0_xattn_ln_ctx_g': (1.0, 0.2),
     'L0_xattn_ln_ctx_b': (0.0, 0.1),
     'L0_xattn_bo': (0.0, 0.1),
     'L0_ffn_rb': (0.0, 0.417)}
    factors = {'L0_attn_bq': 8.0,
     'L0_xattn_cos': 5.764,
     'L0_xattn_sin': 5.726,
     'L0_ffn_Wr': 7.468,
     'L0_ffn_W1': 3.363,
     'L0_ffn_W2': 3.362,
     'L0_ffn_W3': 3.397,
     'L0_ffn_Ws1': 3.009,
     'L0_ffn_Ws2': 2.985,
     'L0_ffn_Ws3': 3.021}
    for name, (base, spread) in spreads.items():
        noise = np.random.default_rng([zlib.crc32(name.encode()), seed]).standard_normal(out[name].shape)
        drawn = base * np.exp(spread * noise) if base else spread * noise
        out[name] = jnp.asarray(drawn.astype(out[name].dtype))
    for name, factor in factors.items():
        out[name] = (out[name] * factor).astype(out[name].dtype)
    return out
```

```python
import math
from contextlib import ExitStack

import concourse.bass as bass
from concourse import mybir

P = 128
F32 = mybir.dt.float32
F32R = mybir.dt.float32r
BF16 = mybir.dt.bfloat16
U32 = mybir.dt.uint32
ALU = mybir.AluOpType
ACT = mybir.ActivationFunctionType
AX = mybir.AxisListType
EPS = 1e-5

S, B, D = 8, 512, 256
H, HD = 16, 64
INNER = H * HD
CTX = 1024
SCALE = float(HD) ** -0.5
CLIP = 11.0
E, FF = 8, 512
KD = D // P
PAIRS = H // 2


class Slots:

    def __init__(self, order, weight=None, silent=()):
        self.at, self.uses, self.fills, self.fill_at = {}, {}, {}, {}
        for key, slot in order:
            self.at[key] = (slot, self.uses.get(slot, 0))
            self.uses[slot] = self.uses.get(slot, 0) + 1
            if key[0] not in silent:
                self.fill_at[key] = self.fills.get(slot, 0)
                self.fills[slot] = self.fills.get(slot, 0) + 1
        self.weight = weight or {}

    def slot(self, key):
        return self.at[key][0]

    def filled(self, key, i):
        return i * self.fills[self.slot(key)] + (self.fill_at[key] + 1)

    def free(self, key, i):
        slot, k = self.at[key]
        w = self.weight.get(slot, 1)
        return i * (self.uses[slot] * w) + k * w

    def drained(self, key, i):
        slot, k = self.at[key]
        w = self.weight.get(slot, 1)
        return i * (self.uses[slot] * w) + (k + 1) * w


def split_weights(nc, ctx, name, parts):
    with ExitStack() as c:
        raw = c.enter_context(nc.sbuf_tensor(f"{name}_raw", [P, 2, 2048], F32))
        loaded = [c.enter_context(nc.semaphore(f"{name}_loaded{k}")) for k in range(2)]
        hi_done = c.enter_context(nc.semaphore(f"{name}_hi_done"))
        lo_done = c.enter_context(nc.semaphore(f"{name}_lo_done"))
        with nc.Block() as block:

            @block.sync
            def _(sp):
                for n, (src, hi, lo) in enumerate(parts):
                    if n >= 2:
                        sp.wait_ge(lo_done, n - 1)
                    w = hi.shape[1]
                    sp.dma_start(raw[:, n % 2, 0:w].rearrange("p (a n) -> p a n", a=src.shape[1]), src
                                 ).then_inc(loaded[n % 2], 16)

            @block.scalar
            def _(act):
                for n, (src, hi, lo) in enumerate(parts):
                    act.wait_ge(loaded[n % 2], 16 * (n // 2 + 1))
                    act.activation(hi, raw[:, n % 2, 0:hi.shape[1]], ACT.Copy).then_inc(hi_done, 1)

            @block.vector
            def _(dve):
                for n, (src, hi, lo) in enumerate(parts):
                    dve.wait_ge(hi_done, n + 1)
                    dve.tensor_tensor(lo, raw[:, n % 2, 0:hi.shape[1]], hi.bitcast(F32), ALU.subtract
                                      ).then_inc(lo_done, 1)


def three_terms(w_hi, w_lo, x_hi, x_lo):
    return ((w_hi, x_hi), (w_hi, x_lo), (w_lo, x_hi))


def self_attention(nc, x, Wkv, bkv, Wq, bq, Wp, bp, x1_dram, ident, identb):
    CH, TT, BI = 8, 4, 16
    BIG = 1e30
    with ExitStack() as ctx:
        def sb(name, shape, dt=F32):
            return ctx.enter_context(nc.sbuf_tensor(name, shape, dt))

        def sem(name):
            return ctx.enter_context(nc.semaphore(name))

        wq = [sb(f"a_wq_{n}", [P, KD * INNER], F32R) for n in "hl"]
        wk = [sb(f"a_wk_{n}", [P, KD * INNER], F32R) for n in "hl"]
        wv = [sb(f"a_wv_{n}", [P, KD * INNER], F32R) for n in "hl"]
        wp = [sb(f"a_wp_{n}", [P, PAIRS * D], F32R) for n in "hl"]
        kv = Wkv.rearrange("(k p) n -> p k n", p=P)
        parts = []
        for (hi, lo), src in ((wk, kv[:, :, 0:INNER]), (wq, Wq.rearrange("(k p) n -> p k n", p=P)),
                              (wv, kv[:, :, INNER:2 * INNER]), (wp, Wp.rearrange("(k p) n -> p k n", p=P))):
            parts.append((src, hi[:, :], lo[:, :]))
        split_weights(nc, ctx, "a_w", parts)

        mneg = sb("a_mneg", [P, P], BF16)
        ident4 = sb("a_ident4", [P, 4, P], BF16)
        same16 = sb("a_same16", [P, BI])
        bq_sb = sb("a_bq", [P, PAIRS])
        bk_sb = sb("a_bk", [P, PAIRS])
        bv_sb = sb("a_bv", [P, INNER])
        bp_sb = sb("a_bp", [P, D])
        mhalf = sb("a_mhalf", [P, TT])
        xt = sb("a_xt", [P, 2, TT, D])
        xT = [sb(f"a_xT_{n}", [P, KD, TT * P], F32R) for n in "hl"]
        QT = sb("a_QT", [P, PAIRS, TT * P])
        KB = sb("a_KB", [P, PAIRS, TT, 2 * P])
        V = sb("a_V", [P, TT, INNER])
        Sc = sb("a_Sc", [P, 2, H, S])
        mx = sb("a_mx", [P, H])
        den = sb("a_den", [P, H])
        Pe = sb("a_Pe", [P, H, P])
        PT = sb("a_PT", [P, H, P])
        OT = [sb(f"a_OT_{n}", [P, PAIRS, P], F32R) for n in "hl"]
        y = sb("a_y", [P, 2, D])
        st = sb("a_st", [P, 6])
        mv = sb("a_mv", [P, 2])
        ve = sb("a_ve", [P, 1])
        rs = sb("a_rs", [P, 1])
        x1t = sb("a_x1t", [P, 2, TT, D])
        ps = ctx.enter_context(nc.psum_tensor("a_ps", [P, 8, 512], F32))

        order = [(("x", k), 6 + k) for k in range(KD)]
        order += [(("proj", n), n % 4) for n in range(24)]
        n = 24

        def s_group(t):
            nonlocal n
            out = []
            for q in range(4):
                out.append((("s", t, q), n % 4))
                n += 1
            return out

        turn = [0]

        def ring45(key):
            turn[0] += 1
            return key, 4 + (turn[0] - 1) % 2

        order += s_group(0)
        for t in range(TT):
            if t + 1 < TT:
                order += s_group(t + 1)
            order += [ring45(("pt", t, q)) for q in range(4)]
            order += [(("o", t, k), 6 + k) for k in range(2)]
            order.append(ring45(("y", t)))
        assert turn[0] % 2 == 0 and n % 4 == 0
        slots = Slots(order)
        filled = [sem(f"a_filled{i}") for i in range(8)]
        drained = [sem(f"a_drained{i}") for i in range(8)]
        consts = sem("a_consts")
        consts_in = sem("a_consts_in")
        x_in = [sem(f"a_x_in{k}") for k in range(2)]
        xh = sem("a_xh")
        xl = sem("a_xl")
        compact = sem("a_compact")
        exped = sem("a_exped")
        probs = sem("a_probs")
        spread = sem("a_spread")
        oth = sem("a_oth")
        otl = sem("a_otl")
        biased = sem("a_biased")
        var_ready = sem("a_var_ready")
        rstd_ready = sem("a_rstd_ready")
        x1_ready = sem("a_x1_ready")
        stats_taken = sem("a_stats_taken")
        stored = [sem(f"a_stored{k}") for k in range(2)]
        dchain = sem("a_dchain")

        def wait_filled(eng, key, c):
            eng.wait_ge(filled[slots.slot(key)], slots.filled(key, c))

        def wait_free(eng, key, c):
            eng.wait_ge(drained[slots.slot(key)], slots.free(key, c))

        def bank(key):
            return ps[:, slots.slot(key), :]

        with nc.Block() as block:

            @block.sync
            def _(sp):
                sp.dma_start(bq_sb[:, :], bq.rearrange("(c p) -> p c", p=P),
                             allow_slow_non_contiguous=True).then_inc(consts_in, 16)
                sp.dma_start(bk_sb[:, :], bkv[0:INNER].rearrange("(c p) -> p c", p=P),
                             allow_slow_non_contiguous=True).then_inc(consts_in, 16)
                sp.dma_start(bv_sb[:, :], bkv[INNER:2 * INNER].partition_broadcast(P)).then_inc(consts_in, 16)
                sp.dma_start(bp_sb[:, :], bp.partition_broadcast(P)).then_inc(consts_in, 16)

                def load(half, c):
                    for s in range(S):
                        src = x[s].rearrange("(c t b) d -> c b t d", t=TT, b=BI)[bass.ds(c, 1)]
                        sp.dma_start(xt[BI * s:BI * s + BI, half], src.rearrange("c b t d -> (c b) t d")
                                     ).then_inc(x_in[half], 16)

                def store(half, c):
                    for s in range(S):
                        dst = x1_dram[s].rearrange("(c t b) d -> c b t d", t=TT, b=BI)[bass.ds(c, 1)]
                        sp.dma_start(dst.rearrange("c b t d -> (c b) t d"), x1t[BI * s:BI * s + BI, half]
                                     ).then_inc(stored[half], 16)

                load(0, 0)
                with sp.Fori(0, CH // 2) as i:
                    sp.wait_ge(x1_ready, (2 * i) * TT)
                    load(1, 2 * i + 1)
                    sp.wait_ge(x1_ready, (2 * i + 1) * TT)
                    store(0, 2 * i)
                    load(0, (2 * i + 2) % CH)
                    sp.wait_ge(x1_ready, (2 * i + 2) * TT)
                    store(1, 2 * i + 1)
                for half in range(2):
                    sp.wait_ge(stored[half], 16 * S * (CH // 2))
                sp.wait_ge(x_in[0], 16 * S * (CH // 2 + 1))

            @block.gpsimd
            def _(pool):
                pool.memset(mneg[:, :], -BIG).then_inc(consts, 1)
                pool.memset(same16[:, :], 0.0).then_inc(consts, 1)
                pool.memset(mhalf[:, :], -0.5).then_inc(consts, 1)
                pool.memset(KB[:, :, :, :], 0.0).then_inc(consts, 1)
                pool.wait_ge(consts, 4)
                k = 4
                for a in range(-(S - 1), S):
                    pool.affine_select(out=mneg[:, :], in_=mneg[:, :], compare_op=ALU.not_equal, fill=0.0,
                                       base=-BI * a, pattern=[[-1, P]], channel_multiplier=1).then_inc(consts, 1)
                    k += 1
                    pool.wait_ge(consts, k)
                for a in range(S):
                    pool.affine_select(out=same16[:, :], in_=same16[:, :], compare_op=ALU.not_equal, fill=1.0,
                                       base=-BI * a, pattern=[[-1, BI]], channel_multiplier=1).then_inc(consts, 1)
                    k += 1
                    pool.wait_ge(consts, k)
                for a in range(4):
                    pool.tensor_copy(ident4[:, a, :], identb[:, :]).then_inc(consts, 1)
                pool.wait_ge(consts_in, 64)
                with pool.Fori(0, CH // 2) as i:
                    for half in range(2):
                        c = 2 * i + half
                        wait_filled(pool, ("x", 1), c)
                        for t in range(TT):
                            pool.tensor_tensor(xt[:, half, t], xt[:, half, t], bp_sb[:, :], ALU.add
                                               ).then_inc(biased, 1)
                        for t in range(TT):
                            pool.wait_ge(probs, c * TT + t + 1)
                            wait_filled(pool, ("pt", t - 1, 3) if t else ("x", 0), c)
                            pool.tensor_tensor(
                                Pe[:, :, :].rearrange("p h (t b) -> p (h t) b", b=BI),
                                Sc[:, t % 2].rearrange("p h t -> p (h t)").unsqueeze(2).broadcast_to([P, H * S, BI]),
                                same16[:, :].unsqueeze(1).broadcast_to([P, H * S, BI]), ALU.mult
                            ).then_inc(spread, 1)
                            if t:
                                pool.wait_ge(var_ready, c * TT + t)
                                pool.tensor_tensor(rs[:, :], ve[:, :], mhalf[:, 0:1], ALU.pow).then_inc(rstd_ready, 1)
                        pool.wait_ge(var_ready, c * TT + TT)
                        pool.tensor_tensor(rs[:, :], ve[:, :], mhalf[:, 0:1], ALU.pow).then_inc(rstd_ready, 1)

            def chunk(pe, i, c, half):
                pe.wait_ge(x_in[half], (i + 1) * (16 * S))
                for k in range(KD):
                    wait_free(pe, ("x", k), c)
                    for t in range(TT):
                        mm = pe.transpose(bank(("x", k))[:, t * P:(t + 1) * P], xt[:, half, t, k * P:(k + 1) * P],
                                          ident[:, :])
                    mm.then_inc(filled[6 + k], 1)
                pe.wait_ge(xl, (c + 1) * KD)
                for n in range(24):
                    wait_free(pe, ("proj", n), c)
                    if n < 16:
                        w = wk if n < 8 else wq
                        col = (n % 8) * P
                        terms = [t for k in range(KD) for t in three_terms(
                            w[0][:, k * INNER + col:k * INNER + col + P], w[1][:, k * INNER + col:k * INNER + col + P],
                            xT[0][:, k, :], xT[1][:, k, :])]
                    else:
                        t, h2 = (n - 16) // 2, (n - 16) % 2
                        cols = [slice(k * INNER + h2 * 512, k * INNER + h2 * 512 + 512) for k in range(KD)]
                        terms = [u for k in range(KD) for u in three_terms(
                            xT[0][:, k, t * P:(t + 1) * P], xT[1][:, k, t * P:(t + 1) * P],
                            wv[0][:, cols[k]], wv[1][:, cols[k]])]
                    for a, (lhsT, rhs) in enumerate(terms):
                        mm = pe.matmul(bank(("proj", n)), lhsT, rhs, start=(a == 0), stop=(a == len(terms) - 1))
                    mm.then_inc(filled[slots.slot(("proj", n))], 1)

                def scores(t):
                    for q in range(4):
                        key = ("s", t, q)
                        wait_free(pe, key, c)
                        if t == 0 and q == 0:
                            for n in range(20, 24):
                                pe.wait_ge(drained[n % 4], slots.drained(("proj", n), c))
                        pe.matmul(bank(key), mneg[:, :], ident4[:, :, :].rearrange("p a b -> p (a b)"),
                                  start=True, stop=True)
                        for a in range(2):
                            pair = 2 * q + a
                            mm = pe.matmul(bank(key)[:, a * 256:(a + 1) * 256], QT[:, pair, t * P:(t + 1) * P],
                                           KB[:, pair, t, :], start=False, stop=True, skip_group_check=True)
                        mm.then_inc(filled[slots.slot(key)], 1)

                scores(0)
                for t in range(TT):
                    if t + 1 < TT:
                        scores(t + 1)
                    pe.wait_ge(spread, c * TT + t + 1)
                    for q in range(4):
                        key = ("pt", t, q)
                        wait_free(pe, key, c)
                        for a in range(4):
                            mm = pe.transpose(bank(key)[:, a * P:(a + 1) * P], Pe[:, 4 * q + a, :], ident[:, :])
                        mm.then_inc(filled[slots.slot(key)], 1)
                    for k in range(2):
                        key = ("o", t, k)
                        wait_free(pe, key, c)
                        for q in (2 * k, 2 * k + 1):
                            pe.wait_ge(drained[slots.slot(("pt", t, q))], slots.drained(("pt", t, q), c))
                        for pair in range(4 * k, 4 * k + 4):
                            for hh in range(2):
                                h = 2 * pair + hh
                                mm = pe.matmul(bank(key)[hh * HD:(hh + 1) * HD, (pair % 4) * P:(pair % 4 + 1) * P],
                                               V[:, t, h * HD:(h + 1) * HD], PT[:, h, :], start=True, stop=True)
                        mm.then_inc(filled[6 + k], 1)
                    key = ("y", t)
                    wait_free(pe, key, c)
                    pe.wait_ge(otl, (c * TT + t) * 2 + 2)
                    a = 0
                    for pair in range(PAIRS):
                        for lhsT, rhs in three_terms(OT[0][:, pair, :], OT[1][:, pair, :],
                                                     wp[0][:, pair * D:(pair + 1) * D], wp[1][:, pair * D:(pair + 1) * D]):
                            mm = pe.matmul(bank(key)[:, 0:D], lhsT, rhs, start=(a == 0), stop=(a == 3 * PAIRS - 1))
                            a += 1
                    mm.then_inc(filled[slots.slot(key)], 1)

            @block.tensor
            def _(pe):
                pe.wait_ge(consts, 4 + 15 + 8 + 4)
                with pe.Fori(0, CH // 2) as i:
                    for half in range(2):
                        chunk(pe, i, 2 * i + half, half)

            @block.scalar
            def _(act):
                act.wait_ge(consts_in, 64)
                with act.Fori(0, CH) as c:
                    for k in range(KD):
                        wait_filled(act, ("x", k), c)
                        act.activation(xT[0][:, k, :], bank(("x", k)), ACT.Copy).then_inc(xh, 1)
                    for n in range(8, 16):
                        wait_filled(act, ("proj", n), c)
                        act.activation(QT[:, n - 8, :], bank(("proj", n)), ACT.Identity, bias=bq_sb[:, n - 8:n - 7]
                                       ).then_inc(drained[slots.slot(("proj", n))], 1)
                    for t in range(TT):
                        act.wait_ge(compact, c * TT + t + 1)
                        act.activation(Sc[:, t % 2], Sc[:, t % 2], ACT.Exp, scale=SCALE).then_inc(exped, 1)
                        for q in range(4):
                            key = ("pt", t, q)
                            wait_filled(act, key, c)
                            if q == 0 and t:
                                wait_filled(act, ("o", t - 1, 1), c)
                            act.activation(PT[:, 4 * q:4 * q + 4, :].rearrange("p h n -> p (h n)"), bank(key), ACT.Copy
                                           ).then_inc(drained[slots.slot(key)], 1)
                        for k in range(2):
                            key = ("o", t, k)
                            wait_filled(act, key, c)
                            if k == 0 and t:
                                wait_filled(act, ("y", t - 1), c)
                            act.activation(OT[0][:, 4 * k:4 * k + 4, :].rearrange("p h n -> p (h n)"), bank(key),
                                           ACT.Copy).then_inc(oth, 1)

            @block.vector
            def _(dve):
                LINKS = 5 * TT
                dve.wait_ge(consts, 4 + 15 + 8 + 4)
                dve.wait_ge(consts_in, 64)
                with dve.Fori(0, CH // 2) as i:
                    for half in range(2):
                        c = 2 * i + half
                        made = [0]

                        def link(ins):
                            made[0] += 1
                            ins.then_inc(dchain, 1)
                            dve.wait_ge(dchain, c * LINKS + made[0])

                        for k in range(KD):
                            dve.wait_ge(xh, c * KD + k + 1)
                            ins = dve.tensor_tensor(xT[1][:, k, :], bank(("x", k)), xT[0][:, k, :].bitcast(F32),
                                                    ALU.subtract)
                            ins.then_inc(xl, 1)
                            dve.wait_ge(xl, c * KD + k + 1)
                            dve.sem_inc(drained[6 + k], 1)
                        for n in range(8):
                            wait_filled(dve, ("proj", n), c)
                            for hh in range(2):
                                ins = dve.tensor_scalar(
                                    KB[hh * HD:(hh + 1) * HD, n, :, hh * P:(hh + 1) * P],
                                    bank(("proj", n))[hh * HD:(hh + 1) * HD].rearrange("p (t n) -> p t n", t=TT),
                                    bk_sb[hh * HD:(hh + 1) * HD, n:n + 1], None, ALU.add)
                            ins.then_inc(drained[slots.slot(("proj", n))], 1)
                        for n in range(16, 24):
                            wait_filled(dve, ("proj", n), c)
                            t, h2 = (n - 16) // 2, (n - 16) % 2
                            dve.tensor_tensor(V[:, t, h2 * 512:(h2 + 1) * 512], bank(("proj", n)),
                                              bv_sb[:, h2 * 512:(h2 + 1) * 512], ALU.add
                                              ).then_inc(drained[slots.slot(("proj", n))], 1)

                        def compact_scores(t):
                            for q in range(4):
                                key = ("s", t, q)
                                wait_filled(dve, key, c)
                                ins = dve.tensor_reduce(Sc[:, t % 2, 4 * q:4 * q + 4, :].rearrange("p h t -> p (h t)"),
                                                        bank(key).rearrange("p (a b) -> p a b", b=BI), AX.X, ALU.max)
                                if q < 3:
                                    ins.then_inc(drained[slots.slot(key)], 1)
                            ins.then_inc(drained[slots.slot(key)], 1)
                            dve.wait_ge(drained[slots.slot(key)], slots.drained(key, c))
                            link(dve.tensor_reduce(mx[:, :], Sc[:, t % 2], AX.X, ALU.max))
                            dve.tensor_tensor(Sc[:, t % 2], Sc[:, t % 2], mx[:, :].unsqueeze(2).broadcast_to([P, H, S]),
                                              ALU.subtract).then_inc(compact, 1)

                        def normalise(t):
                            dve.wait_ge(exped, c * TT + t + 1)
                            link(dve.tensor_reduce(den[:, :], Sc[:, t % 2], AX.X, ALU.add))
                            link(dve.reciprocal(den[:, :], den[:, :]))
                            dve.tensor_tensor(Sc[:, t % 2], Sc[:, t % 2], den[:, :].unsqueeze(2).broadcast_to([P, H, S]),
                                              ALU.mult).then_inc(probs, 1)

                        def lo_of_o(t):
                            for k in range(2):
                                dve.wait_ge(oth, (c * TT + t) * 2 + k + 1)
                                dve.tensor_tensor(OT[1][:, 4 * k:4 * k + 4, :].rearrange("p h n -> p (h n)"),
                                                  bank(("o", t, k)),
                                                  OT[0][:, 4 * k:4 * k + 4, :].rearrange("p h n -> p (h n)").bitcast(F32),
                                                  ALU.subtract).then_inc(otl, 1)
                                dve.wait_ge(otl, (c * TT + t) * 2 + k + 1)
                                dve.sem_inc(drained[6 + k], 1)

                        def residual(t):
                            wait_filled(dve, ("y", t), c)
                            dve.wait_ge(biased, c * TT + t + 1)
                            ins = dve.tensor_tensor(y[:, t % 2], bank(("y", t))[:, 0:D], xt[:, half, t], ALU.add)
                            slot = slots.slot(("y", t))
                            ins.then_inc(drained[slot], 1)
                            dve.wait_ge(drained[slot], slots.drained(("y", t), c))
                            link(dve.bn_stats(st[:, :], y[:, t % 2]))
                            dve.sem_inc(stats_taken, 1)
                            link(dve.bn_aggr(mv[:, :], st[:, :]))
                            dve.tensor_scalar(ve[:, :], mv[:, 1:2], EPS, None, ALU.add).then_inc(var_ready, 1)

                        def norm(t):
                            dve.wait_ge(rstd_ready, c * TT + t + 1)
                            if t == 0:
                                dve.wait_ge(stored[half], i * (16 * S))
                            dve.tensor_scalar(x1t[:, half, t], y[:, t % 2], mv[:, 0:1], rs[:, :], ALU.subtract,
                                              ALU.mult).then_inc(x1_ready, 1)

                        compact_scores(0)
                        normalise(0)
                        for t in range(TT):
                            if t + 1 < TT:
                                compact_scores(t + 1)
                            if t:
                                residual(t - 1)
                            lo_of_o(t)
                            if t:
                                norm(t - 1)
                            if t + 1 < TT:
                                normalise(t + 1)
                        residual(TT - 1)
                        norm(TT - 1)
                        assert made[0] == LINKS


def cross_attention(nc, x1_dram, context, cos, sin, lg, lb, cg, cb, Wq, Wkv, Wo, bo, x2_dram, ident, identr):
    NT, CT = B // P, CTX // P
    HG, PG = H // 2, PAIRS // 2
    LO, HI = math.exp(-CLIP), math.exp(CLIP)
    with ExitStack() as ctx:
        def sb(name, shape, dt=F32):
            return ctx.enter_context(nc.sbuf_tensor(name, shape, dt))

        def sem(name):
            return ctx.enter_context(nc.semaphore(name))

        wq = [sb(f"b_wq_{n}", [P, KD * INNER], F32R) for n in "hl"]
        wk = [sb(f"b_wk_{n}", [P, KD * INNER], F32R) for n in "hl"]
        wv = [sb(f"b_wv_{n}", [P, KD * INNER], F32R) for n in "hl"]
        wo = [sb(f"b_wo_{n}", [P, PAIRS * D], F32R) for n in "hl"]
        kv = Wkv.rearrange("(k p) n -> p k n", p=P)
        parts = []
        for (hi, lo), src in ((wk, kv[:, :, 0:INNER]), (wv, kv[:, :, INNER:2 * INNER]),
                              (wq, Wq.rearrange("(k p) n -> p k n", p=P)), (wo, Wo.rearrange("(k p) n -> p k n", p=P))):
            parts.append((src, hi[:, :], lo[:, :]))
        split_weights(nc, ctx, "b_w", parts)

        cos_sb = sb("b_cos", [P, CT, HD // 2])
        sin_sb = sb("b_sin", [P, CT, 2, HD // 2])
        ones = sb("b_ones", [P, HD])
        gam = sb("b_gam", [P, 2, KD])
        bet = sb("b_bet", [P, 2, KD])
        bo_sb = sb("b_bo", [P, D])
        mhalf = sb("b_mhalf", [P, CT + NT])
        rows = sb("b_rows", [P, CT + NT, D])
        x1 = sb("b_x1", [P, NT, D])
        cT = [sb(f"b_cT_{n}", [P, KD, CTX], F32R) for n in "hl"]
        lT = [sb(f"b_lT_{n}", [P, KD, B], F32R) for n in "hl"]
        KT = sb("b_KT", [P, HG, CTX], F32R)
        V = sb("b_V", [P, CT, HG * HD])
        QQ = sb("b_QQ", [P, 2, 2, 2, B], F32R)
        OT = [sb(f"b_OT_{n}", [P, PG, B], F32R) for n in "hl"]
        probs = sb("b_probs", [P, 4, 2 * B])
        krot = probs[:, 0, :].rearrange("p (a n) -> p a n", a=2)
        kswap = probs[:, 1, 0:HG * HD]
        knat = QQ[:, 1].rearrange("p a b n -> p (a b n)").rearrange("p (t n) -> p t n", t=2)
        acc = sb("b_acc", [P, 2, B])
        accf = sb("b_accf", [P, 2, B])
        r = sb("b_r", [P, B])
        o = sb("b_o", [P, B])
        zc = [acc[:, :, :].rearrange("p a n -> p (a n)"), probs[:, 2, :]]
        zl = [probs[:, 3, 0:B], probs[:, 3, B:2 * B]]
        st = sb("b_st", [P, CT + NT, 6])
        mv = sb("b_mv", [P, CT + NT, 2])
        ve = sb("b_ve", [P, CT + NT])
        rs = sb("b_rs", [P, CT + NT])
        ps = ctx.enter_context(nc.psum_tensor("b_ps", [P, 8, 512], F32))

        banks = {"A": 0, "B": 2, 4: 4, 5: 5, 6: 6, 7: 7}
        order = [(("cx", 0), "A"), (("cx", 1), "B"), (("lx", 0), 4), (("lx", 1), 5)]
        for g in range(2):
            for t in range(CT):
                order.append((("kv", g, t), "AB"[t % 2]))
                if t == CT - 1:
                    order.append((("q", g, 0), "A"))
                if t:
                    order += [(("kt", g, t - 1, a), 4 + 2 * ((t - 1) % 2) + a) for a in range(2)]
            order += [(("kt", g, CT - 1, a), 4 + 2 * ((CT - 1) % 2) + a) for a in range(2)]
            order += [(("s", g, 0, 0, hh), "AB"[hh]) for hh in range(2)]
            for p in range(PG):
                for j in range(4):
                    if (p, j) != (PG - 1, 3):
                        pn, jn = (p, j + 1) if j < 3 else (p + 1, 0)
                        order += [(("s", g, pn, jn, hh), "AB"[hh]) for hh in range(2)]
                    if j == 1 and p + 1 < PG:
                        order.append((("q", g, p + 1), 7))
                    if j == 0:
                        if p:
                            order.append((("sum", g, p - 1), 6))
                        order.append((("o", g, p), 4 + p % 2))
            order += [(("sum", g, PG - 1), 6), (("y", g, 0), 6), (("y", g, 1), 7)]
        slots = Slots(order, {"A": 2, "B": 2}, ("o",))
        filled = {s: sem(f"b_filled{s}") for s in banks}
        drained = {s: sem(f"b_drained{s}") for s in banks}
        consts = sem("b_consts")
        consts_in = sem("b_consts_in")
        ctx_in = sem("b_ctx_in")
        x1_in = sem("b_x1_in")
        var_ready = sem("b_var_ready")
        rstd_ready = sem("b_rstd_ready")
        normed = sem("b_normed")
        biased = sem("b_biased")
        z_ready = sem("b_z_ready")
        zh_ready = sem("b_zh_ready")
        zl_ready = sem("b_zl_ready")
        rotated = sem("b_rotated")
        kh_ready = sem("b_kh_ready")
        knat_ready = sem("b_knat_ready")
        qh_ready = sem("b_qh_ready")
        exped = sem("b_exped")
        clipped = sem("b_clipped")
        pv_done = sem("b_pv_done")
        acc_ready = sem("b_acc_ready")
        accf_ready = sem("b_accf_ready")
        pchain = sem("b_pchain")
        dchain = sem("b_dchain")
        oh_ready = sem("b_oh_ready")
        ot_ready = sem("b_ot_ready")
        out_ready = sem("b_out_ready")
        stats_taken = sem("b_stats_taken")
        stored = sem("b_stored")

        def wait_filled(eng, key, b):
            eng.wait_ge(filled[slots.slot(key)], slots.filled(key, b))

        def wait_free(eng, key, b):
            eng.wait_ge(drained[slots.slot(key)], slots.free(key, b))

        def wait_drained(eng, key, b):
            eng.wait_ge(drained[slots.slot(key)], slots.drained(key, b))

        def bank(key, a=0):
            return ps[:, banks[slots.slot(key)] + a, :]

        def both(key):
            n = banks[slots.slot(key)]
            return ps[:, n:n + 2, :].rearrange("p a n -> p (a n)")

        def fill(key, ins):
            ins.then_inc(filled[slots.slot(key)], 1)

        def drain(key, ins, n=1):
            ins.then_inc(drained[slots.slot(key)], n)

        def step(g, p, j):
            return (g * PG + p) * 4 + j

        NCONST = 4
        with nc.Block() as block:

            @block.sync
            def _(sp):
                for half in (0, 1):
                    sp.dma_start(sin_sb[:, :, half, :], sin.rearrange("(t p) n -> p t n", p=P)).then_inc(consts_in, 16)
                sp.dma_start(cos_sb[:, :, :], cos.rearrange("(t p) n -> p t n", p=P)).then_inc(consts_in, 16)
                for n, (g_in, b_in) in enumerate(((cg, cb), (lg, lb))):
                    sp.dma_start(gam[:, n, :], g_in.rearrange("(k p) -> p k", p=P), allow_slow_non_contiguous=True
                                 ).then_inc(consts_in, 16)
                    sp.dma_start(bet[:, n, :], b_in.rearrange("(k p) -> p k", p=P), allow_slow_non_contiguous=True
                                 ).then_inc(consts_in, 16)
                sp.dma_start(bo_sb[:, :], bo.partition_broadcast(P)).then_inc(consts_in, 16)

                def load(what, b):
                    if what == "context":
                        sp.dma_start(rows[:, 0:CT, :], context[bass.ds(b, 1)].rearrange("a (t p) d -> p (a t) d", p=P)
                                     ).then_inc(ctx_in, 16)
                    else:
                        sp.dma_start(x1[:, :, :], x1_dram[bass.ds(b, 1)].rearrange("a (t p) d -> p (a t) d", p=P)
                                     ).then_inc(x1_in, 16)

                load("context", 0)
                load("x1", 0)
                with sp.Fori(0, S) as b:
                    sp.wait_ge(zl_ready, (b + 1) * (2 * KD))
                    load("context", (b + 1) % S)
                    sp.wait_ge(out_ready, (b + 1) * NT)
                    load("x1", (b + 1) % S)
                    sp.dma_start(x2_dram[bass.ds(b, 1)].rearrange("a (t p) d -> p (a t) d", p=P), rows[:, CT:CT + NT, :]
                                 ).then_inc(stored, 16)
                sp.wait_ge(stored, 16 * S)
                sp.wait_ge(ctx_in, 16 * (S + 1))
                sp.wait_ge(x1_in, 16 * (S + 1))

            @block.gpsimd
            def _(pool):
                pool.memset(ones[:, :], 1.0).then_inc(consts, 1)
                pool.memset(mhalf[:, :], -0.5).then_inc(consts, 1)
                pool.wait_ge(consts_in, 16 * 8)
                pool.tensor_scalar(sin_sb[:, :, 0, :], sin_sb[:, :, 0, :], -1.0, None, ALU.mult).then_inc(consts, 1)
                pool.wait_ge(consts, 3)
                pool.sem_inc(consts, 1)
                with pool.Fori(0, S) as b:
                    pool.wait_ge(var_ready, 2 * b + 1)
                    pool.tensor_tensor(rs[:, :], ve[:, :], mhalf[:, :], ALU.pow).then_inc(rstd_ready, 1)
                    pool.wait_ge(normed, (b + 1) * (CT + NT))
                    pool.tensor_tensor(x1[:, :, :], x1[:, :, :], bo_sb[:, :].unsqueeze(1).broadcast_to([P, NT, D]),
                                       ALU.add).then_inc(biased, 1)
                    links = 0
                    for g in range(2):
                        for p in range(PG):
                            for j in range(3):
                                for hh in range(2):
                                    pool.wait_ge(clipped, b * (16 * PG) + (step(g, p, j) * 2 + hh + 1))
                                    pr = probs[:, 2 * (j % 2) + hh, :]
                                    if j == 0:
                                        pool.wait_ge(accf_ready, b * (4 * PG) + ((g * PG + p) * 2))
                                        ins = pool.tensor_tensor(acc[:, hh, :], pr[:, 0:B], pr[:, B:2 * B], ALU.add)
                                    else:
                                        ins = pool.tensor_tensor(acc[:, hh, :], acc[:, hh, :], pr[:, 0:B], ALU.add)
                                        links += 1
                                        ins.then_inc(pchain, 1)
                                        pool.wait_ge(pchain, b * (16 * PG // 2) + links)
                                        ins = pool.tensor_tensor(acc[:, hh, :], acc[:, hh, :], pr[:, B:2 * B], ALU.add)
                                    ins.then_inc(acc_ready, 1)
                                    pool.wait_ge(acc_ready, b * (12 * PG) + ((g * PG + p) * 3 + j) * 2 + hh + 1)
                    assert links == 8 * PG
                    pool.wait_ge(var_ready, 2 * b + 2)
                    pool.tensor_tensor(rs[:, 0:NT], ve[:, 0:NT], mhalf[:, 0:NT], ALU.pow).then_inc(rstd_ready, 1)

            def scores(pe, b, g, p, j):
                n = g * PG + p
                for hh in range(2):
                    key = ("s", g, p, j, hh)
                    wait_free(pe, key, b)
                    if j == 0 and hh == 0:
                        wait_drained(pe, ("q", g, p), b)
                    if p == 0:
                        for a in range(2):
                            wait_drained(pe, ("kt", g, 2 * j + 1, a), b)
                            wait_drained(pe, ("kt", g, 2 * j, a), b)
                    for a in range(2):
                        t = 2 * j + a
                        k = KT[:, 2 * p + hh, t * P:(t + 1) * P]
                        pe.matmul(bank(key, a), k, QQ[:, n % 2, hh, 0, :], start=True, stop=False)
                        mm = pe.matmul(bank(key, a), k, QQ[:, n % 2, hh, 1, :], start=False, stop=True)
                    fill(key, mm)

            def queries(pe, b, g, p):
                key = ("q", g, p)
                wait_free(pe, key, b)
                col = (g * PG + p) * P
                terms = [u for k in range(KD) for u in three_terms(
                    wq[0][:, k * INNER + col:k * INNER + col + P], wq[1][:, k * INNER + col:k * INNER + col + P],
                    lT[0][:, k, :], lT[1][:, k, :])]
                for a, (lhsT, rhs) in enumerate(terms):
                    mm = pe.matmul(bank(key), lhsT, rhs, start=(a == 0), stop=(a == len(terms) - 1))
                fill(key, mm)

            def sums(pe, b, g, p):
                key = ("sum", g, p)
                wait_free(pe, key, b)
                pe.wait_ge(accf_ready, b * (4 * PG) + (g * PG + p + 1) * 2)
                for hh in range(2):
                    mm = pe.matmul(bank(key)[hh * HD:(hh + 1) * HD, :], ones[:, :], accf[:, hh, :],
                                   start=True, stop=True)
                fill(key, mm)

            @block.tensor
            def _(pe):
                pe.wait_ge(consts, NCONST)
                with pe.Fori(0, S) as b:
                    for k in range(KD):
                        wait_free(pe, ("cx", k), b)
                        for t in range(CT):
                            if k == 0:
                                pe.wait_ge(normed, b * (CT + NT) + t + 1)
                            mm = pe.transpose(both(("cx", k))[:, t * P:(t + 1) * P], rows[:, t, k * P:(k + 1) * P],
                                              ident[:, :])
                        fill(("cx", k), mm)
                    for k in range(KD):
                        wait_free(pe, ("lx", k), b)
                        for t in range(NT):
                            if k == 0:
                                pe.wait_ge(normed, b * (CT + NT) + CT + t + 1)
                            mm = pe.transpose(bank(("lx", k))[:, t * P:(t + 1) * P], rows[:, CT + t, k * P:(k + 1) * P],
                                              ident[:, :])
                        fill(("lx", k), mm)

                    def k_turn(g, t):
                        pe.wait_ge(knat_ready, b * (2 * CT) + (g * CT + t + 1))
                        for a in range(2):
                            key = ("kt", g, t, a)
                            wait_free(pe, key, b)
                            for h in range(4 * a, 4 * a + 4):
                                mm = pe.transpose(bank(key)[:, (h - 4 * a) * P:(h - 4 * a + 1) * P].bitcast(F32R),
                                                  knat[:, t % 2, h * 2 * HD:(h + 1) * 2 * HD], identr[:, :])
                            fill(key, mm)

                    for g in range(2):
                        for t in range(CT):
                            key = ("kv", g, t)
                            wait_free(pe, key, b)
                            if g == 0 and t == 0:
                                pe.wait_ge(zl_ready, b * (2 * KD) + 2)
                            for a, w in enumerate((wk, wv)):
                                n = 0
                                for k in range(KD):
                                    c0 = k * INNER + g * HG * HD
                                    for lhsT, rhs in three_terms(cT[0][:, k, t * P:(t + 1) * P],
                                                                 cT[1][:, k, t * P:(t + 1) * P],
                                                                 w[0][:, c0:c0 + HG * HD], w[1][:, c0:c0 + HG * HD]):
                                        mm = pe.matmul(bank(key, a), lhsT, rhs, start=(n == 0), stop=(n == 3 * KD - 1))
                                        n += 1
                            fill(key, mm)
                            if t == CT - 1:
                                if g == 0:
                                    pe.wait_ge(zl_ready, (b + 1) * (2 * KD))
                                queries(pe, b, g, 0)
                            if t:
                                k_turn(g, t - 1)
                        k_turn(g, CT - 1)
                        scores(pe, b, g, 0, 0)
                        for p in range(PG):
                            for j in range(4):
                                if j < 3:
                                    scores(pe, b, g, p, j + 1)
                                elif p + 1 < PG:
                                    scores(pe, b, g, p + 1, 0)
                                if j == 1 and p + 1 < PG:
                                    queries(pe, b, g, p + 1)
                                if j == 0 and p:
                                    sums(pe, b, g, p - 1)
                                key = ("o", g, p)
                                if j == 0:
                                    wait_free(pe, key, b)
                                pe.wait_ge(clipped, b * (16 * PG) + (step(g, p, j) + 1) * 2)
                                for t in (2 * j, 2 * j + 1):
                                    for hh in range(2):
                                        mm = pe.matmul(bank(key)[hh * HD:(hh + 1) * HD, :],
                                                       V[:, t, (2 * p + hh) * HD:(2 * p + hh + 1) * HD],
                                                       probs[:, 2 * (j % 2) + hh, (t % 2) * B:(t % 2 + 1) * B],
                                                       start=(t == 0), stop=(t == CT - 1))
                                mm.then_inc(pv_done, 1)
                        sums(pe, b, g, PG - 1)
                        pe.wait_ge(ot_ready, b * (2 * PG) + (g + 1) * PG)
                        for a in range(2):
                            key = ("y", g, a)
                            wait_free(pe, key, b)
                            for t in (2 * a, 2 * a + 1):
                                n = 0
                                for p in range(PG):
                                    c0 = (g * PG + p) * D
                                    for lhsT, rhs in three_terms(OT[0][:, p, t * P:(t + 1) * P],
                                                                 OT[1][:, p, t * P:(t + 1) * P],
                                                                 wo[0][:, c0:c0 + D], wo[1][:, c0:c0 + D]):
                                        mm = pe.matmul(bank(key)[:, (t % 2) * D:(t % 2 + 1) * D], lhsT, rhs,
                                                       start=(n == 0), stop=(n == 3 * PG - 1))
                                        n += 1
                            fill(key, mm)

            @block.scalar
            def _(act):
                act.wait_ge(consts, NCONST)

                def q_hi(b, g, p):
                    key = ("q", g, p)
                    wait_filled(act, key, b)
                    n = g * PG + p
                    for hh in range(2):
                        for to in range(2):
                            ins = act.activation(QQ[to * HD:(to + 1) * HD, n % 2, hh, 0, :],
                                                 bank(key)[hh * HD:(hh + 1) * HD, :], ACT.Copy)
                    ins.then_inc(qh_ready, 1)

                def o_hi(b, g, p):
                    wait_drained(act, ("o", g, p), b)
                    act.activation(OT[0][:, p, :], o[:, :], ACT.Copy).then_inc(oh_ready, 1)

                with act.Fori(0, S) as b:
                    zs = [(("cx", 0), 0, 0), (("cx", 1), 0, 1), (("lx", 0), 1, 0), (("lx", 1), 1, 1)]
                    for n, (key, which, k) in enumerate(zs):
                        wait_filled(act, key, b)
                        z = (zc, zl)[which][k]
                        src = both(key) if which == 0 else bank(key)
                        act.activation(z, src, ACT.Identity, scale=gam[:, which, k:k + 1],
                                       bias=bet[:, which, k:k + 1]).then_inc(z_ready, 1)
                        act.wait_ge(z_ready, b * 4 + n + 1)
                        act.activation((cT, lT)[which][0][:, k, :], z, ACT.Copy
                                       ).then_inc(zh_ready, 1)
                    for g in range(2):
                        def k_turned(t):
                            for a in range(2):
                                key = ("kt", g, t, a)
                                wait_filled(act, key, b)
                                drain(key, act.activation(KT[:, 4 * a:4 * a + 4, t * P:(t + 1) * P],
                                                          bank(key).rearrange("p (h n) -> p h n", n=P), ACT.Copy))

                        for t in range(CT):
                            key = ("kv", g, t)
                            wait_filled(act, key, b)
                            drain(key, act.activation(V[:, t, :], bank(key, 1), ACT.Copy))
                            act.wait_ge(rotated, b * (2 * CT) + (g * CT + t + 1))
                            act.activation(knat[:, t % 2, :].rearrange("p (h a n) -> p h a n", a=2, n=HD)[:, :, 0, :],
                                           krot[:, t % 2, :].rearrange("p (h n) -> p h n", n=HD), ACT.Copy
                                           ).then_inc(kh_ready, 1)
                            if t == CT - 1:
                                q_hi(b, g, 0)
                            if t:
                                k_turned(t - 1)
                        k_turned(CT - 1)
                        for p in range(PG):
                            for j in range(4):
                                for hh in range(2):
                                    key = ("s", g, p, j, hh)
                                    wait_filled(act, key, b)
                                    if (p, j) >= (0, 2):
                                        before = step(g, p, j) - 2
                                        act.wait_ge(pv_done, b * (8 * PG) + before + 1)
                                        if before % 4 == 3:
                                            act.wait_ge(accf_ready, b * (4 * PG) + (before // 4) * 2 + hh + 1)
                                        else:
                                            act.wait_ge(acc_ready, b * (12 * PG)
                                                        + ((before // 4) * 3 + before % 4) * 2 + hh + 1)
                                    ins = act.activation(probs[:, 2 * (j % 2) + hh, :], both(key), ACT.Exp, scale=SCALE)
                                    drain(key, ins, 2)
                                if j == 0 and p >= 2:
                                    o_hi(b, g, p - 2)
                                if j == 2 and p + 1 < PG:
                                    q_hi(b, g, p + 1)
                        o_hi(b, g, PG - 2)
                        o_hi(b, g, PG - 1)

            @block.vector
            def _(dve):
                dve.wait_ge(consts, NCONST)
                LINKS = 2 + 2 * (CT + 2 * PG) + 2
                with dve.Fori(0, S) as b:
                    made = [0]

                    def link(ins):
                        made[0] += 1
                        ins.then_inc(dchain, 1)
                        dve.wait_ge(dchain, b * LINKS + made[0])

                    dve.wait_ge(ctx_in, (b + 1) * 16)
                    for t in range(CT + NT):
                        if t == CT:
                            dve.wait_ge(x1_in, (b + 1) * 16)
                        ins = dve.bn_stats(st[:, t, :], rows[:, t, :] if t < CT else x1[:, t - CT, :])
                    link(ins)
                    dve.sem_inc(stats_taken, 1)
                    for t in range(CT + NT):
                        ins = dve.bn_aggr(mv[:, t, :], st[:, t, :])
                    link(ins)
                    dve.tensor_scalar(ve[:, :], mv[:, :, 1], EPS, None, ALU.add).then_inc(var_ready, 1)
                    dve.wait_ge(rstd_ready, 2 * b + 1)
                    for t in range(CT + NT):
                        if t == CT:
                            dve.wait_ge(stored, b * 16)
                        dve.tensor_scalar(rows[:, t, :], rows[:, t, :] if t < CT else x1[:, t - CT, :],
                                          mv[:, t, 0:1], rs[:, t:t + 1], ALU.subtract, ALU.mult).then_inc(normed, 1)
                    zs = [(("cx", 0), 0, 0), (("cx", 1), 0, 1), (("lx", 0), 1, 0), (("lx", 1), 1, 1)]
                    for n, (key, which, k) in enumerate(zs):
                        dve.wait_ge(zh_ready, b * 4 + n + 1)
                        z = (zc, zl)[which][k]
                        hi, lo = (cT, lT)[which]
                        dve.tensor_tensor(lo[:, k, :], z, hi[:, k, :].bitcast(F32), ALU.subtract
                                          ).then_inc(zl_ready, 1)
                        dve.wait_ge(zl_ready, b * 4 + n + 1)
                        dve.sem_inc(drained[slots.slot(key)], 2 if which == 0 else 1)

                    for g in range(2):
                        def k_lo(t):
                            dve.wait_ge(kh_ready, b * (2 * CT) + (g * CT + t + 1))
                            nat = knat[:, t % 2, :].rearrange("p (h a n) -> p h a n", a=2, n=HD)
                            dve.tensor_tensor(nat[:, :, 1, :], krot[:, t % 2, :].rearrange("p (h n) -> p h n", n=HD),
                                              nat[:, :, 0, :].bitcast(F32), ALU.subtract).then_inc(knat_ready, 1)

                        for t in range(CT):
                            key = ("kv", g, t)
                            wait_filled(dve, key, b)
                            if t >= 2:
                                dve.wait_ge(knat_ready, b * (2 * CT) + (g * CT + t - 1))
                            K = bank(key).rearrange("p (h n) -> p h n", n=HD // 2)
                            dve.tensor_tensor(krot[:, t % 2, :].rearrange("p (h n) -> p h n", n=HD // 2), K,
                                              cos_sb[:, t, :].unsqueeze(1).broadcast_to([P, 2 * HG, HD // 2]), ALU.mult)
                            K = bank(key).rearrange("p (h a n) -> p h a n", a=2, n=HD // 2)[:, :, ::-1, :]
                            dve.wait_ge(rotated, b * (2 * CT) + (g * CT + t))
                            ins = dve.tensor_tensor(
                                kswap.rearrange("p (h a n) -> p h a n", a=2, n=HD // 2), K,
                                sin_sb[:, t, :, :].unsqueeze(1).broadcast_to([P, HG, 2, HD // 2]), ALU.mult)
                            link(ins)
                            dve.sem_inc(drained[slots.slot(key)], 1)
                            dve.tensor_tensor(krot[:, t % 2, :], krot[:, t % 2, :], kswap, ALU.add).then_inc(rotated, 1)
                            if t:
                                k_lo(t - 1)
                        k_lo(CT - 1)

                        def q_lo(p, hh):
                            key = ("q", g, p)
                            n = g * PG + p
                            dve.wait_ge(qh_ready, b * (2 * PG) + n + 1)
                            for to in range(2):
                                rows_ = slice(to * HD, (to + 1) * HD)
                                ins = dve.tensor_tensor(QQ[rows_, n % 2, hh, 1, :], bank(key)[hh * HD:(hh + 1) * HD, :],
                                                        QQ[rows_, n % 2, hh, 0, :].bitcast(F32), ALU.subtract)
                            if hh == 1:
                                drain(key, ins, 2 if p == 0 else 1)

                        def inverse(p, a):
                            key = ("sum", g, p)
                            if a == 0:
                                wait_filled(dve, key, b)
                                if p:
                                    wait_drained(dve, ("o", g, p - 1), b)
                            ins = dve.reciprocal(r[:, a * P:(a + 1) * P], bank(key)[:, a * P:(a + 1) * P])
                            if a == 3:
                                drain(key, ins)

                        def o_scaled(p):
                            wait_drained(dve, ("sum", g, p), b)
                            dve.wait_ge(ot_ready, b * (2 * PG) + (g * PG + p))
                            drain(("o", g, p), dve.tensor_tensor(o[:, :], bank(("o", g, p)), r[:, :], ALU.mult))

                        def o_lo(p):
                            dve.wait_ge(oh_ready, b * (2 * PG) + (g * PG + p + 1))
                            dve.tensor_tensor(OT[1][:, p, :], o[:, :], OT[0][:, p, :].bitcast(F32), ALU.subtract
                                              ).then_inc(ot_ready, 1)

                        q_lo(0, 0)
                        q_lo(0, 1)
                        for p in range(PG):
                            for j in range(4):
                                for hh in range(2):
                                    n = step(g, p, j) * 2 + hh
                                    pr = probs[:, 2 * (j % 2) + hh, :]
                                    wait_drained(dve, ("s", g, p, j, hh), b)
                                    dve.tensor_scalar(pr, pr, HI, LO, ALU.min, ALU.max).then_inc(clipped, 1)
                                    if j == 3:
                                        dve.wait_ge(clipped, b * (16 * PG) + n + 1)
                                        link(dve.tensor_tensor(accf[:, hh, :], pr[:, 0:B], pr[:, B:2 * B], ALU.add))
                                        dve.wait_ge(acc_ready, b * (12 * PG) + ((g * PG + p) * 3 + 2) * 2 + hh + 1)
                                        dve.tensor_tensor(accf[:, hh, :], accf[:, hh, :], acc[:, hh, :], ALU.add
                                                          ).then_inc(accf_ready, 1)
                                    if p and (j, hh) in ((0, 1), (1, 0), (1, 1), (2, 0)):
                                        inverse(p - 1, 2 * j + hh - 1)
                                    if p >= 2 and (j, hh) == (1, 0):
                                        o_lo(p - 2)
                                    if p + 1 < PG and (j, hh) == (2, 1):
                                        q_lo(p + 1, 0)
                                    if p + 1 < PG and (j, hh) == (3, 0):
                                        q_lo(p + 1, 1)
                                    if p and (j, hh) == (3, 1):
                                        o_scaled(p - 1)
                        o_lo(PG - 2)
                        for a in range(4):
                            inverse(PG - 1, a)
                        o_scaled(PG - 1)
                        o_lo(PG - 1)
                        for a in range(2):
                            key = ("y", g, a)
                            wait_filled(dve, key, b)
                            if (g, a) == (0, 0):
                                dve.wait_ge(biased, b + 1)
                            xs = x1[:, 2 * a:2 * a + 2, :].rearrange("p t n -> p (t n)")
                            drain(key, dve.tensor_tensor(xs, bank(key), xs, ALU.add))
                    for a in range(2):
                        wait_drained(dve, ("y", 1, a), b)
                    for t in range(NT):
                        ins = dve.bn_stats(st[:, t, :], x1[:, t, :])
                    link(ins)
                    dve.sem_inc(stats_taken, 1)
                    for t in range(NT):
                        ins = dve.bn_aggr(mv[:, t, :], st[:, t, :])
                    link(ins)
                    dve.tensor_scalar(ve[:, 0:NT], mv[:, 0:NT, 1], EPS, None, ALU.add).then_inc(var_ready, 1)
                    dve.wait_ge(rstd_ready, 2 * b + 2)
                    for t in range(NT):
                        dve.tensor_scalar(rows[:, CT + t, :], x1[:, t, :], mv[:, t, 0:1], rs[:, t:t + 1],
                                          ALU.subtract, ALU.mult).then_inc(out_ready, 1)
                    assert made[0] == LINKS, (made[0], LINKS)


def experts(nc, x2_dram, Wr, rb, W1, W2, W3, Ws1, Ws2, Ws3, out, ident):
    TOK = S * B
    NT, CH, CT = TOK // P, TOK // 512, 4
    HB = FF // P
    RSCALE = 1.0 / math.sqrt(D)
    with ExitStack() as ctx:
        def sb(name, shape, dt=F32):
            return ctx.enter_context(nc.sbuf_tensor(name, shape, dt))

        def sem(name):
            return ctx.enter_context(nc.semaphore(name))

        y = sb("c_y", [P, NT, D])
        xT = [sb(f"c_xT_{n}", [P, KD, TOK], F32R) for n in "hl"]
        w1 = [[sb(f"c_w1_{n}{k}", [P, KD * FF], F32R) for n in "hl"] for k in range(2)]
        w3 = [[sb(f"c_w3_{n}{k}", [P, KD * FF], F32R) for n in "hl"] for k in range(2)]
        w2 = [[sb(f"c_w2_{n}{k}", [P, HB * D], F32R) for n in "hl"] for k in range(2)]
        raw = sb("c_raw", [P, 3, KD * FF])
        hT = [sb(f"c_hT_{n}", [P, 2, HB, 512], F32R) for n in "hl"]
        gate = sb("c_gate", [P, 2, 512])
        hid = sb("c_hid", [P, 2, 512])
        wr = sb("c_wr", [P, KD, E])
        wrs = [sb(f"c_wr_{n}", [P, KD, E], F32R) for n in "hl"]
        rb_sb = sb("c_rb", [P, E])
        logit = sb("c_logit", [P, NT, E])
        biased = sb("c_biased", [P, NT, E])
        top = sb("c_top", [P, NT, 8])
        topi = sb("c_topi", [P, NT, 8], U32)
        topf = sb("c_topf", [P, 2, NT])
        lane = sb("c_lane", [P, E])
        hot = sb("c_hot", [P, 2, NT, E])
        pick = sb("c_pick", [P, 2, NT])
        pmax = sb("c_pmax", [P, NT])
        prod = sb("c_prod", [P, NT, E])
        share = sb("c_share", [P, NT, 1 + E])
        mhalf = sb("c_mhalf", [P, CT])
        st = sb("c_st", [P, CT, 6])
        mv = sb("c_mv", [P, CT, 2])
        ve = sb("c_ve", [P, CT])
        rs = sb("c_rs", [P, CT])
        ps = ctx.enter_context(nc.psum_tensor("c_ps", [P, 8, 512], F32))

        x_in = [sem(f"c_x_in{c}") for c in range(CH)]
        consts_in = sem("c_consts_in")
        consts = sem("c_consts")
        raw_in = sem("c_raw_in")
        raw_taken = sem("c_raw_taken")
        w_ready = sem("c_w_ready")
        turned = sem("c_turned")
        xh_ready = sem("c_xh_ready")
        xl_ready = sem("c_xl_ready")
        logits_done = sem("c_logits_done")
        logits_read = sem("c_logits_read")
        route_in = sem("c_route_in")
        route_exp = sem("c_route_exp")
        rchain = sem("c_rchain")
        h_filled = [sem(f"c_h_filled{k}") for k in range(2)]
        h_drained = [sem(f"c_h_drained{k}") for k in range(2)]
        y_filled = [sem(f"c_y_filled{k}") for k in range(4)]
        y_drained = [sem(f"c_y_drained{k}") for k in range(4)]
        gated = sem("c_gated")
        hid_ready = sem("c_hid_ready")
        hh_ready = sem("c_hh_ready")
        hl_ready = sem("c_hl_ready")
        var_ready = sem("c_var_ready")
        rstd_ready = sem("c_rstd_ready")
        out_ready = sem("c_out_ready")
        stored = sem("c_stored")
        lchain = sem("c_lchain")

        out_v = out.rearrange("s (t p) d -> s p t d", p=P)
        x2_v = x2_dram.rearrange("s (t p) d -> s p t d", p=P)

        def over_experts(eng, body):
            body(0, 0, True, False)
            with eng.Fori(0, (E - 2) // 2) as i:
                for a in range(2):
                    body(2 * i + (1 + a), 1 - a, False, False)
            for n in range(E - 1, E + 1):
                body(n, n % 2, False, n == E)

        with nc.Block() as block:

            @block.sync
            def _(sp):
                for c in range(CH):
                    sp.dma_start(y[:, c * CT:(c + 1) * CT, :], x2_v[c]).then_inc(x_in[c], 16)
                sp.dma_start(wr[:, :, :], Wr.rearrange("(k p) n -> p k n", p=P)).then_inc(consts_in, 16)
                sp.dma_start(rb_sb[:, :], rb.partition_broadcast(P)).then_inc(consts_in, 16)

                def load(n, par, first, last):
                    sp.wait_ge(w_ready, 6 * n)
                    if first:
                        srcs = (Ws1, Ws3, Ws2)
                    else:
                        srcs = [w[bass.ds(n - 1, 1)].rearrange("e k n -> (e k) n") for w in (W1, W3, W2)]
                    for m, src in enumerate(srcs):
                        sp.dma_start(raw[:, m, :].rearrange("p (k n) -> p k n", n=src.shape[1]),
                                     src.rearrange("(k p) n -> p k n", p=P)).then_inc(raw_in, 16)

                over_experts(sp, load)
                for c in range(CH):
                    sp.wait_ge(out_ready, CT * (c + 1))
                    sp.dma_start(out_v[c], y[:, c * CT:(c + 1) * CT, :]).then_inc(stored, 16)
                sp.wait_ge(stored, 16 * CH)

            @block.gpsimd
            def _(pool):
                pool.iota(topi[:, 0, :], pattern=[[1, E]], base=0, channel_multiplier=0).then_inc(consts, 1)
                pool.memset(mhalf[:, :], -0.5).then_inc(consts, 1)
                pool.wait_ge(consts, 2)
                pool.tensor_copy(lane[:, :], topi[:, 0, :]).then_inc(consts, 1)
                pool.memset(share[:, :, 0], 1.0)
                pool.wait_ge(consts_in, 32)
                pool.tensor_copy(wrs[0][:, :, :], wr[:, :, :]).then_inc(consts, 1)
                pool.wait_ge(consts, 4)
                pool.tensor_tensor(wrs[1][:, :, :], wr[:, :, :], wrs[0][:, :, :].bitcast(F32), ALU.subtract
                                   ).then_inc(consts, 1)

                def split(n, par, first, last):
                    pool.wait_ge(raw_in, (n + 1) * 48)
                    if not first:
                        pool.wait_ge(y_filled[3], (n - 1) * (CH // 2))
                    pool.sem_inc(raw_taken, 1)
                    for m, w in enumerate((w1, w3, w2)):
                        pool.tensor_copy(w[par][0][:, :], raw[:, m, :]).then_inc(w_ready, 1)
                    for m, w in enumerate((w1, w3, w2)):
                        pool.wait_ge(w_ready, n * 6 + m + 1)
                        pool.tensor_tensor(w[par][1][:, :], raw[:, m, :], w[par][0][:, :].bitcast(F32), ALU.subtract
                                           ).then_inc(w_ready, 1)

                over_experts(pool, split)
                for c in range(CH):
                    pool.wait_ge(var_ready, c + 1)
                    pool.tensor_tensor(rs[:, :], ve[:, :], mhalf[:, :], ALU.pow).then_inc(rstd_ready, 1)

            def second(pe, n, c, par, half):
                k = 2 * (c % 2) + half
                pe.wait_ge(y_drained[k], n * (CH // 2) + c // 2)
                if half == 0:
                    pe.wait_ge(hl_ready, (n * CH + c + 1) * HB)
                for t in (2 * half, 2 * half + 1):
                    a = 0
                    for hb in range(HB):
                        for lhsT, rhs in three_terms(hT[0][:, c % 2, hb, t * P:(t + 1) * P],
                                                     hT[1][:, c % 2, hb, t * P:(t + 1) * P],
                                                     w2[par][0][:, hb * D:(hb + 1) * D],
                                                     w2[par][1][:, hb * D:(hb + 1) * D]):
                            mm = pe.matmul(ps[:, 4 + k, (t % 2) * D:(t % 2 + 1) * D], lhsT, rhs,
                                           start=(a == 0), stop=(a == 3 * HB - 1))
                            a += 1
                mm.then_inc(y_filled[k], 1)

            @block.tensor
            def _(pe):
                for c in range(CH):
                    pe.wait_ge(x_in[c], 16)
                    for k in range(KD):
                        n = c * KD + k
                        if n >= 8:
                            pe.wait_ge(xl_ready, n - 7)
                        for t in range(CT):
                            mm = pe.transpose(ps[:, n % 8, t * P:(t + 1) * P], y[:, c * CT + t, k * P:(k + 1) * P],
                                              ident[:, :])
                        mm.then_inc(turned, 1)
                pe.wait_ge(xl_ready, CH * KD)
                pe.wait_ge(consts, 5)
                for t in range(NT):
                    a = 0
                    for k in range(KD):
                        for lhsT, rhs in three_terms(xT[0][:, k, t * P:(t + 1) * P], xT[1][:, k, t * P:(t + 1) * P],
                                                     wrs[0][:, k, :], wrs[1][:, k, :]):
                            mm = pe.matmul(ps[:, 7, t * E:(t + 1) * E], lhsT, rhs, start=(a == 0),
                                           stop=(a == 3 * KD - 1))
                            a += 1
                mm.then_inc(logits_done, 1)
                pe.wait_ge(logits_read, 1)

                def run(n, par, first, last):
                    pe.wait_ge(w_ready, (n + 1) * 6)
                    for c in range(CH):
                        for hb in range(HB):
                            k = hb % 2
                            pe.wait_ge(h_drained[k], (n * CH + c) * (HB // 2) + hb // 2)
                            for m, w in enumerate((w3, w1)):
                                a = 0
                                for kk in range(KD):
                                    c0 = kk * FF + hb * P
                                    for lhsT, rhs in three_terms(w[par][0][:, c0:c0 + P], w[par][1][:, c0:c0 + P],
                                                                 xT[0][:, kk, c * 512:(c + 1) * 512],
                                                                 xT[1][:, kk, c * 512:(c + 1) * 512]):
                                        mm = pe.matmul(ps[:, 2 * k + m, :], lhsT, rhs, start=(a == 0),
                                                       stop=(a == 3 * KD - 1))
                                        a += 1
                            mm.then_inc(h_filled[k], 1)
                            if k == 1 and (c or not first):
                                before = (n, c - 1, par) if c else (n - 1, CH - 1, 1 - par)
                                second(pe, *before, hb // 2)
                    if last:
                        for half in range(2):
                            second(pe, n, CH - 1, par, half)

                over_experts(pe, run)

            @block.scalar
            def _(act):
                for n in range(CH * KD):
                    act.wait_ge(turned, n + 1)
                    act.activation(xT[0][:, n % KD, (n // KD) * 512:(n // KD + 1) * 512], ps[:, n % 8, :], ACT.Copy
                                   ).then_inc(xh_ready, 1)

                def run(n, par, first, last):
                    for c in range(CH):
                        u = n * CH + c

                        def hi(hb):
                            act.wait_ge(hid_ready, u * HB + hb + 1)
                            act.activation(hT[0][:, c % 2, hb, :], hid[:, hb % 2, :], ACT.Copy).then_inc(hh_ready, 1)

                        for hb in range(HB):
                            k = hb % 2
                            act.wait_ge(h_filled[k], u * (HB // 2) + hb // 2 + 1)
                            act.activation(gate[:, k, :], ps[:, 2 * k, :], ACT.Silu).then_inc(gated, 1)
                            if hb:
                                hi(hb - 1)
                        hi(HB - 1)
                        if first and c == 0:
                            act.wait_ge(route_in, 1)
                            act.activation(pick[:, :, :], pick[:, :, :], ACT.Exp).then_inc(route_exp, 1)

                over_experts(act, run)

            @block.vector
            def _(dve):
                for n in range(CH * KD):
                    dve.wait_ge(xh_ready, n + 1)
                    cols = slice((n // KD) * 512, (n // KD + 1) * 512)
                    dve.tensor_tensor(xT[1][:, n % KD, cols], ps[:, n % 8, :], xT[0][:, n % KD, cols].bitcast(F32),
                                      ALU.subtract).then_inc(xl_ready, 1)
                dve.wait_ge(logits_done, 1)
                dve.tensor_scalar(logit[:, :, :].rearrange("p t e -> p (t e)"), ps[:, 7, 0:NT * E], RSCALE, None,
                                  ALU.mult).then_inc(logits_read, 1)

                def routing():
                    made = [0]

                    def link(ins):
                        made[0] += 1
                        ins.then_inc(rchain, 1)
                        dve.wait_ge(rchain, made[0])

                    dve.wait_ge(consts, 5)
                    dve.wait_ge(logits_read, 1)
                    link(dve.tensor_tensor(biased[:, :, :], logit[:, :, :],
                                           rb_sb[:, :].unsqueeze(1).broadcast_to([P, NT, E]), ALU.add))
                    for t in range(NT):
                        ins = dve.max(top[:, t, :], biased[:, t, :])
                    link(ins)
                    for t in range(NT):
                        ins = dve.max_index(topi[:, t, :], top[:, t, :], biased[:, t, :])
                    link(ins)
                    link(dve.tensor_copy(topf[:, :, :], topi[:, :, 0:2].rearrange("p t a -> p a t")))
                    for a in range(2):
                        ins = dve.tensor_tensor(hot[:, a], lane[:, :].unsqueeze(1).broadcast_to([P, NT, E]),
                                                topf[:, a, :].unsqueeze(2).broadcast_to([P, NT, E]), ALU.is_equal)
                    link(ins)
                    for a in range(2):
                        link(dve.tensor_tensor(prod[:, :, :], hot[:, a], logit[:, :, :], ALU.mult))
                        link(dve.tensor_reduce(pick[:, a, :], prod[:, :, :], AX.X, ALU.add))
                    link(dve.tensor_tensor(pmax[:, :], pick[:, 0, :], pick[:, 1, :], ALU.max))
                    dve.tensor_tensor(pick[:, :, :], pick[:, :, :], pmax[:, :].unsqueeze(1).broadcast_to([P, 2, NT]),
                                      ALU.subtract).then_inc(route_in, 1)
                    dve.wait_ge(route_exp, 1)
                    link(dve.tensor_tensor(pmax[:, :], pick[:, 0, :], pick[:, 1, :], ALU.add))
                    link(dve.reciprocal(pmax[:, :], pmax[:, :]))
                    link(dve.tensor_tensor(pick[:, :, :], pick[:, :, :],
                                           pmax[:, :].unsqueeze(1).broadcast_to([P, 2, NT]), ALU.mult))
                    for a in range(2):
                        link(dve.tensor_tensor(hot[:, a], hot[:, a],
                                               pick[:, a, :].unsqueeze(2).broadcast_to([P, NT, E]), ALU.mult))
                    link(dve.tensor_tensor(share[:, :, 1:1 + E], hot[:, 0], hot[:, 1], ALU.add))

                def add_up(n, c, half):
                    k = 2 * (c % 2) + half
                    dve.wait_ge(y_filled[k], n * (CH // 2) + c // 2 + 1)
                    for a in range(2):
                        t = c * CT + 2 * half + a
                        src = ps[:, 4 + k, a * D:(a + 1) * D]
                        ins = dve.scalar_tensor_tensor(y[:, t, :], src, share[:, t, bass.ds(n, 1)], y[:, t, :],
                                                       ALU.mult, ALU.add)
                    ins.then_inc(y_drained[k], 1)

                def layer_norm(c):
                    t0 = c * CT
                    for half in range(2):
                        dve.wait_ge(y_drained[2 * (c % 2) + half], E * (CH // 2) + c // 2 + 1)
                    for t in range(CT):
                        ins = dve.bn_stats(st[:, t, :], y[:, t0 + t, :])
                    ins.then_inc(lchain, 1)
                    dve.wait_ge(lchain, 2 * c + 1)
                    for t in range(CT):
                        ins = dve.bn_aggr(mv[:, t, :], st[:, t, :])
                    ins.then_inc(lchain, 1)
                    dve.wait_ge(lchain, 2 * c + 2)
                    dve.tensor_scalar(ve[:, :], mv[:, :, 1], EPS, None, ALU.add).then_inc(var_ready, 1)
                    dve.wait_ge(rstd_ready, c + 1)
                    for t in range(CT):
                        dve.tensor_scalar(y[:, t0 + t, :], y[:, t0 + t, :], mv[:, t, 0:1], rs[:, t:t + 1],
                                          ALU.subtract, ALU.mult).then_inc(out_ready, 1)

                def run(n, par, first, last):
                    for c in range(CH):
                        u = n * CH + c
                        before = (n, c - 1) if c else None if first else (n - 1, CH - 1)

                        def lo(hb):
                            dve.wait_ge(hh_ready, u * HB + hb + 1)
                            dve.tensor_tensor(hT[1][:, c % 2, hb, :], hid[:, hb % 2, :],
                                              hT[0][:, c % 2, hb, :].bitcast(F32), ALU.subtract).then_inc(hl_ready, 1)

                        for hb in range(HB):
                            k = hb % 2
                            dve.wait_ge(gated, u * HB + hb + 1)
                            if hb >= 2 or c or not first:
                                dve.wait_ge(hl_ready, u * HB + hb - 1)
                            dve.tensor_tensor(hid[:, k, :], ps[:, 2 * k + 1, :], gate[:, k, :], ALU.mult
                                              ).then_inc(hid_ready, 1)
                            dve.wait_ge(hid_ready, u * HB + hb + 1)
                            dve.sem_inc(h_drained[k], 1)
                            if hb:
                                lo(hb - 1)
                            if hb == 2 and before:
                                add_up(*before, 0)
                        lo(HB - 1)
                        if before:
                            add_up(*before, 1)
                        if last and c:
                            layer_norm(c - 1)
                        if first and c == 0:
                            routing()
                    if last:
                        for half in range(2):
                            add_up(n, CH - 1, half)
                        layer_norm(CH - 1)

                over_experts(dve, run)


def build(nc, x, ctx_1024, aWkv, abkv, aWq, abq, aWp, abp, cos, sin, lg, lb, cg, cb, xWq, xWkv, xWo, xbo,
          Wr, rb, W1, W2, W3, Ws1, Ws2, Ws3, out, upto="abc", x1_out=None, x2_out=None):
    x1_dram = x1_out if x1_out is not None else nc.dram_tensor("x1", (S, B, D), F32, kind="Internal").ap()
    with ExitStack() as ctx:
        ident = ctx.enter_context(nc.sbuf_tensor("ident", [P, P], F32))
        identr = ctx.enter_context(nc.sbuf_tensor("identr", [P, P], F32R))
        identb = ctx.enter_context(nc.sbuf_tensor("identb", [P, P], BF16))
        made = ctx.enter_context(nc.semaphore("ident_made"))
        with nc.Block() as block:

            @block.gpsimd
            def _(pool):
                pool.memset(ident[:, :], 0.0).then_inc(made, 1)
                pool.wait_ge(made, 1)
                pool.affine_select(out=ident[:, :], in_=ident[:, :], compare_op=ALU.not_equal, fill=1.0, base=0,
                                   pattern=[[-1, P]], channel_multiplier=1).then_inc(made, 1)
                pool.wait_ge(made, 2)
                pool.tensor_copy(identr[:, :], ident[:, :]).then_inc(made, 1)
                pool.tensor_copy(identb[:, :], ident[:, :]).then_inc(made, 1)

        x2_dram = x2_out if x2_out is not None else nc.dram_tensor("x2", (S, B, D), F32, kind="Internal").ap()
        if "a" in upto:
            self_attention(nc, x, aWkv, abkv, aWq, abq, aWp, abp, x1_dram, ident, identb)
        if "b" in upto:
            cross_attention(nc, x1_dram, ctx_1024, cos, sin, lg, lb, cg, cb, xWq, xWkv, xWo, xbo, x2_dram, ident, identr)
        if "c" in upto:
            experts(nc, x2_dram, Wr, rb, W1, W2, W3, Ws1, Ws2, Ws3, out, ident)


_INS = ['x', 'ctx_1024', 'L0_attn_Wkv', 'L0_attn_bkv', 'L0_attn_Wq', 'L0_attn_bq', 'L0_attn_Wp', 'L0_attn_bp',
        'L0_xattn_cos', 'L0_xattn_sin', 'L0_xattn_ln_lat_g', 'L0_xattn_ln_lat_b', 'L0_xattn_ln_ctx_g',
        'L0_xattn_ln_ctx_b', 'L0_xattn_Wq', 'L0_xattn_Wkv', 'L0_xattn_Wo', 'L0_xattn_bo', 'L0_ffn_Wr', 'L0_ffn_rb',
        'L0_ffn_W1', 'L0_ffn_W2', 'L0_ffn_W3', 'L0_ffn_Ws1', 'L0_ffn_Ws2', 'L0_ffn_Ws3']
_OUTS = [((S, B, D), 'float32')]


def kernel(**inputs):
    import numpy as _np
    import concourse.bacc as _bacc
    from concourse import mybir as _mybir
    from concourse.bass_utils import run_bass_kernel_spmd as _run

    nc = _bacc.Bacc("TRN2", target_bir_lowering=False, num_devices=1, dynamic_dma_scratch_size=1024)
    arrays, args = {}, []
    for name in _INS:
        a = _np.ascontiguousarray(inputs[name])
        arrays[f"in_{name}_dram"] = a
        args.append(nc.dram_tensor(f"in_{name}_dram", a.shape, _mybir.dt.from_np(a.dtype), kind="ExternalInput").ap())
    for i, (shape, dtype) in enumerate(_OUTS):
        dt = _mybir.dt.from_np(_np.dtype(dtype))
        args.append(nc.dram_tensor(f"out_{i}_dram", shape, dt, kind="ExternalOutput").ap())
    build(nc, *args)
    r = _run(nc, [arrays], core_ids=[0])
    return r.results[0]["out_0_dram"]
```

```python
import math
from contextlib import ExitStack

import concourse.bass as bass
from concourse import mybir

P = 128
F32 = mybir.dt.float32
F32R = mybir.dt.float32r
BF16 = mybir.dt.bfloat16
U32 = mybir.dt.uint32
ALU = mybir.AluOpType
ACT = mybir.ActivationFunctionType
AX = mybir.AxisListType
EPS = 1e-5

S, B, D = 8, 512, 256
H, HD = 16, 64
INNER = H * HD
CTX = 1024
SCALE = float(HD) ** -0.5
CLIP = 11.0
E, FF = 8, 512
KD = D // P
PAIRS = H // 2


class Slots:

    def __init__(self, order, weight=None, silent=()):
        self.at, self.uses, self.fills, self.fill_at = {}, {}, {}, {}
        for key, slot in order:
            self.at[key] = (slot, self.uses.get(slot, 0))
            self.uses[slot] = self.uses.get(slot, 0) + 1
            if key[0] not in silent:
                self.fill_at[key] = self.fills.get(slot, 0)
                self.fills[slot] = self.fills.get(slot, 0) + 1
        self.weight = weight or {}

    def slot(self, key):
        return self.at[key][0]

    def filled(self, key, i):
        return i * self.fills[self.slot(key)] + (self.fill_at[key] + 1)

    def free(self, key, i):
        slot, k = self.at[key]
        w = self.weight.get(slot, 1)
        return i * (self.uses[slot] * w) + k * w

    def drained(self, key, i):
        slot, k = self.at[key]
        w = self.weight.get(slot, 1)
        return i * (self.uses[slot] * w) + (k + 1) * w


def split_weights(nc, ctx, name, parts):
    with ExitStack() as c:
        raw = c.enter_context(nc.sbuf_tensor(f"{name}_raw", [P, 2, 2048], F32))
        loaded = [c.enter_context(nc.semaphore(f"{name}_loaded{k}")) for k in range(2)]
        hi_done = c.enter_context(nc.semaphore(f"{name}_hi_done"))
        lo_done = c.enter_context(nc.semaphore(f"{name}_lo_done"))
        with nc.Block() as block:

            @block.sync
            def _(sp):
                for n, (src, hi, lo) in enumerate(parts):
                    if n >= 2:
                        sp.wait_ge(lo_done, n - 1)
                    w = hi.shape[1]
                    sp.dma_start(raw[:, n % 2, 0:w].rearrange("p (a n) -> p a n", a=src.shape[1]), src
                                 ).then_inc(loaded[n % 2], 16)

            @block.scalar
            def _(act):
                for n, (src, hi, lo) in enumerate(parts):
                    act.wait_ge(loaded[n % 2], 16 * (n // 2 + 1))
                    act.activation(hi, raw[:, n % 2, 0:hi.shape[1]], ACT.Copy).then_inc(hi_done, 1)

            @block.vector
            def _(dve):
                for n, (src, hi, lo) in enumerate(parts):
                    dve.wait_ge(hi_done, n + 1)
                    dve.tensor_tensor(lo, raw[:, n % 2, 0:hi.shape[1]], hi.bitcast(F32), ALU.subtract
                                      ).then_inc(lo_done, 1)


def three_terms(w_hi, w_lo, x_hi, x_lo):
    return ((w_hi, x_hi), (w_hi, x_lo), (w_lo, x_hi))


def self_attention(nc, x, Wkv, bkv, Wq, bq, Wp, bp, x1_dram, ident, identb):
    CH, TT, BI = 8, 4, 16
    BIG = 1e30
    with ExitStack() as ctx:
        def sb(name, shape, dt=F32):
            return ctx.enter_context(nc.sbuf_tensor(name, shape, dt))

        def sem(name):
            return ctx.enter_context(nc.semaphore(name))

        wq = [sb(f"a_wq_{n}", [P, KD * INNER], F32R) for n in "hl"]
        wk = [sb(f"a_wk_{n}", [P, KD * INNER], F32R) for n in "hl"]
        wv = [sb(f"a_wv_{n}", [P, KD * INNER], F32R) for n in "hl"]
        wp = [sb(f"a_wp_{n}", [P, PAIRS * D], F32R) for n in "hl"]
        kv = Wkv.rearrange("(k p) n -> p k n", p=P)
        parts = []
        for (hi, lo), src in ((wk, kv[:, :, 0:INNER]), (wq, Wq.rearrange("(k p) n -> p k n", p=P)),
                              (wv, kv[:, :, INNER:2 * INNER]), (wp, Wp.rearrange("(k p) n -> p k n", p=P))):
            parts.append((src, hi[:, :], lo[:, :]))
        split_weights(nc, ctx, "a_w", parts)

        mneg = sb("a_mneg", [P, P], BF16)
        ident4 = sb("a_ident4", [P, 4, P], BF16)
        same16 = sb("a_same16", [P, BI])
        bq_sb = sb("a_bq", [P, PAIRS])
        bk_sb = sb("a_bk", [P, PAIRS])
        bv_sb = sb("a_bv", [P, INNER])
        bp_sb = sb("a_bp", [P, D])
        mhalf = sb("a_mhalf", [P, TT])
        xt = sb("a_xt", [P, 2, TT, D])
        xT = [sb(f"a_xT_{n}", [P, KD, TT * P], F32R) for n in "hl"]
        QT = sb("a_QT", [P, PAIRS, TT * P])
        KB = sb("a_KB", [P, PAIRS, TT, 2 * P])
        V = sb("a_V", [P, TT, INNER])
        Sc = sb("a_Sc", [P, 2, H, S])
        mx = sb("a_mx", [P, H])
        den = sb("a_den", [P, H])
        Pe = sb("a_Pe", [P, H, P])
        PT = sb("a_PT", [P, H, P])
        OT = [sb(f"a_OT_{n}", [P, PAIRS, P], F32R) for n in "hl"]
        y = sb("a_y", [P, 2, D])
        st = sb("a_st", [P, 6])
        mv = sb("a_mv", [P, 2])
        ve = sb("a_ve", [P, 1])
        rs = sb("a_rs", [P, 1])
        x1t = sb("a_x1t", [P, 2, TT, D])
        ps = ctx.enter_context(nc.psum_tensor("a_ps", [P, 8, 512], F32))

        order = [(("x", k), 6 + k) for k in range(KD)]
        order += [(("proj", n), n % 4) for n in range(24)]
        n = 24

        def s_group(t):
            nonlocal n
            out = []
            for q in range(4):
                out.append((("s", t, q), n % 4))
                n += 1
            return out

        turn = [0]

        def ring45(key):
            turn[0] += 1
            return key, 4 + (turn[0] - 1) % 2

        order += s_group(0)
        for t in range(TT):
            if t + 1 < TT:
                order += s_group(t + 1)
            order += [ring45(("pt", t, q)) for q in range(4)]
            order += [(("o", t, k), 6 + k) for k in range(2)]
            order.append(ring45(("y", t)))
        assert turn[0] % 2 == 0 and n % 4 == 0
        slots = Slots(order)
        filled = [sem(f"a_filled{i}") for i in range(8)]
        drained = [sem(f"a_drained{i}") for i in range(8)]
        consts = sem("a_consts")
        consts_in = sem("a_consts_in")
        x_in = [sem(f"a_x_in{k}") for k in range(2)]
        xh = sem("a_xh")
        xl = sem("a_xl")
        compact = sem("a_compact")
        exped = sem("a_exped")
        probs = sem("a_probs")
        spread = sem("a_spread")
        oth = sem("a_oth")
        otl = sem("a_otl")
        biased = sem("a_biased")
        var_ready = sem("a_var_ready")
        rstd_ready = sem("a_rstd_ready")
        x1_ready = sem("a_x1_ready")
        stats_taken = sem("a_stats_taken")
        stored = [sem(f"a_stored{k}") for k in range(2)]
        dchain = sem("a_dchain")

        def wait_filled(eng, key, c):
            eng.wait_ge(filled[slots.slot(key)], slots.filled(key, c))

        def wait_free(eng, key, c):
            eng.wait_ge(drained[slots.slot(key)], slots.free(key, c))

        def bank(key):
            return ps[:, slots.slot(key), :]

        with nc.Block() as block:

            @block.sync
            def _(sp):
                sp.dma_start(bq_sb[:, :], bq.rearrange("(c p) -> p c", p=P),
                             allow_slow_non_contiguous=True).then_inc(consts_in, 16)
                sp.dma_start(bk_sb[:, :], bkv[0:INNER].rearrange("(c p) -> p c", p=P),
                             allow_slow_non_contiguous=True).then_inc(consts_in, 16)
                sp.dma_start(bv_sb[:, :], bkv[INNER:2 * INNER].partition_broadcast(P)).then_inc(consts_in, 16)
                sp.dma_start(bp_sb[:, :], bp.partition_broadcast(P)).then_inc(consts_in, 16)

                def load(half, c):
                    for s in range(S):
                        src = x[s].rearrange("(c t b) d -> c b t d", t=TT, b=BI)[bass.ds(c, 1)]
                        sp.dma_start(xt[BI * s:BI * s + BI, half], src.rearrange("c b t d -> (c b) t d")
                                     ).then_inc(x_in[half], 16)

                def store(half, c):
                    for s in range(S):
                        dst = x1_dram[s].rearrange("(c t b) d -> c b t d", t=TT, b=BI)[bass.ds(c, 1)]
                        sp.dma_start(dst.rearrange("c b t d -> (c b) t d"), x1t[BI * s:BI * s + BI, half]
                                     ).then_inc(stored[half], 16)

                load(0, 0)
                with sp.Fori(0, CH // 2) as i:
                    sp.wait_ge(x1_ready, (2 * i) * TT)
                    load(1, 2 * i + 1)
                    sp.wait_ge(x1_ready, (2 * i + 1) * TT)
                    store(0, 2 * i)
                    load(0, (2 * i + 2) % CH)
                    sp.wait_ge(x1_ready, (2 * i + 2) * TT)
                    store(1, 2 * i + 1)
                for half in range(2):
                    sp.wait_ge(stored[half], 16 * S * (CH // 2))
                sp.wait_ge(x_in[0], 16 * S * (CH // 2 + 1))

            @block.gpsimd
            def _(pool):
                pool.memset(mneg[:, :], -BIG).then_inc(consts, 1)
                pool.memset(same16[:, :], 0.0).then_inc(consts, 1)
                pool.memset(mhalf[:, :], -0.5).then_inc(consts, 1)
                pool.memset(KB[:, :, :, :], 0.0).then_inc(consts, 1)
                pool.wait_ge(consts, 4)
                k = 4
                for a in range(-(S - 1), S):
                    pool.affine_select(out=mneg[:, :], in_=mneg[:, :], compare_op=ALU.not_equal, fill=0.0,
                                       base=-BI * a, pattern=[[-1, P]], channel_multiplier=1).then_inc(consts, 1)
                    k += 1
                    pool.wait_ge(consts, k)
                for a in range(S):
                    pool.affine_select(out=same16[:, :], in_=same16[:, :], compare_op=ALU.not_equal, fill=1.0,
                                       base=-BI * a, pattern=[[-1, BI]], channel_multiplier=1).then_inc(consts, 1)
                    k += 1
                    pool.wait_ge(consts, k)
                for a in range(4):
                    pool.tensor_copy(ident4[:, a, :], identb[:, :]).then_inc(consts, 1)
                pool.wait_ge(consts_in, 64)
                with pool.Fori(0, CH // 2) as i:
                    for half in range(2):
                        c = 2 * i + half
                        wait_filled(pool, ("x", 1), c)
                        for t in range(TT):
                            pool.tensor_tensor(xt[:, half, t], xt[:, half, t], bp_sb[:, :], ALU.add
                                               ).then_inc(biased, 1)
                        for t in range(TT):
                            pool.wait_ge(probs, c * TT + t + 1)
                            wait_filled(pool, ("pt", t - 1, 3) if t else ("x", 0), c)
                            pool.tensor_tensor(
                                Pe[:, :, :].rearrange("p h (t b) -> p (h t) b", b=BI),
                                Sc[:, t % 2].rearrange("p h t -> p (h t)").unsqueeze(2).broadcast_to([P, H * S, BI]),
                                same16[:, :].unsqueeze(1).broadcast_to([P, H * S, BI]), ALU.mult
                            ).then_inc(spread, 1)
                            if t:
                                pool.wait_ge(var_ready, c * TT + t)
                                pool.tensor_tensor(rs[:, :], ve[:, :], mhalf[:, 0:1], ALU.pow).then_inc(rstd_ready, 1)
                        pool.wait_ge(var_ready, c * TT + TT)
                        pool.tensor_tensor(rs[:, :], ve[:, :], mhalf[:, 0:1], ALU.pow).then_inc(rstd_ready, 1)

            def chunk(pe, i, c, half):
                pe.wait_ge(x_in[half], (i + 1) * (16 * S))
                for k in range(KD):
                    wait_free(pe, ("x", k), c)
                    for t in range(TT):
                        mm = pe.transpose(bank(("x", k))[:, t * P:(t + 1) * P], xt[:, half, t, k * P:(k + 1) * P],
                                          ident[:, :])
                    mm.then_inc(filled[6 + k], 1)
                pe.wait_ge(xl, (c + 1) * KD)
                for n in range(24):
                    wait_free(pe, ("proj", n), c)
                    if n < 16:
                        w = wk if n < 8 else wq
                        col = (n % 8) * P
                        terms = [t for k in range(KD) for t in three_terms(
                            w[0][:, k * INNER + col:k * INNER + col + P], w[1][:, k * INNER + col:k * INNER + col + P],
                            xT[0][:, k, :], xT[1][:, k, :])]
                    else:
                        t, h2 = (n - 16) // 2, (n - 16) % 2
                        cols = [slice(k * INNER + h2 * 512, k * INNER + h2 * 512 + 512) for k in range(KD)]
                        terms = [u for k in range(KD) for u in three_terms(
                            xT[0][:, k, t * P:(t + 1) * P], xT[1][:, k, t * P:(t + 1) * P],
                            wv[0][:, cols[k]], wv[1][:, cols[k]])]
                    for a, (lhsT, rhs) in enumerate(terms):
                        mm = pe.matmul(bank(("proj", n)), lhsT, rhs, start=(a == 0), stop=(a == len(terms) - 1))
                    mm.then_inc(filled[slots.slot(("proj", n))], 1)

                def scores(t):
                    for q in range(4):
                        key = ("s", t, q)
                        wait_free(pe, key, c)
                        if t == 0 and q == 0:
                            for n in range(20, 24):
                                pe.wait_ge(drained[n % 4], slots.drained(("proj", n), c))
                        pe.matmul(bank(key), mneg[:, :], ident4[:, :, :].rearrange("p a b -> p (a b)"),
                                  start=True, stop=True)
                        for a in range(2):
                            pair = 2 * q + a
                            mm = pe.matmul(bank(key)[:, a * 256:(a + 1) * 256], QT[:, pair, t * P:(t + 1) * P],
                                           KB[:, pair, t, :], start=False, stop=True, skip_group_check=True)
                        mm.then_inc(filled[slots.slot(key)], 1)

                scores(0)
                for t in range(TT):
                    if t + 1 < TT:
                        scores(t + 1)
                    pe.wait_ge(spread, c * TT + t + 1)
                    for q in range(4):
                        key = ("pt", t, q)
                        wait_free(pe, key, c)
                        for a in range(4):
                            mm = pe.transpose(bank(key)[:, a * P:(a + 1) * P], Pe[:, 4 * q + a, :], ident[:, :])
                        mm.then_inc(filled[slots.slot(key)], 1)
                    for k in range(2):
                        key = ("o", t, k)
                        wait_free(pe, key, c)
                        for q in (2 * k, 2 * k + 1):
                            pe.wait_ge(drained[slots.slot(("pt", t, q))], slots.drained(("pt", t, q), c))
                        for pair in range(4 * k, 4 * k + 4):
                            for hh in range(2):
                                h = 2 * pair + hh
                                mm = pe.matmul(bank(key)[hh * HD:(hh + 1) * HD, (pair % 4) * P:(pair % 4 + 1) * P],
                                               V[:, t, h * HD:(h + 1) * HD], PT[:, h, :], start=True, stop=True)
                        mm.then_inc(filled[6 + k], 1)
                    key = ("y", t)
                    wait_free(pe, key, c)
                    pe.wait_ge(otl, (c * TT + t) * 2 + 2)
                    a = 0
                    for pair in range(PAIRS):
                        for lhsT, rhs in three_terms(OT[0][:, pair, :], OT[1][:, pair, :],
                                                     wp[0][:, pair * D:(pair + 1) * D], wp[1][:, pair * D:(pair + 1) * D]):
                            mm = pe.matmul(bank(key)[:, 0:D], lhsT, rhs, start=(a == 0), stop=(a == 3 * PAIRS - 1))
                            a += 1
                    mm.then_inc(filled[slots.slot(key)], 1)

            @block.tensor
            def _(pe):
                pe.wait_ge(consts, 4 + 15 + 8 + 4)
                with pe.Fori(0, CH // 2) as i:
                    for half in range(2):
                        chunk(pe, i, 2 * i + half, half)

            @block.scalar
            def _(act):
                act.wait_ge(consts_in, 64)
                with act.Fori(0, CH) as c:
                    for k in range(KD):
                        wait_filled(act, ("x", k), c)
                        act.activation(xT[0][:, k, :], bank(("x", k)), ACT.Copy).then_inc(xh, 1)
                    for n in range(8, 16):
                        wait_filled(act, ("proj", n), c)
                        act.activation(QT[:, n - 8, :], bank(("proj", n)), ACT.Identity, bias=bq_sb[:, n - 8:n - 7]
                                       ).then_inc(drained[slots.slot(("proj", n))], 1)
                    for t in range(TT):
                        act.wait_ge(compact, c * TT + t + 1)
                        act.activation(Sc[:, t % 2], Sc[:, t % 2], ACT.Exp, scale=SCALE).then_inc(exped, 1)
                        for q in range(4):
                            key = ("pt", t, q)
                            wait_filled(act, key, c)
                            if q == 0 and t:
                                wait_filled(act, ("o", t - 1, 1), c)
                            act.activation(PT[:, 4 * q:4 * q + 4, :].rearrange("p h n -> p (h n)"), bank(key), ACT.Copy
                                           ).then_inc(drained[slots.slot(key)], 1)
                        for k in range(2):
                            key = ("o", t, k)
                            wait_filled(act, key, c)
                            if k == 0 and t:
                                wait_filled(act, ("y", t - 1), c)
                            act.activation(OT[0][:, 4 * k:4 * k + 4, :].rearrange("p h n -> p (h n)"), bank(key),
                                           ACT.Copy).then_inc(oth, 1)

            @block.vector
            def _(dve):
                LINKS = 5 * TT
                dve.wait_ge(consts, 4 + 15 + 8 + 4)
                dve.wait_ge(consts_in, 64)
                with dve.Fori(0, CH // 2) as i:
                    for half in range(2):
                        c = 2 * i + half
                        made = [0]

                        def link(ins):
                            made[0] += 1
                            ins.then_inc(dchain, 1)
                            dve.wait_ge(dchain, c * LINKS + made[0])

                        for k in range(KD):
                            dve.wait_ge(xh, c * KD + k + 1)
                            ins = dve.tensor_tensor(xT[1][:, k, :], bank(("x", k)), xT[0][:, k, :].bitcast(F32),
                                                    ALU.subtract)
                            ins.then_inc(xl, 1)
                            dve.wait_ge(xl, c * KD + k + 1)
                            dve.sem_inc(drained[6 + k], 1)
                        for n in range(8):
                            wait_filled(dve, ("proj", n), c)
                            for hh in range(2):
                                ins = dve.tensor_scalar(
                                    KB[hh * HD:(hh + 1) * HD, n, :, hh * P:(hh + 1) * P],
                                    bank(("proj", n))[hh * HD:(hh + 1) * HD].rearrange("p (t n) -> p t n", t=TT),
                                    bk_sb[hh * HD:(hh + 1) * HD, n:n + 1], None, ALU.add)
                            ins.then_inc(drained[slots.slot(("proj", n))], 1)
                        for n in range(16, 24):
                            wait_filled(dve, ("proj", n), c)
                            t, h2 = (n - 16) // 2, (n - 16) % 2
                            dve.tensor_tensor(V[:, t, h2 * 512:(h2 + 1) * 512], bank(("proj", n)),
                                              bv_sb[:, h2 * 512:(h2 + 1) * 512], ALU.add
                                              ).then_inc(drained[slots.slot(("proj", n))], 1)

                        def compact_scores(t):
                            for q in range(4):
                                key = ("s", t, q)
                                wait_filled(dve, key, c)
                                ins = dve.tensor_reduce(Sc[:, t % 2, 4 * q:4 * q + 4, :].rearrange("p h t -> p (h t)"),
                                                        bank(key).rearrange("p (a b) -> p a b", b=BI), AX.X, ALU.max)
                                if q < 3:
                                    ins.then_inc(drained[slots.slot(key)], 1)
                            ins.then_inc(drained[slots.slot(key)], 1)
                            dve.wait_ge(drained[slots.slot(key)], slots.drained(key, c))
                            link(dve.tensor_reduce(mx[:, :], Sc[:, t % 2], AX.X, ALU.max))
                            dve.tensor_tensor(Sc[:, t % 2], Sc[:, t % 2], mx[:, :].unsqueeze(2).broadcast_to([P, H, S]),
                                              ALU.subtract).then_inc(compact, 1)

                        def normalise(t):
                            dve.wait_ge(exped, c * TT + t + 1)
                            link(dve.tensor_reduce(den[:, :], Sc[:, t % 2], AX.X, ALU.add))
                            link(dve.reciprocal(den[:, :], den[:, :]))
                            dve.tensor_tensor(Sc[:, t % 2], Sc[:, t % 2], den[:, :].unsqueeze(2).broadcast_to([P, H, S]),
                                              ALU.mult).then_inc(probs, 1)

                        def lo_of_o(t):
                            for k in range(2):
                                dve.wait_ge(oth, (c * TT + t) * 2 + k + 1)
                                dve.tensor_tensor(OT[1][:, 4 * k:4 * k + 4, :].rearrange("p h n -> p (h n)"),
                                                  bank(("o", t, k)),
                                                  OT[0][:, 4 * k:4 * k + 4, :].rearrange("p h n -> p (h n)").bitcast(F32),
                                                  ALU.subtract).then_inc(otl, 1)
                                dve.wait_ge(otl, (c * TT + t) * 2 + k + 1)
                                dve.sem_inc(drained[6 + k], 1)

                        def residual(t):
                            wait_filled(dve, ("y", t), c)
                            dve.wait_ge(biased, c * TT + t + 1)
                            ins = dve.tensor_tensor(y[:, t % 2], bank(("y", t))[:, 0:D], xt[:, half, t], ALU.add)
                            slot = slots.slot(("y", t))
                            ins.then_inc(drained[slot], 1)
                            dve.wait_ge(drained[slot], slots.drained(("y", t), c))
                            link(dve.bn_stats(st[:, :], y[:, t % 2]))
                            dve.sem_inc(stats_taken, 1)
                            link(dve.bn_aggr(mv[:, :], st[:, :]))
                            dve.tensor_scalar(ve[:, :], mv[:, 1:2], EPS, None, ALU.add).then_inc(var_ready, 1)

                        def norm(t):
                            dve.wait_ge(rstd_ready, c * TT + t + 1)
                            if t == 0:
                                dve.wait_ge(stored[half], i * (16 * S))
                            dve.tensor_scalar(x1t[:, half, t], y[:, t % 2], mv[:, 0:1], rs[:, :], ALU.subtract,
                                              ALU.mult).then_inc(x1_ready, 1)

                        compact_scores(0)
                        normalise(0)
                        for t in range(TT):
                            if t + 1 < TT:
                                compact_scores(t + 1)
                            if t:
                                residual(t - 1)
                            lo_of_o(t)
                            if t:
                                norm(t - 1)
                            if t + 1 < TT:
                                normalise(t + 1)
                        residual(TT - 1)
                        norm(TT - 1)
                        assert made[0] == LINKS


def cross_attention(nc, x1_dram, context, cos, sin, lg, lb, cg, cb, Wq, Wkv, Wo, bo, x2_dram, ident, identr):
    NT, CT = B // P, CTX // P
    HG, PG = H // 2, PAIRS // 2
    LO, HI = math.exp(-CLIP), math.exp(CLIP)
    with ExitStack() as ctx:
        def sb(name, shape, dt=F32):
            return ctx.enter_context(nc.sbuf_tensor(name, shape, dt))

        def sem(name):
            return ctx.enter_context(nc.semaphore(name))

        wq = [sb(f"b_wq_{n}", [P, KD * INNER], F32R) for n in "hl"]
        wk = [sb(f"b_wk_{n}", [P, KD * INNER], F32R) for n in "hl"]
        wv = [sb(f"b_wv_{n}", [P, KD * INNER], F32R) for n in "hl"]
        wo = [sb(f"b_wo_{n}", [P, PAIRS * D], F32R) for n in "hl"]
        kv = Wkv.rearrange("(k p) n -> p k n", p=P)
        parts = []
        for (hi, lo), src in ((wk, kv[:, :, 0:INNER]), (wv, kv[:, :, INNER:2 * INNER]),
                              (wq, Wq.rearrange("(k p) n -> p k n", p=P)), (wo, Wo.rearrange("(k p) n -> p k n", p=P))):
            parts.append((src, hi[:, :], lo[:, :]))
        split_weights(nc, ctx, "b_w", parts)

        cos_sb = sb("b_cos", [P, CT, HD // 2])
        sin_sb = sb("b_sin", [P, CT, 2, HD // 2])
        ones = sb("b_ones", [P, HD])
        gam = sb("b_gam", [P, 2, KD])
        bet = sb("b_bet", [P, 2, KD])
        bo_sb = sb("b_bo", [P, D])
        mhalf = sb("b_mhalf", [P, CT + NT])
        rows = sb("b_rows", [P, CT + NT, D])
        x1 = sb("b_x1", [P, NT, D])
        cT = [sb(f"b_cT_{n}", [P, KD, CTX], F32R) for n in "hl"]
        lT = [sb(f"b_lT_{n}", [P, KD, B], F32R) for n in "hl"]
        KT = sb("b_KT", [P, HG, CTX], F32R)
        V = sb("b_V", [P, CT, HG * HD])
        QQ = sb("b_QQ", [P, 2, 2, 2, B], F32R)
        OT = [sb(f"b_OT_{n}", [P, PG, B], F32R) for n in "hl"]
        probs = sb("b_probs", [P, 4, 2 * B])
        krot = probs[:, 0, :].rearrange("p (a n) -> p a n", a=2)
        kswap = probs[:, 1, 0:HG * HD]
        knat = QQ[:, 1].rearrange("p a b n -> p (a b n)").rearrange("p (t n) -> p t n", t=2)
        acc = sb("b_acc", [P, 2, B])
        accf = sb("b_accf", [P, 2, B])
        r = sb("b_r", [P, B])
        o = sb("b_o", [P, B])
        zc = sb("b_zc", [P, 512])
        zl = [probs[:, 3, 0:B], probs[:, 3, B:2 * B]]
        st = sb("b_st", [P, CT + NT, 6])
        mv = sb("b_mv", [P, CT + NT, 2])
        ve = sb("b_ve", [P, CT + NT])
        rs = sb("b_rs", [P, CT + NT])
        ps = ctx.enter_context(nc.psum_tensor("b_ps", [P, 8, 512], F32))

        Q0_AT = 5

        def cx_step(p):
            return 3 if p + 1 < PG else 1

        banks = {"A": 0, "B": 2, 4: 4, 5: 5, 6: 6, 7: 7}
        order = []
        for g in range(2):
            for t in range(CT):
                order.append((("kv", g, t), "AB"[t % 2] if t <= Q0_AT else "BA"[t % 2]))
                if g == 0 and t < KD:
                    order.append((("lx", t), 6 + t))
                if t == Q0_AT:
                    order.append((("q", g, 0), "A"))
                if t >= 2:
                    order += [(("kt", g, t - 2, a), 4 + 2 * (t % 2) + a) for a in range(2)]
            order += [(("kt", g, t, a), 4 + 2 * (t % 2) + a) for t in (CT - 2, CT - 1) for a in range(2)]
            order += [(("s", g, 0, 0, hh), "AB"[hh]) for hh in range(2)]
            for p in range(PG):
                for j in range(4):
                    if (p, j) != (PG - 1, 3):
                        pn, jn = (p, j + 1) if j < 3 else (p + 1, 0)
                        order += [(("s", g, pn, jn, hh), "AB"[hh]) for hh in range(2)]
                    if j == 0:
                        if p:
                            order.append((("sum", g, p - 1), 6))
                        if p + 1 < PG:
                            order.append((("q", g, p + 1), 7))
                        order.append((("o", g, p), 4 + p % 2))
                    if g == 1 and j == cx_step(p):
                        order.append((("cx", p), 7))
            order += [(("sum", g, PG - 1), 6), (("y", g, 0), 7), (("y", g, 1), 4)]
        slots = Slots(order, {"A": 2, "B": 2}, ("o", "cx"))
        filled = {s: sem(f"b_filled{s}") for s in banks}
        drained = {s: sem(f"b_drained{s}") for s in banks}
        consts = sem("b_consts")
        consts_in = sem("b_consts_in")
        ctx_in = sem("b_ctx_in")
        lat_in = sem("b_lat_in")
        x1_in = sem("b_x1_in")
        cx_turned = sem("b_cx_turned")
        q_ready = sem("b_q_ready")
        q_spread = sem("b_q_spread")
        var_ready = sem("b_var_ready")
        rstd_ready = sem("b_rstd_ready")
        normed = sem("b_normed")
        biased = sem("b_biased")
        z_ready = sem("b_z_ready")
        zh_ready = sem("b_zh_ready")
        zl_ready = sem("b_zl_ready")
        rotated = sem("b_rotated")
        kh_ready = sem("b_kh_ready")
        knat_ready = sem("b_knat_ready")
        qh_ready = sem("b_qh_ready")
        exped = sem("b_exped")
        clipped = sem("b_clipped")
        pv_done = sem("b_pv_done")
        acc_ready = sem("b_acc_ready")
        accf_ready = sem("b_accf_ready")
        pchain = sem("b_pchain")
        dchain = sem("b_dchain")
        oh_ready = sem("b_oh_ready")
        ot_ready = sem("b_ot_ready")
        out_ready = sem("b_out_ready")
        stats_taken = sem("b_stats_taken")
        stored = sem("b_stored")

        def wait_filled(eng, key, b):
            eng.wait_ge(filled[slots.slot(key)], slots.filled(key, b))

        def wait_free(eng, key, b):
            eng.wait_ge(drained[slots.slot(key)], slots.free(key, b))

        def wait_drained(eng, key, b):
            eng.wait_ge(drained[slots.slot(key)], slots.drained(key, b))

        def bank(key, a=0):
            return ps[:, banks[slots.slot(key)] + a, :]

        def both(key):
            n = banks[slots.slot(key)]
            return ps[:, n:n + 2, :].rearrange("p a n -> p (a n)")

        def fill(key, ins):
            ins.then_inc(filled[slots.slot(key)], 1)

        def drain(key, ins, n=1):
            ins.then_inc(drained[slots.slot(key)], n)

        def step(g, p, j):
            return (g * PG + p) * 4 + j

        def block_rows(c):
            return c % KD, 4 * (c // KD)

        ZB = 2 * KD
        ZN = ZB + KD
        ROWS = CT + NT
        NCONST = 4
        with nc.Block() as block:

            @block.sync
            def _(sp):
                for half in (0, 1):
                    sp.dma_start(sin_sb[:, :, half, :], sin.rearrange("(t p) n -> p t n", p=P)).then_inc(consts_in, 16)
                sp.dma_start(cos_sb[:, :, :], cos.rearrange("(t p) n -> p t n", p=P)).then_inc(consts_in, 16)
                for n, (g_in, b_in) in enumerate(((cg, cb), (lg, lb))):
                    sp.dma_start(gam[:, n, :], g_in.rearrange("(k p) -> p k", p=P), allow_slow_non_contiguous=True
                                 ).then_inc(consts_in, 16)
                    sp.dma_start(bet[:, n, :], b_in.rearrange("(k p) -> p k", p=P), allow_slow_non_contiguous=True
                                 ).then_inc(consts_in, 16)
                sp.dma_start(bo_sb[:, :], bo.partition_broadcast(P)).then_inc(consts_in, 16)

                def load(what, b):
                    dst, src, done = {"context": (rows[:, 0:CT, :], context, ctx_in),
                                      "latents": (rows[:, CT:ROWS, :], x1_dram, lat_in),
                                      "residual": (x1[:, :, :], x1_dram, x1_in)}[what]
                    sp.dma_start(dst, src[bass.ds(b, 1)].rearrange("a (t p) d -> p (a t) d", p=P)).then_inc(done, 16)

                def spread(b, g, p):
                    n = g * PG + p
                    sp.wait_ge(q_ready, b * (2 * PG) + n + 1)
                    for hh in range(2):
                        here, there = slice(hh * HD, (hh + 1) * HD), slice((1 - hh) * HD, (2 - hh) * HD)
                        sp.dma_start(QQ[there, n % 2, hh, :, :].bitcast(F32), QQ[here, n % 2, hh, :, :].bitcast(F32)
                                     ).then_inc(q_spread, 16)

                load("context", 0)
                load("latents", 0)
                with sp.Fori(0, S) as b:
                    sp.wait_ge(z_ready, ZB + b * ZN)
                    load("context", (b + 1) % S)
                    sp.wait_ge(stored, b * 16)
                    load("residual", b)
                    sp.wait_ge(z_ready, ZB + b * ZN + KD)
                    load("latents", (b + 1) % S)
                    for g in range(2):
                        for p in range(PG):
                            spread(b, g, p)
                    sp.wait_ge(out_ready, (b + 1) * NT)
                    sp.dma_start(x2_dram[bass.ds(b, 1)].rearrange("a (t p) d -> p (a t) d", p=P), x1[:, :, :]
                                 ).then_inc(stored, 16)
                sp.wait_ge(stored, 16 * S)

            @block.gpsimd
            def _(pool):
                pool.memset(ones[:, :], 1.0).then_inc(consts, 1)
                pool.memset(mhalf[:, :], -0.5).then_inc(consts, 1)
                pool.wait_ge(consts_in, 16 * 8)
                pool.tensor_scalar(sin_sb[:, :, 0, :], sin_sb[:, :, 0, :], -1.0, None, ALU.mult).then_inc(consts, 1)
                pool.wait_ge(consts, 3)
                pool.sem_inc(consts, 1)
                pool.wait_ge(var_ready, 1)
                pool.tensor_tensor(rs[:, :], ve[:, :], mhalf[:, :], ALU.pow).then_inc(rstd_ready, 1)
                with pool.Fori(0, S) as b:
                    links = 0
                    for g in range(2):
                        for t in range(CT):
                            pool.wait_ge(kh_ready, b * (2 * CT) + (g * CT + t + 1))
                            nat = knat[:, t % 2, :].rearrange("p (h a n) -> p h a n", a=2, n=HD)
                            pool.tensor_tensor(nat[:, :, 1, :], krot[:, t % 2, :].rearrange("p (h n) -> p h n", n=HD),
                                               nat[:, :, 0, :].bitcast(F32), ALU.subtract).then_inc(knat_ready, 1)
                        if g == 0:
                            pool.wait_ge(x1_in, (b + 1) * 16)
                            pool.tensor_tensor(x1[:, :, :], x1[:, :, :],
                                               bo_sb[:, :].unsqueeze(1).broadcast_to([P, NT, D]), ALU.add
                                               ).then_inc(biased, 1)
                        for p in range(PG):
                            for j in range(3):
                                for hh in range(2):
                                    pool.wait_ge(clipped, b * (16 * PG) + (step(g, p, j) * 2 + hh + 1))
                                    pr = probs[:, 2 * (j % 2) + hh, :]
                                    if j == 0:
                                        pool.wait_ge(accf_ready, b * (4 * PG) + ((g * PG + p) * 2))
                                        ins = pool.tensor_tensor(acc[:, hh, :], pr[:, 0:B], pr[:, B:2 * B], ALU.add)
                                    else:
                                        ins = pool.tensor_tensor(acc[:, hh, :], acc[:, hh, :], pr[:, 0:B], ALU.add)
                                        links += 1
                                        ins.then_inc(pchain, 1)
                                        pool.wait_ge(pchain, b * (16 * PG // 2) + links)
                                        ins = pool.tensor_tensor(acc[:, hh, :], acc[:, hh, :], pr[:, B:2 * B], ALU.add)
                                    ins.then_inc(acc_ready, 1)
                                    pool.wait_ge(acc_ready, b * (12 * PG) + ((g * PG + p) * 3 + j) * 2 + hh + 1)
                                if (g, p, j) == (1, 0, 0):
                                    pool.wait_ge(var_ready, 2 * b + 2)
                                    pool.tensor_tensor(rs[:, :], ve[:, :], mhalf[:, :], ALU.pow).then_inc(rstd_ready, 1)
                    assert links == 8 * PG
                    pool.wait_ge(var_ready, 2 * b + 3)
                    pool.tensor_tensor(rs[:, 0:NT], ve[:, 0:NT], mhalf[:, 0:NT], ALU.pow).then_inc(rstd_ready, 1)

            def scores(pe, b, g, p, j):
                n = g * PG + p
                for hh in range(2):
                    key = ("s", g, p, j, hh)
                    wait_free(pe, key, b)
                    if j == 0 and hh == 0:
                        pe.wait_ge(q_spread, b * (32 * 2 * PG) + 32 * (n + 1))
                    if p == 0:
                        for a in range(2):
                            wait_drained(pe, ("kt", g, 2 * j + 1, a), b)
                            wait_drained(pe, ("kt", g, 2 * j, a), b)
                    for a in range(2):
                        t = 2 * j + a
                        k = KT[:, 2 * p + hh, t * P:(t + 1) * P]
                        pe.matmul(bank(key, a), k, QQ[:, n % 2, hh, 0, :], start=True, stop=False)
                        mm = pe.matmul(bank(key, a), k, QQ[:, n % 2, hh, 1, :], start=False, stop=True)
                    fill(key, mm)

            def queries(pe, b, g, p):
                key = ("q", g, p)
                wait_free(pe, key, b)
                col = (g * PG + p) * P
                terms = [u for k in range(KD) for u in three_terms(
                    wq[0][:, k * INNER + col:k * INNER + col + P], wq[1][:, k * INNER + col:k * INNER + col + P],
                    lT[0][:, k, :], lT[1][:, k, :])]
                for a, (lhsT, rhs) in enumerate(terms):
                    mm = pe.matmul(bank(key), lhsT, rhs, start=(a == 0), stop=(a == len(terms) - 1))
                fill(key, mm)

            def sums(pe, b, g, p):
                key = ("sum", g, p)
                wait_free(pe, key, b)
                pe.wait_ge(accf_ready, b * (4 * PG) + (g * PG + p + 1) * 2)
                for hh in range(2):
                    mm = pe.matmul(bank(key)[hh * HD:(hh + 1) * HD, :], ones[:, :], accf[:, hh, :],
                                   start=True, stop=True)
                fill(key, mm)

            def keys_values(pe, b, g, t):
                key = ("kv", g, t)
                wait_free(pe, key, b)
                if g == 0 and t in (0, CT // 2):
                    pe.wait_ge(zl_ready, b * ZN + (ZB if t else KD))
                for a, w in enumerate((wk, wv)):
                    n = 0
                    for k in range(KD):
                        c0 = k * INNER + g * HG * HD
                        for lhsT, rhs in three_terms(cT[0][:, k, t * P:(t + 1) * P], cT[1][:, k, t * P:(t + 1) * P],
                                                     w[0][:, c0:c0 + HG * HD], w[1][:, c0:c0 + HG * HD]):
                            mm = pe.matmul(bank(key, a), lhsT, rhs, start=(n == 0), stop=(n == 3 * KD - 1))
                            n += 1
                fill(key, mm)

            def context_turn(pe, c, dst, before):
                k, t0 = block_rows(c)
                pe.wait_ge(normed, before + t0 + 4)
                for a in range(4):
                    mm = pe.transpose(dst[:, a * P:(a + 1) * P], rows[:, t0 + a, k * P:(k + 1) * P], ident[:, :])
                mm.then_inc(cx_turned, 1)

            @block.tensor
            def _(pe):
                pe.wait_ge(consts, NCONST)
                for c in range(ZB):
                    context_turn(pe, c, ps[:, 4 + c, :], 0)
                keys_values(pe, 0, 0, 0)
                with pe.Fori(0, S) as b:
                    def latents_turn(k):
                        key = ("lx", k)
                        wait_free(pe, key, b)
                        if k == 0:
                            pe.wait_ge(normed, (b + 1) * ROWS)
                            pe.wait_ge(z_ready, ZB + b * ZN)
                        for t in range(NT):
                            mm = pe.transpose(bank(key)[:, t * P:(t + 1) * P], rows[:, CT + t, k * P:(k + 1) * P],
                                              ident[:, :])
                        fill(key, mm)

                    def k_turn(g, t):
                        pe.wait_ge(knat_ready, b * (2 * CT) + (g * CT + t + 1))
                        for a in range(2):
                            key = ("kt", g, t, a)
                            wait_free(pe, key, b)
                            for h in range(4 * a, 4 * a + 4):
                                mm = pe.transpose(bank(key)[:, (h - 4 * a) * P:(h - 4 * a + 1) * P].bitcast(F32R),
                                                  knat[:, t % 2, h * 2 * HD:(h + 1) * 2 * HD], identr[:, :])
                            fill(key, mm)

                    for g in range(2):
                        for t in range(CT):
                            if t:
                                keys_values(pe, b, g, t)
                            if g == 0 and t < KD:
                                latents_turn(t)
                            if t == Q0_AT:
                                if g == 0:
                                    pe.wait_ge(zl_ready, ZB + b * ZN + KD)
                                queries(pe, b, g, 0)
                            if t >= 2:
                                k_turn(g, t - 2)
                        k_turn(g, CT - 2)
                        k_turn(g, CT - 1)
                        scores(pe, b, g, 0, 0)
                        for p in range(PG):
                            for j in range(4):
                                if j < 3:
                                    scores(pe, b, g, p, j + 1)
                                elif p + 1 < PG:
                                    scores(pe, b, g, p + 1, 0)
                                if j == 0 and p:
                                    sums(pe, b, g, p - 1)
                                if j == 0 and p + 1 < PG:
                                    queries(pe, b, g, p + 1)
                                if g == 1 and j == cx_step(p):
                                    wait_free(pe, ("cx", p), b)
                                    context_turn(pe, p, bank(("cx", p)), (b + 1) * ROWS)
                                key = ("o", g, p)
                                if j == 0:
                                    wait_free(pe, key, b)
                                pe.wait_ge(clipped, b * (16 * PG) + (step(g, p, j) + 1) * 2)
                                for t in (2 * j, 2 * j + 1):
                                    for hh in range(2):
                                        mm = pe.matmul(bank(key)[hh * HD:(hh + 1) * HD, :],
                                                       V[:, t, (2 * p + hh) * HD:(2 * p + hh + 1) * HD],
                                                       probs[:, 2 * (j % 2) + hh, (t % 2) * B:(t % 2 + 1) * B],
                                                       start=(t == 0), stop=(t == CT - 1))
                                mm.then_inc(pv_done, 1)
                        def project(a, pairs):
                            for t in (2 * a, 2 * a + 1):
                                for p in pairs:
                                    c0 = (g * PG + p) * D
                                    for n, (lhsT, rhs) in enumerate(three_terms(
                                            OT[0][:, p, t * P:(t + 1) * P], OT[1][:, p, t * P:(t + 1) * P],
                                            wo[0][:, c0:c0 + D], wo[1][:, c0:c0 + D])):
                                        mm = pe.matmul(bank(("y", g, a))[:, (t % 2) * D:(t % 2 + 1) * D], lhsT, rhs,
                                                       start=(t % 2 == 0 and p == 0 and n == 0), stop=(p >= PG - 2 and n == 2),
                                                       skip_group_check=True)
                            return mm

                        sums(pe, b, g, PG - 1)
                        keys_values(pe, b + 1 if g == 1 else b, 1 - g, 0)
                        pe.wait_ge(ot_ready, b * (2 * PG) + (g + 1) * PG - 1)
                        for a in range(2):
                            wait_free(pe, ("y", g, a), b)
                            project(a, range(PG - 1))
                        pe.wait_ge(ot_ready, b * (2 * PG) + (g + 1) * PG)
                        for a in range(2):
                            fill(("y", g, a), project(a, [PG - 1]))

            @block.scalar
            def _(act):
                act.wait_ge(consts, NCONST)

                def q_hi(b, g, p):
                    key = ("q", g, p)
                    wait_filled(act, key, b)
                    n = g * PG + p
                    for hh in range(2):
                        own = slice(hh * HD, (hh + 1) * HD)
                        ins = act.activation(QQ[own, n % 2, hh, 0, :], bank(key)[own, :], ACT.Copy)
                    ins.then_inc(qh_ready, 1)

                def o_hi(b, g, p):
                    wait_drained(act, ("o", g, p), b)
                    act.activation(OT[0][:, p, :], o[:, :], ACT.Copy).then_inc(oh_ready, 1)

                def z_split(n, src, which, k, z, hi):
                    act.activation(z, src, ACT.Identity, scale=gam[:, which, k:k + 1],
                                   bias=bet[:, which, k:k + 1]).then_inc(z_ready, 1)
                    act.wait_ge(z_ready, n + 1)
                    act.activation(hi, z, ACT.Copy).then_inc(zh_ready, 1)

                for c in range(ZB):
                    k, t0 = block_rows(c)
                    act.wait_ge(cx_turned, c + 1)
                    z_split(c, ps[:, 4 + c, :], 0, k, probs[:, c, 0:512], cT[0][:, k, t0 * P:(t0 + 4) * P])
                def v_read(b, g, t):
                    key = ("kv", g, t)
                    wait_filled(act, key, b)
                    drain(key, act.activation(V[:, t, :], bank(key, 1), ACT.Copy))

                def k_hi(b, g, t):
                    act.wait_ge(rotated, b * (2 * CT) + (g * CT + t + 1))
                    act.activation(knat[:, t % 2, :].rearrange("p (h a n) -> p h a n", a=2, n=HD)[:, :, 0, :],
                                   krot[:, t % 2, :].rearrange("p (h n) -> p h n", n=HD), ACT.Copy
                                   ).then_inc(kh_ready, 1)

                v_read(0, 0, 0)
                k_hi(0, 0, 0)
                with act.Fori(0, S) as b:
                    def context_split(c):
                        k, t0 = block_rows(c)
                        act.wait_ge(cx_turned, ZB * (b + 1) + c + 1)
                        if c:
                            act.wait_ge(zl_ready, ZB + b * ZN + KD + c)
                        z_split(ZB + b * ZN + KD + c, bank(("cx", c)), 0, k, zc[:, :], cT[0][:, k, t0 * P:(t0 + 4) * P])
                        act.sem_inc(drained[slots.slot(("cx", c))], 1)

                    for g in range(2):
                        def k_turned(t):
                            for a in range(2):
                                key = ("kt", g, t, a)
                                wait_filled(act, key, b)
                                drain(key, act.activation(KT[:, 4 * a:4 * a + 4, t * P:(t + 1) * P],
                                                          bank(key).rearrange("p (h n) -> p h n", n=P), ACT.Copy))

                        for t in range(CT):
                            if t:
                                v_read(b, g, t)
                            if t >= 2:
                                k_turned(t - 2)
                            if g == 0 and t < KD:
                                wait_filled(act, ("lx", t), b)
                                z_split(ZB + b * ZN + t, bank(("lx", t)), 1, t, zl[t], lT[0][:, t, :])
                                act.sem_inc(drained[slots.slot(("lx", t))], 1)
                            if t:
                                k_hi(b, g, t)
                            if t == Q0_AT:
                                q_hi(b, g, 0)
                        k_turned(CT - 2)
                        k_turned(CT - 1)
                        for p in range(PG):
                            for j in range(4):
                                for hh in range(2):
                                    key = ("s", g, p, j, hh)
                                    wait_filled(act, key, b)
                                    if (p, j) >= (0, 2):
                                        before = step(g, p, j) - 2
                                        act.wait_ge(pv_done, b * (8 * PG) + before + 1)
                                        if before % 4 == 3:
                                            act.wait_ge(accf_ready, b * (4 * PG) + (before // 4) * 2 + hh + 1)
                                        else:
                                            act.wait_ge(acc_ready, b * (12 * PG)
                                                        + ((before // 4) * 3 + before % 4) * 2 + hh + 1)
                                    ins = act.activation(probs[:, 2 * (j % 2) + hh, :], both(key), ACT.Exp, scale=SCALE)
                                    drain(key, ins, 2)
                                    if g == 1 and p and (j, hh) == (0, 0):
                                        context_split(p - 1)
                                    if g == 1 and p == PG - 1 and (j, hh) == (2, 0):
                                        context_split(p)
                                if j == 1 and p + 1 < PG:
                                    q_hi(b, g, p + 1)
                                if j == 3 and p:
                                    o_hi(b, g, p - 1)
                        last = g == 1
                        v_read(b + 1 if last else b, 1 - g, 0)
                        o_hi(b, g, PG - 1)
                        k_hi(b + 1 if last else b, 1 - g, 0)

            @block.vector
            def _(dve):
                dve.wait_ge(consts, NCONST)
                LINKS = 2 * (CT + PG) + 2
                made = [0]

                def link(ins, b):
                    made[0] += 1
                    ins.then_inc(dchain, 1)
                    dve.wait_ge(dchain, b * LINKS + made[0])

                def row_sums(t):
                    return dve.bn_stats(st[:, t, :], rows[:, t, :]).then_inc(stats_taken, 1)

                def variances(b, taken):
                    dve.wait_ge(stats_taken, taken)
                    dve.sem_inc(stats_taken, 1)
                    for t in range(ROWS):
                        ins = dve.bn_aggr(mv[:, t, :], st[:, t, :])
                    link(ins, b)
                    dve.tensor_scalar(ve[:, :], mv[:, :, 1], EPS, None, ALU.add).then_inc(var_ready, 1)

                def normalise(t, dst, src, done):
                    dve.tensor_scalar(dst, src, mv[:, t, 0:1], rs[:, t:t + 1], ALU.subtract, ALU.mult).then_inc(done, 1)

                def z_lo(n, z, hi, lo):
                    dve.wait_ge(zh_ready, n + 1)
                    dve.tensor_tensor(lo, z, hi.bitcast(F32), ALU.subtract).then_inc(zl_ready, 1)

                def k_cos(b, g, t):
                    key = ("kv", g, t)
                    wait_filled(dve, key, b)
                    if t >= 2:
                        dve.wait_ge(knat_ready, b * (2 * CT) + (g * CT + t - 1))
                    dve.tensor_tensor(krot[:, t % 2, :].rearrange("p (h n) -> p h n", n=HD // 2),
                                      bank(key).rearrange("p (h n) -> p h n", n=HD // 2),
                                      cos_sb[:, t, :].unsqueeze(1).broadcast_to([P, 2 * HG, HD // 2]), ALU.mult)

                def k_sin(b, g, t, at):
                    key = ("kv", g, t)
                    dve.wait_ge(rotated, b * (2 * CT) + (g * CT + t))
                    link(dve.tensor_tensor(
                        kswap.rearrange("p (h a n) -> p h a n", a=2, n=HD // 2),
                        bank(key).rearrange("p (h a n) -> p h a n", a=2, n=HD // 2)[:, :, ::-1, :],
                        sin_sb[:, t, :, :].unsqueeze(1).broadcast_to([P, HG, 2, HD // 2]), ALU.mult), at)
                    dve.sem_inc(drained[slots.slot(key)], 1)
                    dve.tensor_tensor(krot[:, t % 2, :], krot[:, t % 2, :], kswap, ALU.add).then_inc(rotated, 1)

                dve.wait_ge(ctx_in, 16)
                dve.wait_ge(lat_in, 16)
                for t in range(ROWS):
                    row_sums(t)
                variances(0, ROWS)
                dve.wait_ge(rstd_ready, 1)
                for t in range(ROWS):
                    normalise(t, rows[:, t, :], rows[:, t, :], normed)
                for c in range(ZB):
                    k, t0 = block_rows(c)
                    cols = slice(t0 * P, (t0 + 4) * P)
                    z_lo(c, probs[:, c, 0:512], cT[0][:, k, cols], cT[1][:, k, cols])
                k_cos(0, 0, 0)
                k_sin(0, 0, 0, 0)
                TAKEN = ROWS + 1 + NT + 1
                FIRST = ROWS + 1
                with dve.Fori(0, S) as b:
                    def context_lo(c):
                        k, t0 = block_rows(c)
                        cols = slice(t0 * P, (t0 + 4) * P)
                        z_lo(ZB + b * ZN + KD + c, zc[:, :], cT[0][:, k, cols], cT[1][:, k, cols])

                    for g in range(2):
                        def q_lo(p):
                            key = ("q", g, p)
                            n = g * PG + p
                            dve.wait_ge(qh_ready, b * (2 * PG) + n + 1)
                            for hh in range(2):
                                own = slice(hh * HD, (hh + 1) * HD)
                                ins = dve.tensor_tensor(QQ[own, n % 2, hh, 1, :], bank(key)[own, :],
                                                        QQ[own, n % 2, hh, 0, :].bitcast(F32), ALU.subtract)
                            ins.then_inc(q_ready, 1)
                            dve.wait_ge(q_ready, b * (2 * PG) + n + 1)
                            dve.sem_inc(drained[slots.slot(key)], 2 if p == 0 else 1)

                        for t in range(CT):
                            if t:
                                k_cos(b, g, t)
                                k_sin(b, g, t, b)
                            if g == 0 and t < KD:
                                z_lo(ZB + b * ZN + t, zl[t], lT[0][:, t, :], lT[1][:, t, :])
                            if t == Q0_AT:
                                q_lo(0)
                        def inverse(p, a):
                            key = ("sum", g, p)
                            if a == 0:
                                wait_filled(dve, key, b)
                                if p:
                                    wait_drained(dve, ("o", g, p - 1), b)
                            ins = dve.reciprocal(r[:, a * P:(a + 1) * P], bank(key)[:, a * P:(a + 1) * P])
                            if a == 3:
                                drain(key, ins)

                        def o_scaled(p):
                            wait_drained(dve, ("sum", g, p), b)
                            dve.wait_ge(ot_ready, b * (2 * PG) + (g * PG + p))
                            drain(("o", g, p), dve.tensor_tensor(o[:, :], bank(("o", g, p)), r[:, :], ALU.mult))

                        def o_lo(p):
                            dve.wait_ge(oh_ready, b * (2 * PG) + (g * PG + p + 1))
                            dve.tensor_tensor(OT[1][:, p, :], o[:, :], OT[0][:, p, :].bitcast(F32), ALU.subtract
                                              ).then_inc(ot_ready, 1)

                        for p in range(PG):
                            for j in range(4):
                                for hh in range(2):
                                    n = step(g, p, j) * 2 + hh
                                    at = (j, hh)
                                    pr = probs[:, 2 * (j % 2) + hh, :]
                                    wait_drained(dve, ("s", g, p, j, hh), b)
                                    dve.tensor_scalar(pr, pr, HI, LO, ALU.min, ALU.max).then_inc(clipped, 1)
                                    if p and at == (3, 0):
                                        o_scaled(p - 1)
                                    if j == 3:
                                        dve.wait_ge(clipped, b * (16 * PG) + n + 1)
                                        ins = dve.tensor_tensor(accf[:, hh, :], pr[:, 0:B], pr[:, B:2 * B], ALU.add)
                                        if hh == 1:
                                            link(ins, b)
                                            for h2 in range(2):
                                                dve.wait_ge(acc_ready, b * (12 * PG) + ((g * PG + p) * 3 + 2) * 2 + h2 + 1)
                                                dve.tensor_tensor(accf[:, h2, :], accf[:, h2, :], acc[:, h2, :], ALU.add
                                                                  ).then_inc(accf_ready, 1)
                                    if p and at in ((1, 0), (2, 0), (2, 1)):
                                        inverse(p - 1, {(1, 0): 0, (2, 0): 1, (2, 1): 2}[at])
                                        if at == (2, 1):
                                            inverse(p - 1, 3)
                                    if p + 1 < PG and at == (1, 1):
                                        q_lo(p + 1)
                                    if p >= 2 and at == (0, 0):
                                        o_lo(p - 2)
                                    if g == 0 and at == (0, 1):
                                        if p == 0:
                                            dve.wait_ge(ctx_in, (b + 2) * 16)
                                            dve.wait_ge(lat_in, (b + 2) * 16)
                                        for t in (2 * p, 2 * p + 1, CT + p):
                                            row_sums(t)
                                    if (g, p) == (1, 0) and at == (0, 1):
                                        variances(b, FIRST + b * TAKEN + ROWS)
                                    if g == 1 and p < 3 and at == (((2, 0), (0, 1), (0, 1))[p]):
                                        if p == 0:
                                            dve.wait_ge(rstd_ready, 2 * b + 2)
                                        for t in range(4 * p, 4 * p + 4):
                                            normalise(t, rows[:, t, :], rows[:, t, :], normed)
                                    if g == 1 and p and at == (0, 1):
                                        context_lo(p - 1)
                        o_lo(PG - 2)
                        for a in range(4):
                            inverse(PG - 1, a)
                        o_scaled(PG - 1)
                        after = b + 1 if g == 1 else b
                        k_cos(after, 1 - g, 0)
                        o_lo(PG - 1)
                        k_sin(after, 1 - g, 0, b)
                        if g == 1:
                            context_lo(PG - 1)
                        for a in range(2):
                            key = ("y", g, a)
                            wait_filled(dve, key, b)
                            if (g, a) == (0, 0):
                                dve.wait_ge(biased, b + 1)
                            xs = x1[:, 2 * a:2 * a + 2, :].rearrange("p t n -> p (t n)")
                            drain(key, dve.tensor_tensor(xs, bank(key), xs, ALU.add))
                    for a in range(2):
                        wait_drained(dve, ("y", 1, a), b)
                    for t in range(NT):
                        dve.bn_stats(st[:, t, :], x1[:, t, :]).then_inc(stats_taken, 1)
                    dve.wait_ge(stats_taken, FIRST + b * TAKEN + ROWS + 1 + NT)
                    dve.sem_inc(stats_taken, 1)
                    for t in range(NT):
                        ins = dve.bn_aggr(mv[:, t, :], st[:, t, :])
                    link(ins, b)
                    dve.tensor_scalar(ve[:, 0:NT], mv[:, 0:NT, 1], EPS, None, ALU.add).then_inc(var_ready, 1)
                    dve.wait_ge(rstd_ready, 2 * b + 3)
                    for t in range(NT):
                        normalise(t, x1[:, t, :], x1[:, t, :], out_ready)
                assert made[0] == LINKS + 2, (made[0], LINKS)


def experts(nc, x2_dram, Wr, rb, W1, W2, W3, Ws1, Ws2, Ws3, out, ident):
    TOK = S * B
    NT, CH, CT = TOK // P, TOK // 512, 4
    HB = FF // P
    RSCALE = 1.0 / math.sqrt(D)
    with ExitStack() as ctx:
        def sb(name, shape, dt=F32):
            return ctx.enter_context(nc.sbuf_tensor(name, shape, dt))

        def sem(name):
            return ctx.enter_context(nc.semaphore(name))

        y = sb("c_y", [P, NT, D])
        xT = [sb(f"c_xT_{n}", [P, KD, TOK], F32R) for n in "hl"]
        w1 = [[sb(f"c_w1_{n}{k}", [P, KD * FF], F32R) for n in "hl"] for k in range(2)]
        w3 = [[sb(f"c_w3_{n}{k}", [P, KD * FF], F32R) for n in "hl"] for k in range(2)]
        w2 = [[sb(f"c_w2_{n}{k}", [P, HB * D], F32R) for n in "hl"] for k in range(2)]
        raw = sb("c_raw", [P, 3, KD * FF])
        hT = [sb(f"c_hT_{n}", [P, 2, HB, 512], F32R) for n in "hl"]
        gate = sb("c_gate", [P, 2, 512])
        hid = sb("c_hid", [P, 2, 512])
        wr = sb("c_wr", [P, KD, E])
        wrs = [sb(f"c_wr_{n}", [P, KD, E], F32R) for n in "hl"]
        rb_sb = sb("c_rb", [P, E])
        logit = sb("c_logit", [P, NT, E])
        biased = sb("c_biased", [P, NT, E])
        top = sb("c_top", [P, NT, 8])
        topi = sb("c_topi", [P, NT, 8], U32)
        topf = sb("c_topf", [P, 2, NT])
        lane = sb("c_lane", [P, E])
        hot = sb("c_hot", [P, 2, NT, E])
        pick = sb("c_pick", [P, 2, NT])
        pmax = sb("c_pmax", [P, NT])
        prod = sb("c_prod", [P, NT, E])
        share = sb("c_share", [P, NT, 1 + E])
        mhalf = sb("c_mhalf", [P, CT])
        st = sb("c_st", [P, CT, 6])
        mv = sb("c_mv", [P, CT, 2])
        ve = sb("c_ve", [P, CT])
        rs = sb("c_rs", [P, CT])
        ps = ctx.enter_context(nc.psum_tensor("c_ps", [P, 8, 512], F32))

        x_in = [sem(f"c_x_in{c}") for c in range(CH)]
        consts_in = sem("c_consts_in")
        consts = sem("c_consts")
        raw_in = sem("c_raw_in")
        raw_taken = sem("c_raw_taken")
        w_ready = sem("c_w_ready")
        turned = sem("c_turned")
        xh_ready = sem("c_xh_ready")
        xl_ready = sem("c_xl_ready")
        logits_done = sem("c_logits_done")
        logits_read = sem("c_logits_read")
        route_in = sem("c_route_in")
        route_exp = sem("c_route_exp")
        rchain = sem("c_rchain")
        h_filled = [sem(f"c_h_filled{k}") for k in range(2)]
        h_drained = [sem(f"c_h_drained{k}") for k in range(2)]
        y_filled = [sem(f"c_y_filled{k}") for k in range(4)]
        y_drained = [sem(f"c_y_drained{k}") for k in range(4)]
        gated = sem("c_gated")
        hid_ready = sem("c_hid_ready")
        hh_ready = sem("c_hh_ready")
        hl_ready = sem("c_hl_ready")
        var_ready = sem("c_var_ready")
        rstd_ready = sem("c_rstd_ready")
        out_ready = sem("c_out_ready")
        stored = sem("c_stored")
        lchain = sem("c_lchain")

        out_v = out.rearrange("s (t p) d -> s p t d", p=P)
        x2_v = x2_dram.rearrange("s (t p) d -> s p t d", p=P)

        def over_experts(eng, body):
            body(0, 0, True, False)
            with eng.Fori(0, (E - 2) // 2) as i:
                for a in range(2):
                    body(2 * i + (1 + a), 1 - a, False, False)
            for n in range(E - 1, E + 1):
                body(n, n % 2, False, n == E)

        with nc.Block() as block:

            @block.sync
            def _(sp):
                for c in range(CH):
                    sp.dma_start(y[:, c * CT:(c + 1) * CT, :], x2_v[c]).then_inc(x_in[c], 16)
                sp.dma_start(wr[:, :, :], Wr.rearrange("(k p) n -> p k n", p=P)).then_inc(consts_in, 16)
                sp.dma_start(rb_sb[:, :], rb.partition_broadcast(P)).then_inc(consts_in, 16)

                def load(n, par, first, last):
                    sp.wait_ge(w_ready, 6 * n)
                    if first:
                        srcs = (Ws1, Ws3, Ws2)
                    else:
                        srcs = [w[bass.ds(n - 1, 1)].rearrange("e k n -> (e k) n") for w in (W1, W3, W2)]
                    for m, src in enumerate(srcs):
                        sp.dma_start(raw[:, m, :].rearrange("p (k n) -> p k n", n=src.shape[1]),
                                     src.rearrange("(k p) n -> p k n", p=P)).then_inc(raw_in, 16)

                over_experts(sp, load)
                for c in range(CH):
                    sp.wait_ge(out_ready, CT * (c + 1))
                    sp.dma_start(out_v[c], y[:, c * CT:(c + 1) * CT, :]).then_inc(stored, 16)
                sp.wait_ge(stored, 16 * CH)

            @block.gpsimd
            def _(pool):
                pool.iota(topi[:, 0, :], pattern=[[1, E]], base=0, channel_multiplier=0).then_inc(consts, 1)
                pool.memset(mhalf[:, :], -0.5).then_inc(consts, 1)
                pool.wait_ge(consts, 2)
                pool.tensor_copy(lane[:, :], topi[:, 0, :]).then_inc(consts, 1)
                pool.memset(share[:, :, 0], 1.0)
                pool.wait_ge(consts_in, 32)
                pool.tensor_copy(wrs[0][:, :, :], wr[:, :, :]).then_inc(consts, 1)
                pool.wait_ge(consts, 4)
                pool.tensor_tensor(wrs[1][:, :, :], wr[:, :, :], wrs[0][:, :, :].bitcast(F32), ALU.subtract
                                   ).then_inc(consts, 1)

                def split(n, par, first, last):
                    pool.wait_ge(raw_in, (n + 1) * 48)
                    if not first:
                        pool.wait_ge(y_filled[3], (n - 1) * (CH // 2))
                    pool.sem_inc(raw_taken, 1)
                    for m, w in enumerate((w1, w3, w2)):
                        pool.tensor_copy(w[par][0][:, :], raw[:, m, :]).then_inc(w_ready, 1)
                    for m, w in enumerate((w1, w3, w2)):
                        pool.wait_ge(w_ready, n * 6 + m + 1)
                        pool.tensor_tensor(w[par][1][:, :], raw[:, m, :], w[par][0][:, :].bitcast(F32), ALU.subtract
                                           ).then_inc(w_ready, 1)

                over_experts(pool, split)
                for c in range(CH):
                    pool.wait_ge(var_ready, c + 1)
                    pool.tensor_tensor(rs[:, :], ve[:, :], mhalf[:, :], ALU.pow).then_inc(rstd_ready, 1)

            def second(pe, n, c, par, half):
                k = 2 * (c % 2) + half
                pe.wait_ge(y_drained[k], n * (CH // 2) + c // 2)
                if half == 0:
                    pe.wait_ge(hl_ready, (n * CH + c + 1) * HB)
                for t in (2 * half, 2 * half + 1):
                    a = 0
                    for hb in range(HB):
                        for lhsT, rhs in three_terms(hT[0][:, c % 2, hb, t * P:(t + 1) * P],
                                                     hT[1][:, c % 2, hb, t * P:(t + 1) * P],
                                                     w2[par][0][:, hb * D:(hb + 1) * D],
                                                     w2[par][1][:, hb * D:(hb + 1) * D]):
                            mm = pe.matmul(ps[:, 4 + k, (t % 2) * D:(t % 2 + 1) * D], lhsT, rhs,
                                           start=(a == 0), stop=(a == 3 * HB - 1))
                            a += 1
                mm.then_inc(y_filled[k], 1)

            @block.tensor
            def _(pe):
                for c in range(CH):
                    pe.wait_ge(x_in[c], 16)
                    for k in range(KD):
                        n = c * KD + k
                        if n >= 8:
                            pe.wait_ge(xl_ready, n - 7)
                        for t in range(CT):
                            mm = pe.transpose(ps[:, n % 8, t * P:(t + 1) * P], y[:, c * CT + t, k * P:(k + 1) * P],
                                              ident[:, :])
                        mm.then_inc(turned, 1)
                pe.wait_ge(xl_ready, CH * KD)
                pe.wait_ge(consts, 5)
                for t in range(NT):
                    a = 0
                    for k in range(KD):
                        for lhsT, rhs in three_terms(xT[0][:, k, t * P:(t + 1) * P], xT[1][:, k, t * P:(t + 1) * P],
                                                     wrs[0][:, k, :], wrs[1][:, k, :]):
                            mm = pe.matmul(ps[:, 7, t * E:(t + 1) * E], lhsT, rhs, start=(a == 0),
                                           stop=(a == 3 * KD - 1))
                            a += 1
                mm.then_inc(logits_done, 1)
                pe.wait_ge(logits_read, 1)

                def run(n, par, first, last):
                    pe.wait_ge(w_ready, (n + 1) * 6)
                    for c in range(CH):
                        for hb in range(HB):
                            k = hb % 2
                            pe.wait_ge(h_drained[k], (n * CH + c) * (HB // 2) + hb // 2)
                            for m, w in enumerate((w3, w1)):
                                a = 0
                                for kk in range(KD):
                                    c0 = kk * FF + hb * P
                                    for lhsT, rhs in three_terms(w[par][0][:, c0:c0 + P], w[par][1][:, c0:c0 + P],
                                                                 xT[0][:, kk, c * 512:(c + 1) * 512],
                                                                 xT[1][:, kk, c * 512:(c + 1) * 512]):
                                        mm = pe.matmul(ps[:, 2 * k + m, :], lhsT, rhs, start=(a == 0),
                                                       stop=(a == 3 * KD - 1))
                                        a += 1
                            mm.then_inc(h_filled[k], 1)
                            if k == 1 and (c or not first):
                                before = (n, c - 1, par) if c else (n - 1, CH - 1, 1 - par)
                                second(pe, *before, hb // 2)
                    if last:
                        for half in range(2):
                            second(pe, n, CH - 1, par, half)

                over_experts(pe, run)

            @block.scalar
            def _(act):
                for n in range(CH * KD):
                    act.wait_ge(turned, n + 1)
                    act.activation(xT[0][:, n % KD, (n // KD) * 512:(n // KD + 1) * 512], ps[:, n % 8, :], ACT.Copy
                                   ).then_inc(xh_ready, 1)

                def run(n, par, first, last):
                    for c in range(CH):
                        u = n * CH + c

                        def hi(hb):
                            act.wait_ge(hid_ready, u * HB + hb + 1)
                            act.activation(hT[0][:, c % 2, hb, :], hid[:, hb % 2, :], ACT.Copy).then_inc(hh_ready, 1)

                        for hb in range(HB):
                            k = hb % 2
                            act.wait_ge(h_filled[k], u * (HB // 2) + hb // 2 + 1)
                            act.activation(gate[:, k, :], ps[:, 2 * k, :], ACT.Silu).then_inc(gated, 1)
                            if hb:
                                hi(hb - 1)
                        hi(HB - 1)
                        if first and c == 0:
                            act.wait_ge(route_in, 1)
                            act.activation(pick[:, :, :], pick[:, :, :], ACT.Exp).then_inc(route_exp, 1)

                over_experts(act, run)

            @block.vector
            def _(dve):
                for n in range(CH * KD):
                    dve.wait_ge(xh_ready, n + 1)
                    cols = slice((n // KD) * 512, (n // KD + 1) * 512)
                    dve.tensor_tensor(xT[1][:, n % KD, cols], ps[:, n % 8, :], xT[0][:, n % KD, cols].bitcast(F32),
                                      ALU.subtract).then_inc(xl_ready, 1)
                dve.wait_ge(logits_done, 1)
                dve.tensor_scalar(logit[:, :, :].rearrange("p t e -> p (t e)"), ps[:, 7, 0:NT * E], RSCALE, None,
                                  ALU.mult).then_inc(logits_read, 1)

                def routing():
                    made = [0]

                    def link(ins):
                        made[0] += 1
                        ins.then_inc(rchain, 1)
                        dve.wait_ge(rchain, made[0])

                    dve.wait_ge(consts, 5)
                    dve.wait_ge(logits_read, 1)
                    link(dve.tensor_tensor(biased[:, :, :], logit[:, :, :],
                                           rb_sb[:, :].unsqueeze(1).broadcast_to([P, NT, E]), ALU.add))
                    for t in range(NT):
                        ins = dve.max(top[:, t, :], biased[:, t, :])
                    link(ins)
                    for t in range(NT):
                        ins = dve.max_index(topi[:, t, :], top[:, t, :], biased[:, t, :])
                    link(ins)
                    link(dve.tensor_copy(topf[:, :, :], topi[:, :, 0:2].rearrange("p t a -> p a t")))
                    for a in range(2):
                        ins = dve.tensor_tensor(hot[:, a], lane[:, :].unsqueeze(1).broadcast_to([P, NT, E]),
                                                topf[:, a, :].unsqueeze(2).broadcast_to([P, NT, E]), ALU.is_equal)
                    link(ins)
                    for a in range(2):
                        link(dve.tensor_tensor(prod[:, :, :], hot[:, a], logit[:, :, :], ALU.mult))
                        link(dve.tensor_reduce(pick[:, a, :], prod[:, :, :], AX.X, ALU.add))
                    link(dve.tensor_tensor(pmax[:, :], pick[:, 0, :], pick[:, 1, :], ALU.max))
                    dve.tensor_tensor(pick[:, :, :], pick[:, :, :], pmax[:, :].unsqueeze(1).broadcast_to([P, 2, NT]),
                                      ALU.subtract).then_inc(route_in, 1)
                    dve.wait_ge(route_exp, 1)
                    link(dve.tensor_tensor(pmax[:, :], pick[:, 0, :], pick[:, 1, :], ALU.add))
                    link(dve.reciprocal(pmax[:, :], pmax[:, :]))
                    link(dve.tensor_tensor(pick[:, :, :], pick[:, :, :],
                                           pmax[:, :].unsqueeze(1).broadcast_to([P, 2, NT]), ALU.mult))
                    for a in range(2):
                        link(dve.tensor_tensor(hot[:, a], hot[:, a],
                                               pick[:, a, :].unsqueeze(2).broadcast_to([P, NT, E]), ALU.mult))
                    link(dve.tensor_tensor(share[:, :, 1:1 + E], hot[:, 0], hot[:, 1], ALU.add))

                def add_up(n, c, half):
                    k = 2 * (c % 2) + half
                    dve.wait_ge(y_filled[k], n * (CH // 2) + c // 2 + 1)
                    for a in range(2):
                        t = c * CT + 2 * half + a
                        src = ps[:, 4 + k, a * D:(a + 1) * D]
                        ins = dve.scalar_tensor_tensor(y[:, t, :], src, share[:, t, bass.ds(n, 1)], y[:, t, :],
                                                       ALU.mult, ALU.add)
                    ins.then_inc(y_drained[k], 1)

                def layer_norm(c):
                    t0 = c * CT
                    for half in range(2):
                        dve.wait_ge(y_drained[2 * (c % 2) + half], E * (CH // 2) + c // 2 + 1)
                    for t in range(CT):
                        ins = dve.bn_stats(st[:, t, :], y[:, t0 + t, :])
                    ins.then_inc(lchain, 1)
                    dve.wait_ge(lchain, 2 * c + 1)
                    for t in range(CT):
                        ins = dve.bn_aggr(mv[:, t, :], st[:, t, :])
                    ins.then_inc(lchain, 1)
                    dve.wait_ge(lchain, 2 * c + 2)
                    dve.tensor_scalar(ve[:, :], mv[:, :, 1], EPS, None, ALU.add).then_inc(var_ready, 1)
                    dve.wait_ge(rstd_ready, c + 1)
                    for t in range(CT):
                        dve.tensor_scalar(y[:, t0 + t, :], y[:, t0 + t, :], mv[:, t, 0:1], rs[:, t:t + 1],
                                          ALU.subtract, ALU.mult).then_inc(out_ready, 1)

                def run(n, par, first, last):
                    for c in range(CH):
                        u = n * CH + c
                        before = (n, c - 1) if c else None if first else (n - 1, CH - 1)

                        def lo(hb):
                            dve.wait_ge(hh_ready, u * HB + hb + 1)
                            dve.tensor_tensor(hT[1][:, c % 2, hb, :], hid[:, hb % 2, :],
                                              hT[0][:, c % 2, hb, :].bitcast(F32), ALU.subtract).then_inc(hl_ready, 1)

                        for hb in range(HB):
                            k = hb % 2
                            dve.wait_ge(gated, u * HB + hb + 1)
                            if hb >= 2 or c or not first:
                                dve.wait_ge(hl_ready, u * HB + hb - 1)
                            dve.tensor_tensor(hid[:, k, :], ps[:, 2 * k + 1, :], gate[:, k, :], ALU.mult
                                              ).then_inc(hid_ready, 1)
                            dve.wait_ge(hid_ready, u * HB + hb + 1)
                            dve.sem_inc(h_drained[k], 1)
                            if hb:
                                lo(hb - 1)
                            if hb == 2 and before:
                                add_up(*before, 0)
                        lo(HB - 1)
                        if before:
                            add_up(*before, 1)
                        if last and c:
                            layer_norm(c - 1)
                        if first and c == 0:
                            routing()
                    if last:
                        for half in range(2):
                            add_up(n, CH - 1, half)
                        layer_norm(CH - 1)

                over_experts(dve, run)


def build(nc, x, ctx_1024, aWkv, abkv, aWq, abq, aWp, abp, cos, sin, lg, lb, cg, cb, xWq, xWkv, xWo, xbo,
          Wr, rb, W1, W2, W3, Ws1, Ws2, Ws3, out, upto="abc", x1_out=None, x2_out=None):
    x1_dram = x1_out if x1_out is not None else nc.dram_tensor("x1", (S, B, D), F32, kind="Internal").ap()
    with ExitStack() as ctx:
        ident = ctx.enter_context(nc.sbuf_tensor("ident", [P, P], F32))
        identr = ctx.enter_context(nc.sbuf_tensor("identr", [P, P], F32R))
        identb = ctx.enter_context(nc.sbuf_tensor("identb", [P, P], BF16))
        made = ctx.enter_context(nc.semaphore("ident_made"))
        with nc.Block() as block:

            @block.gpsimd
            def _(pool):
                pool.memset(ident[:, :], 0.0).then_inc(made, 1)
                pool.wait_ge(made, 1)
                pool.affine_select(out=ident[:, :], in_=ident[:, :], compare_op=ALU.not_equal, fill=1.0, base=0,
                                   pattern=[[-1, P]], channel_multiplier=1).then_inc(made, 1)
                pool.wait_ge(made, 2)
                pool.tensor_copy(identr[:, :], ident[:, :]).then_inc(made, 1)
                pool.tensor_copy(identb[:, :], ident[:, :]).then_inc(made, 1)

        x2_dram = x2_out if x2_out is not None else nc.dram_tensor("x2", (S, B, D), F32, kind="Internal").ap()
        if "a" in upto:
            self_attention(nc, x, aWkv, abkv, aWq, abq, aWp, abp, x1_dram, ident, identb)
        if "b" in upto:
            cross_attention(nc, x1_dram, ctx_1024, cos, sin, lg, lb, cg, cb, xWq, xWkv, xWo, xbo, x2_dram, ident, identr)
        if "c" in upto:
            experts(nc, x2_dram, Wr, rb, W1, W2, W3, Ws1, Ws2, Ws3, out, ident)


_INS = ['x', 'ctx_1024', 'L0_attn_Wkv', 'L0_attn_bkv', 'L0_attn_Wq', 'L0_attn_bq', 'L0_attn_Wp', 'L0_attn_bp',
        'L0_xattn_cos', 'L0_xattn_sin', 'L0_xattn_ln_lat_g', 'L0_xattn_ln_lat_b', 'L0_xattn_ln_ctx_g',
        'L0_xattn_ln_ctx_b', 'L0_xattn_Wq', 'L0_xattn_Wkv', 'L0_xattn_Wo', 'L0_xattn_bo', 'L0_ffn_Wr', 'L0_ffn_rb',
        'L0_ffn_W1', 'L0_ffn_W2', 'L0_ffn_W3', 'L0_ffn_Ws1', 'L0_ffn_Ws2', 'L0_ffn_Ws3']
_OUTS = [((S, B, D), 'float32')]


def kernel(**inputs):
    import numpy as _np
    import concourse.bacc as _bacc
    from concourse import mybir as _mybir
    from concourse.bass_utils import run_bass_kernel_spmd as _run

    nc = _bacc.Bacc("TRN2", target_bir_lowering=False, num_devices=1, dynamic_dma_scratch_size=1024)
    arrays, args = {}, []
    for name in _INS:
        a = _np.ascontiguousarray(inputs[name])
        arrays[f"in_{name}_dram"] = a
        args.append(nc.dram_tensor(f"in_{name}_dram", a.shape, _mybir.dt.from_np(a.dtype), kind="ExternalInput").ap())
    for i, (shape, dtype) in enumerate(_OUTS):
        dt = _mybir.dt.from_np(_np.dtype(dtype))
        args.append(nc.dram_tensor(f"out_{i}_dram", shape, dt, kind="ExternalOutput").ap())
    build(nc, *args)
    r = _run(nc, [arrays], core_ids=[0])
    return r.results[0]["out_0_dram"]
```

```python
import math
from contextlib import ExitStack

import concourse.bass as bass
from concourse import mybir

P = 128
F32 = mybir.dt.float32
F32R = mybir.dt.float32r
BF16 = mybir.dt.bfloat16
U32 = mybir.dt.uint32
ALU = mybir.AluOpType
ACT = mybir.ActivationFunctionType
AX = mybir.AxisListType
EPS = 1e-5

S, B, D = 8, 512, 256
H, HD = 16, 64
INNER = H * HD
CTX = 1024
SCALE = float(HD) ** -0.5
CLIP = 11.0
E, FF = 8, 512
KD = D // P
PAIRS = H // 2


class Slots:

    def __init__(self, order, weight=None, silent=()):
        self.at, self.uses, self.fills, self.fill_at = {}, {}, {}, {}
        for key, slot in order:
            self.at[key] = (slot, self.uses.get(slot, 0))
            self.uses[slot] = self.uses.get(slot, 0) + 1
            if key[0] not in silent:
                self.fill_at[key] = self.fills.get(slot, 0)
                self.fills[slot] = self.fills.get(slot, 0) + 1
        self.weight = weight or {}

    def slot(self, key):
        return self.at[key][0]

    def filled(self, key, i):
        return i * self.fills[self.slot(key)] + (self.fill_at[key] + 1)

    def free(self, key, i):
        slot, k = self.at[key]
        w = self.weight.get(slot, 1)
        return i * (self.uses[slot] * w) + k * w

    def drained(self, key, i):
        slot, k = self.at[key]
        w = self.weight.get(slot, 1)
        return i * (self.uses[slot] * w) + (k + 1) * w


def weight_views(Wq, Wkv, Wo):
    kv = Wkv.rearrange("(k p) n -> p k n", p=P)
    return [kv[:, :, 0:INNER], kv[:, :, INNER:2 * INNER]] + [w.rearrange("(k p) n -> p k n", p=P) for w in (Wq, Wo)]


def load_weights(sp, views, raw, loaded):
    for n, view in enumerate(views):
        sp.dma_start(raw[:, n, :].rearrange("p (a n) -> p a n", a=view.shape[1]), view).then_inc(loaded[n], 16)


class Weights:

    def __init__(self, nc, ctx, name, raw, loaded, parts):
        self.raw, self.loaded, self.parts = raw, loaded, parts
        self.hi_done = ctx.enter_context(nc.semaphore(f"{name}_hi_done"))
        self.lo_done = ctx.enter_context(nc.semaphore(f"{name}_lo_done"))

    def split_hi(self, act, n):
        act.wait_ge(self.loaded[n], 16)
        act.activation(self.parts[n][0][:, :], self.raw[:, n, :], ACT.Copy).then_inc(self.hi_done, 1)

    def split_lo(self, dve, n):
        hi, lo = self.parts[n]
        dve.wait_ge(self.hi_done, n + 1)
        dve.tensor_tensor(lo[:, :], self.raw[:, n, :], hi[:, :].bitcast(F32), ALU.subtract).then_inc(self.lo_done, 1)


def three_terms(w_hi, w_lo, x_hi, x_lo):
    return ((w_hi, x_hi), (w_hi, x_lo), (w_lo, x_hi))


def self_attention(nc, x, Wkv, bkv, Wq, bq, Wp, bp, x1_dram, ident, identb, raw, loaded, load_next):
    CH, TT, BI = 8, 4, 16
    BIG = 1e30
    with ExitStack() as ctx:
        def sb(name, shape, dt=F32):
            return ctx.enter_context(nc.sbuf_tensor(name, shape, dt))

        def sem(name):
            return ctx.enter_context(nc.semaphore(name))

        wq = [sb(f"a_wq_{n}", [P, KD * INNER], F32R) for n in "hl"]
        wk = [sb(f"a_wk_{n}", [P, KD * INNER], F32R) for n in "hl"]
        wv = [sb(f"a_wv_{n}", [P, KD * INNER], F32R) for n in "hl"]
        wp = [sb(f"a_wp_{n}", [P, PAIRS * D], F32R) for n in "hl"]
        weights = Weights(nc, ctx, "a_w", raw, loaded, (wk, wv, wq, wp))

        mneg = sb("a_mneg", [P, P], BF16)
        ident4 = sb("a_ident4", [P, 4, P], BF16)
        same16 = sb("a_same16", [P, BI])
        bq_sb = sb("a_bq", [P, PAIRS])
        bk_sb = sb("a_bk", [P, PAIRS])
        bv_sb = sb("a_bv", [P, INNER])
        bp_sb = sb("a_bp", [P, D])
        mhalf = sb("a_mhalf", [P, TT])
        xt = sb("a_xt", [P, 2, TT, D])
        xT = [sb(f"a_xT_{n}", [P, KD, TT * P], F32R) for n in "hl"]
        QT = sb("a_QT", [P, PAIRS, TT * P])
        KB = sb("a_KB", [P, PAIRS, TT, 2 * P])
        V = sb("a_V", [P, TT, INNER])
        Sc = sb("a_Sc", [P, 2, H, S])
        mx = sb("a_mx", [P, H])
        den = sb("a_den", [P, H])
        Pe = sb("a_Pe", [P, H, P])
        PT = sb("a_PT", [P, H, P])
        OT = [sb(f"a_OT_{n}", [P, PAIRS, P], F32R) for n in "hl"]
        y = sb("a_y", [P, 2, D])
        st = sb("a_st", [P, 6])
        mv = sb("a_mv", [P, 2])
        ve = sb("a_ve", [P, 1])
        rs = sb("a_rs", [P, 1])
        x1t = sb("a_x1t", [P, 2, TT, D])
        ps = ctx.enter_context(nc.psum_tensor("a_ps", [P, 8, 512], F32))

        EARLY = 5
        S_PARTS = 4
        ring = [("x", k) for k in range(KD)] + [("proj", n) for n in range(16)]
        ring += [("s", 0, q) for q in range(S_PARTS)] + [("proj", n) for n in range(16, 20)]
        ring += [("s", 1, q) for q in range(S_PARTS)] + [("proj", n) for n in range(20, 24)]
        ring += [("s", t, q) for t in range(2, TT) for q in range(S_PARTS)]
        order = [(key, n % 4) for n, key in enumerate(ring)]
        steps = [key for t in range(TT)
                 for key in [("pt", t, q) for q in range(4)] + [("o", t, k) for k in range(2)] + [("y", t)]]
        order += [(key, 4 + n % 4) for n, key in enumerate(steps)]
        slots = Slots(order)
        filled = [sem(f"a_filled{i}") for i in range(8)]
        drained = [sem(f"a_drained{i}") for i in range(8)]
        consts = sem("a_consts")
        consts_in = sem("a_consts_in")
        x_in = [sem(f"a_x_in{k}") for k in range(2)]
        xh = sem("a_xh")
        xl = sem("a_xl")
        compact = sem("a_compact")
        exped = sem("a_exped")
        probs = sem("a_probs")
        spread = sem("a_spread")
        oth = sem("a_oth")
        otl = sem("a_otl")
        biased = sem("a_biased")
        var_ready = sem("a_var_ready")
        rstd_ready = sem("a_rstd_ready")
        x1_ready = sem("a_x1_ready")
        stats_taken = sem("a_stats_taken")
        stored = [sem(f"a_stored{k}") for k in range(2)]
        dchain = sem("a_dchain")

        def wait_filled(eng, key, c):
            eng.wait_ge(filled[slots.slot(key)], slots.filled(key, c))

        def wait_free(eng, key, c):
            eng.wait_ge(drained[slots.slot(key)], slots.free(key, c))

        def bank(key):
            return ps[:, slots.slot(key), :]

        with nc.Block() as block:

            @block.sync
            def _(sp):
                def load(half, c):
                    for s in range(S):
                        src = x[s].rearrange("(c t b) d -> c b t d", t=TT, b=BI)[bass.ds(c, 1)]
                        sp.dma_start(xt[BI * s:BI * s + BI, half], src.rearrange("c b t d -> (c b) t d")
                                     ).then_inc(x_in[half], 16)

                def store(half, c):
                    for s in range(S):
                        dst = x1_dram[s].rearrange("(c t b) d -> c b t d", t=TT, b=BI)[bass.ds(c, 1)]
                        sp.dma_start(dst.rearrange("c b t d -> (c b) t d"), x1t[BI * s:BI * s + BI, half]
                                     ).then_inc(stored[half], 16)

                views = weight_views(Wq, Wkv, Wp)
                load_weights(sp, views[:1], raw, loaded)
                load(0, 0)
                sp.dma_start(bq_sb[:, :], bq.rearrange("(c p) -> p c", p=P),
                             allow_slow_non_contiguous=True).then_inc(consts_in, 16)
                sp.dma_start(bk_sb[:, :], bkv[0:INNER].rearrange("(c p) -> p c", p=P),
                             allow_slow_non_contiguous=True).then_inc(consts_in, 16)
                sp.dma_start(bv_sb[:, :], bkv[INNER:2 * INNER].partition_broadcast(P)).then_inc(consts_in, 16)
                sp.dma_start(bp_sb[:, :], bp.partition_broadcast(P)).then_inc(consts_in, 16)

                load_weights(sp, views[1:], raw[:, 1:4], loaded[1:])
                sp.wait_ge(weights.lo_done, 4)
                load_next(sp)
                with sp.Fori(0, CH // 2) as i:
                    sp.wait_ge(x1_ready, (2 * i) * TT)
                    load(1, 2 * i + 1)
                    sp.wait_ge(x1_ready, (2 * i + 1) * TT)
                    store(0, 2 * i)
                    load(0, (2 * i + 2) % CH)
                    sp.wait_ge(x1_ready, (2 * i + 2) * TT)
                    store(1, 2 * i + 1)
                for half in range(2):
                    sp.wait_ge(stored[half], 16 * S * (CH // 2))
                sp.wait_ge(x_in[0], 16 * S * (CH // 2 + 1))

            @block.gpsimd
            def _(pool):
                pool.memset(KB[:, :, :, :], 0.0).then_inc(consts, 1)
                pool.memset(mneg[:, :], -BIG).then_inc(consts, 1)
                pool.memset(same16[:, :], 0.0).then_inc(consts, 1)
                pool.memset(mhalf[:, :], -0.5).then_inc(consts, 1)
                pool.wait_ge(consts, 4)
                k = 4
                for a in range(-(S - 1), S):
                    pool.affine_select(out=mneg[:, :], in_=mneg[:, :], compare_op=ALU.not_equal, fill=0.0,
                                       base=-BI * a, pattern=[[-1, P]], channel_multiplier=1).then_inc(consts, 1)
                    k += 1
                    pool.wait_ge(consts, k)
                for a in range(S):
                    pool.affine_select(out=same16[:, :], in_=same16[:, :], compare_op=ALU.not_equal, fill=1.0,
                                       base=-BI * a, pattern=[[-1, BI]], channel_multiplier=1).then_inc(consts, 1)
                    k += 1
                    pool.wait_ge(consts, k)
                for a in range(4):
                    pool.tensor_copy(ident4[:, a, :], identb[:, :]).then_inc(consts, 1)
                pool.wait_ge(consts_in, 64)
                with pool.Fori(0, CH // 2) as i:
                    for half in range(2):
                        c = 2 * i + half
                        wait_filled(pool, ("x", 1), c)
                        for t in range(TT):
                            pool.tensor_tensor(xt[:, half, t], xt[:, half, t], bp_sb[:, :], ALU.add
                                               ).then_inc(biased, 1)
                        for t in range(TT):
                            pool.wait_ge(probs, c * TT + t + 1)
                            if t:
                                wait_filled(pool, ("pt", t - 1, 3), c)
                            pool.tensor_tensor(
                                Pe[:, :, :].rearrange("p h (t b) -> p (h t) b", b=BI),
                                Sc[:, t % 2].rearrange("p h t -> p (h t)").unsqueeze(2).broadcast_to([P, H * S, BI]),
                                same16[:, :].unsqueeze(1).broadcast_to([P, H * S, BI]), ALU.mult
                            ).then_inc(spread, 1)
                            if t:
                                pool.wait_ge(var_ready, c * TT + t)
                                pool.tensor_tensor(rs[:, :], ve[:, :], mhalf[:, 0:1], ALU.pow).then_inc(rstd_ready, 1)
                        pool.wait_ge(var_ready, c * TT + TT)
                        pool.tensor_tensor(rs[:, :], ve[:, :], mhalf[:, 0:1], ALU.pow).then_inc(rstd_ready, 1)

            def fill(key, mm):
                mm.then_inc(filled[slots.slot(key)], 1)

            def turn_x(pe, c, half, loads):
                pe.wait_ge(x_in[half], loads * (16 * S))
                for k in range(KD):
                    key = ("x", k)
                    wait_free(pe, key, c)
                    for t in range(TT):
                        mm = pe.transpose(bank(key)[:, t * P:(t + 1) * P], xt[:, half, t, k * P:(k + 1) * P], ident[:, :])
                    fill(key, mm)

            def project(pe, c, n):
                key = ("proj", n)
                wait_free(pe, key, c)
                if n == 0:
                    pe.wait_ge(xl, (c + 1) * KD)
                if n in (0, 8):
                    pe.wait_ge(weights.lo_done, 3 if n else 1)
                if n < 16:
                    w = wk if n < 8 else wq
                    col = (n % 8) * P
                    terms = [t for k in range(KD) for t in three_terms(
                        w[0][:, k * INNER + col:k * INNER + col + P], w[1][:, k * INNER + col:k * INNER + col + P],
                        xT[0][:, k, :], xT[1][:, k, :])]
                else:
                    t, h2 = (n - 16) // 2, (n - 16) % 2
                    cols = [slice(k * INNER + h2 * 512, k * INNER + h2 * 512 + 512) for k in range(KD)]
                    terms = [u for k in range(KD) for u in three_terms(
                        xT[0][:, k, t * P:(t + 1) * P], xT[1][:, k, t * P:(t + 1) * P],
                        wv[0][:, cols[k]], wv[1][:, cols[k]])]
                for a, (lhsT, rhs) in enumerate(terms):
                    mm = pe.matmul(bank(key), lhsT, rhs, start=(a == 0), stop=(a == len(terms) - 1))
                fill(key, mm)

            def scores(pe, c, t, parts):
                for q in parts:
                    key = ("s", t, q)
                    wait_free(pe, key, c)
                    pe.matmul(bank(key), mneg[:, :], ident4[:, :, :].rearrange("p a b -> p (a b)"),
                              start=True, stop=True)
                    for a in range(2):
                        pair = 2 * q + a
                        mm = pe.matmul(bank(key)[:, a * 256:(a + 1) * 256], QT[:, pair, t * P:(t + 1) * P],
                                       KB[:, pair, t, :], start=False, stop=True, skip_group_check=True)
                    fill(key, mm)

            def chunk(pe, i, c, half):
                for n in range(EARLY, 16):
                    project(pe, c, n)
                for t in range(2):
                    scores(pe, c, t, range(S_PARTS))
                    for n in range(16 + 4 * t, 20 + 4 * t):
                        project(pe, c, n)
                after = c + 1
                for t in range(TT):
                    pe.wait_ge(spread, c * TT + t + 1)
                    for q in range(4):
                        key = ("pt", t, q)
                        wait_free(pe, key, c)
                        for a in range(4):
                            mm = pe.transpose(bank(key)[:, a * P:(a + 1) * P], Pe[:, 4 * q + a, :], ident[:, :])
                        fill(key, mm)
                    if t + 2 < TT:
                        scores(pe, c, t + 2, (0, 1))
                    elif t == 2:
                        turn_x(pe, after, 1 - half, i + 1 + half)
                    else:
                        project(pe, after, 2)
                    for k in range(2):
                        key = ("o", t, k)
                        wait_free(pe, key, c)
                        for q in (2 * k, 2 * k + 1):
                            pe.wait_ge(drained[slots.slot(("pt", t, q))], slots.drained(("pt", t, q), c))
                        for pair in range(4 * k, 4 * k + 4):
                            for hh in range(2):
                                h = 2 * pair + hh
                                mm = pe.matmul(bank(key)[hh * HD:(hh + 1) * HD, (pair % 4) * P:(pair % 4 + 1) * P],
                                               V[:, t, h * HD:(h + 1) * HD], PT[:, h, :], start=True, stop=True)
                        fill(key, mm)
                    if t + 2 < TT:
                        scores(pe, c, t + 2, (2, 3))
                    elif t == 2:
                        project(pe, after, 0)
                        project(pe, after, 1)
                    else:
                        for n in range(3, EARLY):
                            project(pe, after, n)
                    key = ("y", t)
                    wait_free(pe, key, c)
                    pe.wait_ge(otl, (c * TT + t) * 2 + 2)
                    if t == 0:
                        pe.wait_ge(weights.lo_done, 4)
                    a = 0
                    for pair in range(PAIRS):
                        for lhsT, rhs in three_terms(OT[0][:, pair, :], OT[1][:, pair, :],
                                                     wp[0][:, pair * D:(pair + 1) * D], wp[1][:, pair * D:(pair + 1) * D]):
                            mm = pe.matmul(bank(key)[:, 0:D], lhsT, rhs, start=(a == 0), stop=(a == 3 * PAIRS - 1))
                            a += 1
                    fill(key, mm)

            @block.tensor
            def _(pe):
                turn_x(pe, 0, 0, 1)
                for n in range(EARLY):
                    project(pe, 0, n)
                pe.wait_ge(consts, 4 + 15 + 8 + 4)
                with pe.Fori(0, CH // 2) as i:
                    for half in range(2):
                        chunk(pe, i, 2 * i + half, half)

            @block.scalar
            def _(act):
                weights.split_hi(act, 0)

                def x_hi(c):
                    for k in range(KD):
                        wait_filled(act, ("x", k), c)
                        act.activation(xT[0][:, k, :], bank(("x", k)), ACT.Copy).then_inc(xh, 1)

                x_hi(0)
                for n in range(1, 4):
                    weights.split_hi(act, n)
                act.wait_ge(consts_in, 64)
                with act.Fori(0, CH) as c:
                    def exps(t):
                        act.wait_ge(compact, c * TT + t + 1)
                        act.activation(Sc[:, t % 2], Sc[:, t % 2], ACT.Exp, scale=SCALE).then_inc(exped, 1)

                    for n in range(8, 16):
                        wait_filled(act, ("proj", n), c)
                        act.activation(QT[:, n - 8, :], bank(("proj", n)), ACT.Identity, bias=bq_sb[:, n - 8:n - 7]
                                       ).then_inc(drained[slots.slot(("proj", n))], 1)
                    exps(0)
                    exps(1)
                    for t in range(TT):
                        for q in range(4):
                            key = ("pt", t, q)
                            wait_filled(act, key, c)
                            if q == 0 and t:
                                wait_filled(act, ("o", t - 1, 1), c)
                            act.activation(PT[:, 4 * q:4 * q + 4, :].rearrange("p h n -> p (h n)"), bank(key), ACT.Copy
                                           ).then_inc(drained[slots.slot(key)], 1)
                        if t == 2:
                            x_hi(c + 1)
                        for k in range(2):
                            key = ("o", t, k)
                            wait_filled(act, key, c)
                            if k == 0 and t:
                                wait_filled(act, ("y", t - 1), c)
                            act.activation(OT[0][:, 4 * k:4 * k + 4, :].rearrange("p h n -> p (h n)"), bank(key),
                                           ACT.Copy).then_inc(oth, 1)
                        if t + 2 < TT:
                            exps(t + 2)

            @block.vector
            def _(dve):
                LINKS = 5 * TT
                def x_lo(c):
                    for k in range(KD):
                        dve.wait_ge(xh, c * KD + k + 1)
                        dve.tensor_tensor(xT[1][:, k, :], bank(("x", k)), xT[0][:, k, :].bitcast(F32), ALU.subtract
                                          ).then_inc(xl, 1)
                        dve.wait_ge(xl, c * KD + k + 1)
                        dve.sem_inc(drained[slots.slot(("x", k))], 1)

                def keys(c, n):
                    wait_filled(dve, ("proj", n), c)
                    for hh in range(2):
                        ins = dve.tensor_scalar(
                            KB[hh * HD:(hh + 1) * HD, n, :, hh * P:(hh + 1) * P],
                            bank(("proj", n))[hh * HD:(hh + 1) * HD].rearrange("p (t n) -> p t n", t=TT),
                            bk_sb[hh * HD:(hh + 1) * HD, n:n + 1], None, ALU.add)
                    ins.then_inc(drained[slots.slot(("proj", n))], 1)

                weights.split_lo(dve, 0)
                x_lo(0)
                dve.wait_ge(consts, 1)
                dve.wait_ge(consts_in, 64)
                weights.split_lo(dve, 1)
                keys(0, 0)
                keys(0, 1)
                weights.split_lo(dve, 2)
                keys(0, 2)
                keys(0, 3)
                weights.split_lo(dve, 3)
                for n in range(4, EARLY):
                    keys(0, n)
                with dve.Fori(0, CH // 2) as i:
                    for half in range(2):
                        c = 2 * i + half
                        made = [0]

                        def link(ins):
                            made[0] += 1
                            ins.then_inc(dchain, 1)
                            dve.wait_ge(dchain, c * LINKS + made[0])

                        def values(ns):
                            for n in ns:
                                wait_filled(dve, ("proj", n), c)
                                t, h2 = (n - 16) // 2, (n - 16) % 2
                                dve.tensor_tensor(V[:, t, h2 * 512:(h2 + 1) * 512], bank(("proj", n)),
                                                  bv_sb[:, h2 * 512:(h2 + 1) * 512], ALU.add
                                                  ).then_inc(drained[slots.slot(("proj", n))], 1)

                        def compact_scores(t, parts=range(4)):
                            for q in parts:
                                key = ("s", t, q)
                                wait_filled(dve, key, c)
                                ins = dve.tensor_reduce(Sc[:, t % 2, 4 * q:4 * q + 4, :].rearrange("p h t -> p (h t)"),
                                                        bank(key).rearrange("p (a b) -> p a b", b=BI), AX.X, ALU.max)
                                if q < 3:
                                    ins.then_inc(drained[slots.slot(key)], 1)
                            if parts[-1] < 3:
                                return
                            ins.then_inc(drained[slots.slot(key)], 1)
                            dve.wait_ge(drained[slots.slot(key)], slots.drained(key, c))
                            link(dve.tensor_reduce(mx[:, :], Sc[:, t % 2], AX.X, ALU.max))
                            dve.tensor_tensor(Sc[:, t % 2], Sc[:, t % 2], mx[:, :].unsqueeze(2).broadcast_to([P, H, S]),
                                              ALU.subtract).then_inc(compact, 1)

                        def normalise(t):
                            dve.wait_ge(exped, c * TT + t + 1)
                            link(dve.tensor_reduce(den[:, :], Sc[:, t % 2], AX.X, ALU.add))
                            link(dve.reciprocal(den[:, :], den[:, :]))
                            dve.tensor_tensor(Sc[:, t % 2], Sc[:, t % 2], den[:, :].unsqueeze(2).broadcast_to([P, H, S]),
                                              ALU.mult).then_inc(probs, 1)

                        def lo_of_o(t):
                            for k in range(2):
                                dve.wait_ge(oth, (c * TT + t) * 2 + k + 1)
                                dve.tensor_tensor(OT[1][:, 4 * k:4 * k + 4, :].rearrange("p h n -> p (h n)"),
                                                  bank(("o", t, k)),
                                                  OT[0][:, 4 * k:4 * k + 4, :].rearrange("p h n -> p (h n)").bitcast(F32),
                                                  ALU.subtract).then_inc(otl, 1)
                                dve.wait_ge(otl, (c * TT + t) * 2 + k + 1)
                                dve.sem_inc(drained[slots.slot(("o", t, k))], 1)

                        def residual(t):
                            wait_filled(dve, ("y", t), c)
                            dve.wait_ge(biased, c * TT + t + 1)
                            ins = dve.tensor_tensor(y[:, t % 2], bank(("y", t))[:, 0:D], xt[:, half, t], ALU.add)
                            slot = slots.slot(("y", t))
                            ins.then_inc(drained[slot], 1)
                            dve.wait_ge(drained[slot], slots.drained(("y", t), c))
                            link(dve.bn_stats(st[:, :], y[:, t % 2]))
                            dve.sem_inc(stats_taken, 1)
                            link(dve.bn_aggr(mv[:, :], st[:, :]))
                            dve.tensor_scalar(ve[:, :], mv[:, 1:2], EPS, None, ALU.add).then_inc(var_ready, 1)

                        def norm(t):
                            dve.wait_ge(rstd_ready, c * TT + t + 1)
                            if t == 0:
                                dve.wait_ge(stored[half], i * (16 * S))
                            dve.tensor_scalar(x1t[:, half, t], y[:, t % 2], mv[:, 0:1], rs[:, :], ALU.subtract,
                                              ALU.mult).then_inc(x1_ready, 1)

                        for n in range(EARLY, 8):
                            keys(c, n)
                        for t in range(2):
                            compact_scores(t)
                            values([16 + 4 * t])
                            normalise(t)
                            values(range(17 + 4 * t, 20 + 4 * t))
                        for t in range(TT):
                            if t:
                                residual(t - 1)
                            if t + 2 < TT:
                                compact_scores(t + 2, (0, 1))
                            elif t == 2:
                                x_lo(c + 1)
                            else:
                                keys(c + 1, 2)
                            lo_of_o(t)
                            if t:
                                norm(t - 1)
                            if t + 2 < TT:
                                compact_scores(t + 2, (2, 3))
                                normalise(t + 2)
                            else:
                                for n in ((0, 1) if t == 2 else range(3, EARLY)):
                                    keys(c + 1, n)
                        residual(TT - 1)
                        norm(TT - 1)
                        assert made[0] == LINKS


def cross_attention(nc, x1_dram, context, cos, sin, lg, lb, cg, cb, bo, x2_dram, ident, identr, raw, loaded):
    NT, CT = B // P, CTX // P
    HG, PG = H // 2, PAIRS // 2
    LO, HI = math.exp(-CLIP), math.exp(CLIP)
    with ExitStack() as ctx:
        def sb(name, shape, dt=F32):
            return ctx.enter_context(nc.sbuf_tensor(name, shape, dt))

        def sem(name):
            return ctx.enter_context(nc.semaphore(name))

        wq = [sb(f"b_wq_{n}", [P, KD * INNER], F32R) for n in "hl"]
        wk = [sb(f"b_wk_{n}", [P, KD * INNER], F32R) for n in "hl"]
        wv = [sb(f"b_wv_{n}", [P, KD * INNER], F32R) for n in "hl"]
        wo = [sb(f"b_wo_{n}", [P, PAIRS * D], F32R) for n in "hl"]
        weights = Weights(nc, ctx, "b_w", raw, loaded, (wk, wv, wq, wo))

        cos_sb = sb("b_cos", [P, CT, HD // 2])
        sin_sb = sb("b_sin", [P, CT, 2, HD // 2])
        ones = sb("b_ones", [P, HD])
        gam = sb("b_gam", [P, 2, KD])
        bet = sb("b_bet", [P, 2, KD])
        bo_sb = sb("b_bo", [P, D])
        mhalf = sb("b_mhalf", [P, CT + NT])
        rows = sb("b_rows", [P, CT + NT, D])
        x1 = sb("b_x1", [P, NT, D])
        cT = [sb(f"b_cT_{n}", [P, KD, CTX], F32R) for n in "hl"]
        lT = [sb(f"b_lT_{n}", [P, KD, B], F32R) for n in "hl"]
        KT = sb("b_KT", [P, HG, CTX], F32R)
        V = raw[:, 2:4, :].rearrange("p a n -> p (a n)").rearrange("p (t n) -> p t n", t=CT)
        QQ = sb("b_QQ", [P, 2, 2, 2, B], F32R)
        OT = [sb(f"b_OT_{n}", [P, PG, B], F32R) for n in "hl"]
        probs = raw[:, 0:2, :].rearrange("p a n -> p (a n)").rearrange("p (s n) -> p s n", s=4)

        def at_step(j, hh):
            return 2 * ((j + 1) % 2) + hh

        krot = probs[:, 0, :].rearrange("p (a n) -> p a n", a=2)
        kswap = probs[:, 1, 0:HG * HD]
        knat = QQ[:, 1].rearrange("p a b n -> p (a b n)").rearrange("p (t n) -> p t n", t=2)
        acc = sb("b_acc", [P, 2, B])
        accf = sb("b_accf", [P, 2, B])
        r = sb("b_r", [P, B])
        o = sb("b_o", [P, B])
        zc = sb("b_zc", [P, 512])
        zl = [probs[:, 3, 0:B], probs[:, 3, B:2 * B]]
        st = sb("b_st", [P, CT + NT, 6])
        mv = sb("b_mv", [P, CT + NT, 2])
        ve = sb("b_ve", [P, CT + NT])
        rs = sb("b_rs", [P, CT + NT])
        ps = ctx.enter_context(nc.psum_tensor("b_ps", [P, 8, 512], F32))

        Q0_AT = 5

        def cx_step(p):
            return 3 if p + 1 < PG else 1

        banks = {"A": 0, "B": 2, 4: 4, 5: 5, 6: 6, 7: 7}
        order = []
        for g in range(2):
            for t in range(CT):
                order.append((("kv", g, t), "BA"[t % 2] if t <= Q0_AT else "AB"[t % 2]))
                if g == 0 and t < KD:
                    order.append((("lx", t), 6 + t))
                if t == Q0_AT:
                    order.append((("q", g, 0), "B"))
                if t >= 2:
                    order += [(("kt", g, t - 2, a), 4 + 2 * (t % 2) + a) for a in range(2)]
            order += [(("s", g, 0, 0, hh), "AB"[hh]) for hh in range(2)]
            order += [(("kt", g, CT - 2, a), 4 + a) for a in range(2)]
            for p in range(PG):
                for j in range(4):
                    if (p, j) != (PG - 1, 3):
                        pn, jn = (p, j + 1) if j < 3 else (p + 1, 0)
                        order += [(("s", g, pn, jn, hh), "AB"[hh]) for hh in range(2)]
                    if (p, j) == (0, 0):
                        order += [(("kt", g, CT - 1, a), 6 + a) for a in range(2)]
                    if j == 0:
                        if p:
                            order.append((("sum", g, p - 1), 6))
                        if p + 1 < PG:
                            order.append((("q", g, p + 1), 7 if p else 5))
                        order.append((("o", g, p), 4 + p % 2))
                    if g == 1 and j == cx_step(p):
                        order.append((("cx", p), 7))
            order += [(("sum", g, PG - 1), 6), (("y", g, 0), 7), (("y", g, 1), 4)]
        slots = Slots(order, {"A": 2, "B": 2}, ("o", "cx"))
        filled = {s: sem(f"b_filled{s}") for s in banks}
        drained = {s: sem(f"b_drained{s}") for s in banks}
        consts = sem("b_consts")
        consts_in = sem("b_consts_in")
        ctx_in = sem("b_ctx_in")
        lat_in = sem("b_lat_in")
        x1_in = sem("b_x1_in")
        cx_turned = sem("b_cx_turned")
        q_ready = sem("b_q_ready")
        q_spread = sem("b_q_spread")
        var_ready = sem("b_var_ready")
        rstd_ready = sem("b_rstd_ready")
        normed = sem("b_normed")
        biased = sem("b_biased")
        z_ready = sem("b_z_ready")
        zh_ready = sem("b_zh_ready")
        zl_ready = sem("b_zl_ready")
        rotated = sem("b_rotated")
        kh_ready = sem("b_kh_ready")
        knat_ready = sem("b_knat_ready")
        qh_ready = sem("b_qh_ready")
        clipped = sem("b_clipped")
        pv_done = sem("b_pv_done")
        acc_ready = sem("b_acc_ready")
        accf_ready = sem("b_accf_ready")
        pchain = sem("b_pchain")
        dchain = sem("b_dchain")
        oh_ready = sem("b_oh_ready")
        ot_ready = sem("b_ot_ready")
        out_ready = sem("b_out_ready")
        stats_taken = sem("b_stats_taken")
        stored = sem("b_stored")

        def wait_filled(eng, key, b):
            eng.wait_ge(filled[slots.slot(key)], slots.filled(key, b))

        def wait_free(eng, key, b):
            eng.wait_ge(drained[slots.slot(key)], slots.free(key, b))

        def wait_drained(eng, key, b):
            eng.wait_ge(drained[slots.slot(key)], slots.drained(key, b))

        def bank(key, a=0):
            return ps[:, banks[slots.slot(key)] + a, :]

        def both(key):
            n = banks[slots.slot(key)]
            return ps[:, n:n + 2, :].rearrange("p a n -> p (a n)")

        def fill(key, ins):
            ins.then_inc(filled[slots.slot(key)], 1)

        def drain(key, ins, n=1):
            ins.then_inc(drained[slots.slot(key)], n)

        def step(g, p, j):
            return (g * PG + p) * 4 + j

        def block_rows(c):
            return c % KD, 4 * (c // KD)

        ZB = 2 * KD
        ZN = ZB + KD
        ROWS = CT + NT
        NCONST = 4
        with nc.Block() as block:

            @block.sync
            def _(sp):
                sp.dma_start(rows[:, 0:CT, :], context[0].rearrange("(t p) d -> p t d", p=P)).then_inc(ctx_in, 16)
                sp.dma_start(rows[:, CT:ROWS, :], x1_dram[0].rearrange("(t p) d -> p t d", p=P)).then_inc(lat_in, 16)
                for half in (0, 1):
                    sp.dma_start(sin_sb[:, :, half, :], sin.rearrange("(t p) n -> p t n", p=P)).then_inc(consts_in, 16)
                sp.dma_start(cos_sb[:, :, :], cos.rearrange("(t p) n -> p t n", p=P)).then_inc(consts_in, 16)
                for n, (g_in, b_in) in enumerate(((cg, cb), (lg, lb))):
                    sp.dma_start(gam[:, n, :], g_in.rearrange("(k p) -> p k", p=P), allow_slow_non_contiguous=True
                                 ).then_inc(consts_in, 16)
                    sp.dma_start(bet[:, n, :], b_in.rearrange("(k p) -> p k", p=P), allow_slow_non_contiguous=True
                                 ).then_inc(consts_in, 16)
                sp.dma_start(bo_sb[:, :], bo.partition_broadcast(P)).then_inc(consts_in, 16)

                def load(what, b):
                    dst, src, done = {"context": (rows[:, 0:CT, :], context, ctx_in),
                                      "latents": (rows[:, CT:ROWS, :], x1_dram, lat_in),
                                      "residual": (x1[:, :, :], x1_dram, x1_in)}[what]
                    sp.dma_start(dst, src[bass.ds(b, 1)].rearrange("a (t p) d -> p (a t) d", p=P)).then_inc(done, 16)

                def spread(b, g, p):
                    n = g * PG + p
                    sp.wait_ge(q_ready, b * (2 * PG) + n + 1)
                    for hh in range(2):
                        here, there = slice(hh * HD, (hh + 1) * HD), slice((1 - hh) * HD, (2 - hh) * HD)
                        sp.dma_start(QQ[there, n % 2, hh, :, :].bitcast(F32), QQ[here, n % 2, hh, :, :].bitcast(F32)
                                     ).then_inc(q_spread, 16)

                with sp.Fori(0, S) as b:
                    sp.wait_ge(z_ready, ZB + b * ZN)
                    load("context", (b + 1) % S)
                    sp.wait_ge(stored, b * 16)
                    load("residual", b)
                    sp.wait_ge(z_ready, ZB + b * ZN + KD)
                    load("latents", (b + 1) % S)
                    for g in range(2):
                        for p in range(PG):
                            spread(b, g, p)
                    sp.wait_ge(out_ready, (b + 1) * NT)
                    sp.dma_start(x2_dram[bass.ds(b, 1)].rearrange("a (t p) d -> p (a t) d", p=P), x1[:, :, :]
                                 ).then_inc(stored, 16)
                sp.wait_ge(stored, 16 * S)

            @block.gpsimd
            def _(pool):
                pool.memset(ones[:, :], 1.0).then_inc(consts, 1)
                pool.memset(mhalf[:, :], -0.5).then_inc(consts, 1)
                pool.wait_ge(consts, 2)
                pool.wait_ge(var_ready, 1)
                pool.tensor_tensor(rs[:, :], ve[:, :], mhalf[:, :], ALU.pow).then_inc(rstd_ready, 1)
                pool.wait_ge(consts_in, 16 * 8)
                pool.tensor_scalar(sin_sb[:, :, 0, :], sin_sb[:, :, 0, :], -1.0, None, ALU.mult).then_inc(consts, 1)
                pool.wait_ge(consts, 3)
                pool.sem_inc(consts, 1)
                with pool.Fori(0, S) as b:
                    links = 0
                    for g in range(2):
                        for t in range(CT):
                            pool.wait_ge(kh_ready, b * (2 * CT) + (g * CT + t + 1))
                            nat = knat[:, t % 2, :].rearrange("p (h a n) -> p h a n", a=2, n=HD)
                            pool.tensor_tensor(nat[:, :, 1, :], krot[:, t % 2, :].rearrange("p (h n) -> p h n", n=HD),
                                               nat[:, :, 0, :].bitcast(F32), ALU.subtract).then_inc(knat_ready, 1)
                        if g == 0:
                            pool.wait_ge(x1_in, (b + 1) * 16)
                            pool.tensor_tensor(x1[:, :, :], x1[:, :, :],
                                               bo_sb[:, :].unsqueeze(1).broadcast_to([P, NT, D]), ALU.add
                                               ).then_inc(biased, 1)
                        for p in range(PG):
                            for j in range(3):
                                for hh in range(2):
                                    pool.wait_ge(clipped, b * (16 * PG) + (step(g, p, j) * 2 + hh + 1))
                                    pr = probs[:, at_step(j, hh), :]
                                    if j == 0:
                                        pool.wait_ge(accf_ready, b * (4 * PG) + ((g * PG + p) * 2))
                                        ins = pool.tensor_tensor(acc[:, hh, :], pr[:, 0:B], pr[:, B:2 * B], ALU.add)
                                    else:
                                        ins = pool.tensor_tensor(acc[:, hh, :], acc[:, hh, :], pr[:, 0:B], ALU.add)
                                        links += 1
                                        ins.then_inc(pchain, 1)
                                        pool.wait_ge(pchain, b * (16 * PG // 2) + links)
                                        ins = pool.tensor_tensor(acc[:, hh, :], acc[:, hh, :], pr[:, B:2 * B], ALU.add)
                                    ins.then_inc(acc_ready, 1)
                                    pool.wait_ge(acc_ready, b * (12 * PG) + ((g * PG + p) * 3 + j) * 2 + hh + 1)
                                if (g, p, j) == (1, 0, 0):
                                    pool.wait_ge(var_ready, 2 * b + 2)
                                    pool.tensor_tensor(rs[:, :], ve[:, :], mhalf[:, :], ALU.pow).then_inc(rstd_ready, 1)
                    assert links == 8 * PG
                    pool.wait_ge(var_ready, 2 * b + 3)
                    pool.tensor_tensor(rs[:, 0:NT], ve[:, 0:NT], mhalf[:, 0:NT], ALU.pow).then_inc(rstd_ready, 1)

            def scores(pe, b, g, p, j):
                n = g * PG + p
                for hh in range(2):
                    key = ("s", g, p, j, hh)
                    wait_free(pe, key, b)
                    if j == 0 and hh == 0:
                        pe.wait_ge(q_spread, b * (32 * 2 * PG) + 32 * (n + 1))
                    if p == 0:
                        for a in range(2):
                            wait_drained(pe, ("kt", g, 2 * j + 1, a), b)
                            wait_drained(pe, ("kt", g, 2 * j, a), b)
                    for a in range(2):
                        t = 2 * j + a
                        k = KT[:, 2 * p + hh, t * P:(t + 1) * P]
                        pe.matmul(bank(key, a), k, QQ[:, n % 2, hh, 0, :], start=True, stop=False)
                        mm = pe.matmul(bank(key, a), k, QQ[:, n % 2, hh, 1, :], start=False, stop=True)
                    fill(key, mm)

            def queries(pe, b, g, p):
                key = ("q", g, p)
                wait_free(pe, key, b)
                col = (g * PG + p) * P
                terms = [u for k in range(KD) for u in three_terms(
                    wq[0][:, k * INNER + col:k * INNER + col + P], wq[1][:, k * INNER + col:k * INNER + col + P],
                    lT[0][:, k, :], lT[1][:, k, :])]
                for a, (lhsT, rhs) in enumerate(terms):
                    mm = pe.matmul(bank(key), lhsT, rhs, start=(a == 0), stop=(a == len(terms) - 1))
                fill(key, mm)

            def sums(pe, b, g, p):
                key = ("sum", g, p)
                wait_free(pe, key, b)
                pe.wait_ge(accf_ready, b * (4 * PG) + (g * PG + p + 1) * 2)
                for hh in range(2):
                    mm = pe.matmul(bank(key)[hh * HD:(hh + 1) * HD, :], ones[:, :], accf[:, hh, :],
                                   start=True, stop=True)
                fill(key, mm)

            def keys_values(pe, b, g, t):
                key = ("kv", g, t)
                wait_free(pe, key, b)
                if g == 0 and t in (0, CT // 2):
                    pe.wait_ge(zl_ready, b * ZN + (ZB if t else KD))
                for a, w in enumerate((wk, wv)):
                    n = 0
                    for k in range(KD):
                        c0 = k * INNER + g * HG * HD
                        for lhsT, rhs in three_terms(cT[0][:, k, t * P:(t + 1) * P], cT[1][:, k, t * P:(t + 1) * P],
                                                     w[0][:, c0:c0 + HG * HD], w[1][:, c0:c0 + HG * HD]):
                            mm = pe.matmul(bank(key, a), lhsT, rhs, start=(n == 0), stop=(n == 3 * KD - 1))
                            n += 1
                fill(key, mm)

            def context_turn(pe, c, dst, before):
                k, t0 = block_rows(c)
                pe.wait_ge(normed, before + t0 + 4)
                for a in range(4):
                    mm = pe.transpose(dst[:, a * P:(a + 1) * P], rows[:, t0 + a, k * P:(k + 1) * P], ident[:, :])
                mm.then_inc(cx_turned, 1)

            @block.tensor
            def _(pe):
                for c in range(ZB):
                    context_turn(pe, c, ps[:, 4 + c, :], 0)
                keys_values(pe, 0, 0, 0)
                pe.wait_ge(weights.lo_done, 4)
                with pe.Fori(0, S) as b:
                    def latents_turn(k):
                        key = ("lx", k)
                        wait_free(pe, key, b)
                        if k == 0:
                            pe.wait_ge(normed, (b + 1) * ROWS)
                            pe.wait_ge(z_ready, ZB + b * ZN)
                        for t in range(NT):
                            mm = pe.transpose(bank(key)[:, t * P:(t + 1) * P], rows[:, CT + t, k * P:(k + 1) * P],
                                              ident[:, :])
                        fill(key, mm)

                    def k_turn(g, t):
                        pe.wait_ge(knat_ready, b * (2 * CT) + (g * CT + t + 1))
                        for a in range(2):
                            key = ("kt", g, t, a)
                            wait_free(pe, key, b)
                            for h in range(4 * a, 4 * a + 4):
                                mm = pe.transpose(bank(key)[:, (h - 4 * a) * P:(h - 4 * a + 1) * P].bitcast(F32R),
                                                  knat[:, t % 2, h * 2 * HD:(h + 1) * 2 * HD], identr[:, :])
                            fill(key, mm)

                    for g in range(2):
                        for t in range(CT):
                            if t:
                                keys_values(pe, b, g, t)
                            if g == 0 and t < KD:
                                latents_turn(t)
                            if t == Q0_AT:
                                if g == 0:
                                    pe.wait_ge(zl_ready, ZB + b * ZN + KD)
                                queries(pe, b, g, 0)
                            if t >= 2:
                                k_turn(g, t - 2)
                        scores(pe, b, g, 0, 0)
                        k_turn(g, CT - 2)
                        for p in range(PG):
                            for j in range(4):
                                if j < 3:
                                    scores(pe, b, g, p, j + 1)
                                elif p + 1 < PG:
                                    scores(pe, b, g, p + 1, 0)
                                if (p, j) == (0, 0):
                                    k_turn(g, CT - 1)
                                if j == 0 and p:
                                    sums(pe, b, g, p - 1)
                                if j == 0 and p + 1 < PG:
                                    queries(pe, b, g, p + 1)
                                if g == 1 and j == cx_step(p):
                                    wait_free(pe, ("cx", p), b)
                                    context_turn(pe, p, bank(("cx", p)), (b + 1) * ROWS)
                                key = ("o", g, p)
                                if j == 0:
                                    wait_free(pe, key, b)
                                pe.wait_ge(clipped, b * (16 * PG) + (step(g, p, j) + 1) * 2)
                                for t in (2 * j, 2 * j + 1):
                                    for hh in range(2):
                                        mm = pe.matmul(bank(key)[hh * HD:(hh + 1) * HD, :],
                                                       V[:, t, (2 * p + hh) * HD:(2 * p + hh + 1) * HD],
                                                       probs[:, at_step(j, hh), (t % 2) * B:(t % 2 + 1) * B],
                                                       start=(t == 0), stop=(t == CT - 1))
                                mm.then_inc(pv_done, 1)
                        def project(a, pairs):
                            for t in (2 * a, 2 * a + 1):
                                for p in pairs:
                                    c0 = (g * PG + p) * D
                                    for n, (lhsT, rhs) in enumerate(three_terms(
                                            OT[0][:, p, t * P:(t + 1) * P], OT[1][:, p, t * P:(t + 1) * P],
                                            wo[0][:, c0:c0 + D], wo[1][:, c0:c0 + D])):
                                        mm = pe.matmul(bank(("y", g, a))[:, (t % 2) * D:(t % 2 + 1) * D], lhsT, rhs,
                                                       start=(t % 2 == 0 and p == 0 and n == 0), stop=(p >= PG - 2 and n == 2),
                                                       skip_group_check=True)
                            return mm

                        sums(pe, b, g, PG - 1)
                        keys_values(pe, b + 1 if g == 1 else b, 1 - g, 0)
                        pe.wait_ge(ot_ready, b * (2 * PG) + (g + 1) * PG - 1)
                        for a in range(2):
                            wait_free(pe, ("y", g, a), b)
                            project(a, range(PG - 1))
                        pe.wait_ge(ot_ready, b * (2 * PG) + (g + 1) * PG)
                        for a in range(2):
                            fill(("y", g, a), project(a, [PG - 1]))

            @block.scalar
            def _(act):
                for n in range(4):
                    weights.split_hi(act, n)
                act.wait_ge(consts, NCONST)

                def q_hi(b, g, p):
                    key = ("q", g, p)
                    wait_filled(act, key, b)
                    n = g * PG + p
                    for hh in range(2):
                        own = slice(hh * HD, (hh + 1) * HD)
                        ins = act.activation(QQ[own, n % 2, hh, 0, :], bank(key)[own, :], ACT.Copy)
                    ins.then_inc(qh_ready, 1)

                def o_hi(b, g, p):
                    wait_drained(act, ("o", g, p), b)
                    act.activation(OT[0][:, p, :], o[:, :], ACT.Copy).then_inc(oh_ready, 1)

                def z_split(n, src, which, k, z, hi):
                    act.activation(z, src, ACT.Identity, scale=gam[:, which, k:k + 1],
                                   bias=bet[:, which, k:k + 1]).then_inc(z_ready, 1)
                    act.wait_ge(z_ready, n + 1)
                    act.activation(hi, z, ACT.Copy).then_inc(zh_ready, 1)

                for c in range(ZB):
                    k, t0 = block_rows(c)
                    act.wait_ge(cx_turned, c + 1)
                    z_split(c, ps[:, 4 + c, :], 0, k, probs[:, c, 0:512], cT[0][:, k, t0 * P:(t0 + 4) * P])
                def v_read(b, g, t):
                    key = ("kv", g, t)
                    wait_filled(act, key, b)
                    drain(key, act.activation(V[:, t, :], bank(key, 1), ACT.Copy))

                def k_hi(b, g, t):
                    act.wait_ge(rotated, b * (2 * CT) + (g * CT + t + 1))
                    act.activation(knat[:, t % 2, :].rearrange("p (h a n) -> p h a n", a=2, n=HD)[:, :, 0, :],
                                   krot[:, t % 2, :].rearrange("p (h n) -> p h n", n=HD), ACT.Copy
                                   ).then_inc(kh_ready, 1)

                v_read(0, 0, 0)
                k_hi(0, 0, 0)
                with act.Fori(0, S) as b:
                    def context_split(c):
                        k, t0 = block_rows(c)
                        act.wait_ge(cx_turned, ZB * (b + 1) + c + 1)
                        if c:
                            act.wait_ge(zl_ready, ZB + b * ZN + KD + c)
                        z_split(ZB + b * ZN + KD + c, bank(("cx", c)), 0, k, zc[:, :], cT[0][:, k, t0 * P:(t0 + 4) * P])
                        act.sem_inc(drained[slots.slot(("cx", c))], 1)

                    for g in range(2):
                        def k_turned(t):
                            for a in range(2):
                                key = ("kt", g, t, a)
                                wait_filled(act, key, b)
                                drain(key, act.activation(KT[:, 4 * a:4 * a + 4, t * P:(t + 1) * P],
                                                          bank(key).rearrange("p (h n) -> p h n", n=P), ACT.Copy))

                        for t in range(CT):
                            if t:
                                v_read(b, g, t)
                            if t >= 2:
                                k_turned(t - 2)
                            if g == 0 and t < KD:
                                wait_filled(act, ("lx", t), b)
                                z_split(ZB + b * ZN + t, bank(("lx", t)), 1, t, zl[t], lT[0][:, t, :])
                                act.sem_inc(drained[slots.slot(("lx", t))], 1)
                            if t == Q0_AT:
                                q_hi(b, g, 0)
                            if t:
                                k_hi(b, g, t)
                        for p in range(PG):
                            for j in range(4):
                                for hh in range(2):
                                    key = ("s", g, p, j, hh)
                                    wait_filled(act, key, b)
                                    if (p, j) >= (0, 2):
                                        before = step(g, p, j) - 2
                                        act.wait_ge(pv_done, b * (8 * PG) + before + 1)
                                        if before % 4 == 3:
                                            act.wait_ge(accf_ready, b * (4 * PG) + (before // 4) * 2 + hh + 1)
                                        else:
                                            act.wait_ge(acc_ready, b * (12 * PG)
                                                        + ((before // 4) * 3 + before % 4) * 2 + hh + 1)
                                    ins = act.activation(probs[:, at_step(j, hh), :], both(key), ACT.Exp, scale=SCALE)
                                    drain(key, ins, 2)
                                    if g == 1 and p and (j, hh) == (0, 0):
                                        context_split(p - 1)
                                    if g == 1 and p == PG - 1 and (j, hh) == (2, 0):
                                        context_split(p)
                                if (p, j) == (0, 0):
                                    k_turned(CT - 2)
                                    k_turned(CT - 1)
                                if j == 1 and p + 1 < PG:
                                    q_hi(b, g, p + 1)
                                if j == 3 and p:
                                    o_hi(b, g, p - 1)
                        last = g == 1
                        v_read(b + 1 if last else b, 1 - g, 0)
                        o_hi(b, g, PG - 1)
                        k_hi(b + 1 if last else b, 1 - g, 0)

            @block.vector
            def _(dve):
                LINKS = 2 * (CT + PG) + 2
                made = [0]

                def link(ins, b):
                    made[0] += 1
                    ins.then_inc(dchain, 1)
                    dve.wait_ge(dchain, b * LINKS + made[0])

                def row_sums(t):
                    return dve.bn_stats(st[:, t, :], rows[:, t, :]).then_inc(stats_taken, 1)

                def variances(b, taken):
                    dve.wait_ge(stats_taken, taken)
                    dve.sem_inc(stats_taken, 1)
                    for t in range(ROWS):
                        ins = dve.bn_aggr(mv[:, t, :], st[:, t, :])
                    link(ins, b)
                    dve.tensor_scalar(ve[:, :], mv[:, :, 1], EPS, None, ALU.add).then_inc(var_ready, 1)

                def normalise(t, dst, src, done):
                    dve.tensor_scalar(dst, src, mv[:, t, 0:1], rs[:, t:t + 1], ALU.subtract, ALU.mult).then_inc(done, 1)

                def z_lo(n, z, hi, lo):
                    dve.wait_ge(zh_ready, n + 1)
                    dve.tensor_tensor(lo, z, hi.bitcast(F32), ALU.subtract).then_inc(zl_ready, 1)

                def k_cos(b, g, t):
                    key = ("kv", g, t)
                    wait_filled(dve, key, b)
                    if t >= 2:
                        dve.wait_ge(knat_ready, b * (2 * CT) + (g * CT + t - 1))
                    dve.tensor_tensor(krot[:, t % 2, :].rearrange("p (h n) -> p h n", n=HD // 2),
                                      bank(key).rearrange("p (h n) -> p h n", n=HD // 2),
                                      cos_sb[:, t, :].unsqueeze(1).broadcast_to([P, 2 * HG, HD // 2]), ALU.mult)

                def k_sin(b, g, t, at):
                    key = ("kv", g, t)
                    dve.wait_ge(rotated, b * (2 * CT) + (g * CT + t))
                    link(dve.tensor_tensor(
                        kswap.rearrange("p (h a n) -> p h a n", a=2, n=HD // 2),
                        bank(key).rearrange("p (h a n) -> p h a n", a=2, n=HD // 2)[:, :, ::-1, :],
                        sin_sb[:, t, :, :].unsqueeze(1).broadcast_to([P, HG, 2, HD // 2]), ALU.mult), at)
                    dve.sem_inc(drained[slots.slot(key)], 1)
                    dve.tensor_tensor(krot[:, t % 2, :], krot[:, t % 2, :], kswap, ALU.add).then_inc(rotated, 1)

                weights.split_lo(dve, 0)
                for t in range(ROWS):
                    if t in (0, CT):
                        dve.wait_ge(lat_in if t else ctx_in, 16)
                    row_sums(t)
                variances(0, ROWS)
                weights.split_lo(dve, 1)
                dve.wait_ge(rstd_ready, 1)
                for t in range(ROWS):
                    normalise(t, rows[:, t, :], rows[:, t, :], normed)
                weights.split_lo(dve, 2)
                for c in range(ZB):
                    k, t0 = block_rows(c)
                    cols = slice(t0 * P, (t0 + 4) * P)
                    z_lo(c, probs[:, c, 0:512], cT[0][:, k, cols], cT[1][:, k, cols])
                weights.split_lo(dve, 3)
                dve.wait_ge(consts, NCONST)
                k_cos(0, 0, 0)
                k_sin(0, 0, 0, 0)
                TAKEN = ROWS + 1 + NT + 1
                FIRST = ROWS + 1
                with dve.Fori(0, S) as b:
                    def context_lo(c):
                        k, t0 = block_rows(c)
                        cols = slice(t0 * P, (t0 + 4) * P)
                        z_lo(ZB + b * ZN + KD + c, zc[:, :], cT[0][:, k, cols], cT[1][:, k, cols])

                    for g in range(2):
                        def q_lo(p):
                            key = ("q", g, p)
                            n = g * PG + p
                            dve.wait_ge(qh_ready, b * (2 * PG) + n + 1)
                            for hh in range(2):
                                own = slice(hh * HD, (hh + 1) * HD)
                                ins = dve.tensor_tensor(QQ[own, n % 2, hh, 1, :], bank(key)[own, :],
                                                        QQ[own, n % 2, hh, 0, :].bitcast(F32), ALU.subtract)
                            ins.then_inc(q_ready, 1)
                            dve.wait_ge(q_ready, b * (2 * PG) + n + 1)
                            dve.sem_inc(drained[slots.slot(key)], 2 if p == 0 else 1)

                        for t in range(CT):
                            if t:
                                k_cos(b, g, t)
                                k_sin(b, g, t, b)
                            if g == 0 and t < KD:
                                z_lo(ZB + b * ZN + t, zl[t], lT[0][:, t, :], lT[1][:, t, :])
                            if t == Q0_AT:
                                q_lo(0)
                        def inverse(p, a):
                            key = ("sum", g, p)
                            if a == 0:
                                wait_filled(dve, key, b)
                                if p:
                                    wait_drained(dve, ("o", g, p - 1), b)
                            ins = dve.reciprocal(r[:, a * P:(a + 1) * P], bank(key)[:, a * P:(a + 1) * P])
                            if a == 3:
                                drain(key, ins)

                        def o_scaled(p):
                            wait_drained(dve, ("sum", g, p), b)
                            dve.wait_ge(ot_ready, b * (2 * PG) + (g * PG + p))
                            drain(("o", g, p), dve.tensor_tensor(o[:, :], bank(("o", g, p)), r[:, :], ALU.mult))

                        def o_lo(p):
                            dve.wait_ge(oh_ready, b * (2 * PG) + (g * PG + p + 1))
                            dve.tensor_tensor(OT[1][:, p, :], o[:, :], OT[0][:, p, :].bitcast(F32), ALU.subtract
                                              ).then_inc(ot_ready, 1)

                        for p in range(PG):
                            for j in range(4):
                                for hh in range(2):
                                    n = step(g, p, j) * 2 + hh
                                    at = (j, hh)
                                    pr = probs[:, at_step(j, hh), :]
                                    wait_drained(dve, ("s", g, p, j, hh), b)
                                    dve.tensor_scalar(pr, pr, HI, LO, ALU.min, ALU.max).then_inc(clipped, 1)
                                    if 0 < p < PG - 1 and at == (3, 0):
                                        o_scaled(p - 1)
                                    if j == 3:
                                        for h2 in ((hh,) if p + 1 < PG else (0, 1)[:2 * hh]):
                                            dve.wait_ge(clipped, b * (16 * PG) + n + 1)
                                            e = probs[:, at_step(j, h2), :]
                                            ins = dve.tensor_tensor(accf[:, h2, :], e[:, 0:B], e[:, B:2 * B], ALU.add)
                                        if hh == 1:
                                            link(ins, b)
                                            for h2 in range(2):
                                                dve.wait_ge(acc_ready, b * (12 * PG) + ((g * PG + p) * 3 + 2) * 2 + h2 + 1)
                                                dve.tensor_tensor(accf[:, h2, :], accf[:, h2, :], acc[:, h2, :], ALU.add
                                                                  ).then_inc(accf_ready, 1)
                                    if p:
                                        quarters = {(1, 0): (0,), (2, 0): (1,), (2, 1): (2, 3)}
                                        if p == PG - 1:
                                            quarters = {(1, 0): (0,), (1, 1): (1,), (2, 0): (2,), (2, 1): (3,)}
                                        for a in quarters.get(at, ()):
                                            inverse(p - 1, a)
                                    if p + 1 < PG and at == (1, 1):
                                        q_lo(p + 1)
                                    if p >= 2 and at == (0, 0):
                                        o_lo(p - 2)
                                    if g == 0 and at == (0, 1):
                                        if p == 0:
                                            dve.wait_ge(ctx_in, (b + 2) * 16)
                                            dve.wait_ge(lat_in, (b + 2) * 16)
                                        for t in (2 * p, 2 * p + 1, CT + p):
                                            row_sums(t)
                                    if (g, p) == (1, 0) and at == (0, 1):
                                        variances(b, FIRST + b * TAKEN + ROWS)
                                    if g == 1 and p < 3 and at == (((2, 0), (0, 1), (0, 1))[p]):
                                        if p == 0:
                                            dve.wait_ge(rstd_ready, 2 * b + 2)
                                        for t in range(4 * p, 4 * p + 4):
                                            normalise(t, rows[:, t, :], rows[:, t, :], normed)
                                    if g == 1 and p and at == (0, 1):
                                        context_lo(p - 1)
                        o_scaled(PG - 2)
                        for a in range(4):
                            inverse(PG - 1, a)
                            if a == 0:
                                o_lo(PG - 2)
                        o_scaled(PG - 1)
                        after = b + 1 if g == 1 else b
                        k_cos(after, 1 - g, 0)
                        o_lo(PG - 1)
                        k_sin(after, 1 - g, 0, b)
                        for a in range(2):
                            key = ("y", g, a)
                            wait_filled(dve, key, b)
                            if (g, a) == (0, 0):
                                dve.wait_ge(biased, b + 1)
                            xs = x1[:, 2 * a:2 * a + 2, :].rearrange("p t n -> p (t n)")
                            drain(key, dve.tensor_tensor(xs, bank(key), xs, ALU.add))
                    for a in range(2):
                        wait_drained(dve, ("y", 1, a), b)
                    for t in range(NT):
                        dve.bn_stats(st[:, t, :], x1[:, t, :]).then_inc(stats_taken, 1)
                    dve.wait_ge(stats_taken, FIRST + b * TAKEN + ROWS + 1 + NT)
                    dve.sem_inc(stats_taken, 1)
                    for t in range(NT):
                        ins = dve.bn_aggr(mv[:, t, :], st[:, t, :])
                    link(ins, b)
                    dve.tensor_scalar(ve[:, 0:NT], mv[:, 0:NT, 1], EPS, None, ALU.add).then_inc(var_ready, 1)
                    context_lo(PG - 1)
                    dve.wait_ge(rstd_ready, 2 * b + 3)
                    for t in range(NT):
                        normalise(t, x1[:, t, :], x1[:, t, :], out_ready)
                assert made[0] == LINKS + 2, (made[0], LINKS)


def experts(nc, x2_dram, Wr, rb, W1, W2, W3, Ws1, Ws2, Ws3, out, ident):
    TOK = S * B
    NT, CH, CT = TOK // P, TOK // 512, 4
    HB = FF // P
    RSCALE = 1.0 / math.sqrt(D)
    with ExitStack() as ctx:
        def sb(name, shape, dt=F32):
            return ctx.enter_context(nc.sbuf_tensor(name, shape, dt))

        def sem(name):
            return ctx.enter_context(nc.semaphore(name))

        y = sb("c_y", [P, NT, D])
        xT = [sb(f"c_xT_{n}", [P, KD, TOK], F32R) for n in "hl"]
        w1 = [[sb(f"c_w1_{n}{k}", [P, KD * FF], F32R) for n in "hl"] for k in range(2)]
        w3 = [[sb(f"c_w3_{n}{k}", [P, KD * FF], F32R) for n in "hl"] for k in range(2)]
        w2 = [[sb(f"c_w2_{n}{k}", [P, HB * D], F32R) for n in "hl"] for k in range(2)]
        raw = sb("c_raw", [P, 3, KD * FF])
        hT = [sb(f"c_hT_{n}", [P, 2, HB, 512], F32R) for n in "hl"]
        gate = sb("c_gate", [P, 2, 512])
        hid = sb("c_hid", [P, 2, 512])
        lgT = [gate[0:E, 0, :], gate[0:E, 1, :], hid[0:E, 0, :], hid[0:E, 1, :]]
        wr = sb("c_wr", [P, KD, E])
        wrs = [sb(f"c_wr_{n}", [P, KD, E], F32R) for n in "hl"]
        rb_sb = sb("c_rb", [P, E])
        logit = sb("c_logit", [P, NT, E])
        biased = sb("c_biased", [P, NT, E])
        top = sb("c_top", [P, NT, 8])
        topi = sb("c_topi", [P, NT, 8], U32)
        topf = sb("c_topf", [P, 2, NT])
        lane = sb("c_lane", [P, E])
        hot = sb("c_hot", [P, 2, NT, E])
        pick = sb("c_pick", [P, 2, NT])
        pmax = sb("c_pmax", [P, NT])
        prod = sb("c_prod", [P, NT, E])
        share = sb("c_share", [P, NT, 1 + E])
        mhalf = sb("c_mhalf", [P, CT])
        st = sb("c_st", [P, CT, 6])
        mv = sb("c_mv", [P, CT, 2])
        ve = sb("c_ve", [P, CT])
        rs = sb("c_rs", [P, CT])
        ps = ctx.enter_context(nc.psum_tensor("c_ps", [P, 8, 512], F32))

        x_in = [sem(f"c_x_in{c}") for c in range(CH)]
        consts_in = sem("c_consts_in")
        consts = sem("c_consts")
        raw_in = sem("c_raw_in")
        raw_taken = sem("c_raw_taken")
        w_ready = sem("c_w_ready")
        turned = sem("c_turned")
        xh_ready = sem("c_xh_ready")
        xl_ready = sem("c_xl_ready")
        logitsT_done = sem("c_logitsT_done")
        logitsT_read = sem("c_logitsT_read")
        logits_done = sem("c_logits_done")
        first_hi = sem("c_first_hi")
        logits_read = sem("c_logits_read")
        route_in = sem("c_route_in")
        route_exp = sem("c_route_exp")
        rchain = sem("c_rchain")
        h_filled = [sem(f"c_h_filled{k}") for k in range(2)]
        h_drained = [sem(f"c_h_drained{k}") for k in range(2)]
        y_filled = [sem(f"c_y_filled{k}") for k in range(4)]
        y_drained = [sem(f"c_y_drained{k}") for k in range(4)]
        gated = sem("c_gated")
        hid_ready = sem("c_hid_ready")
        hh_ready = sem("c_hh_ready")
        hl_ready = sem("c_hl_ready")
        var_ready = sem("c_var_ready")
        rstd_ready = sem("c_rstd_ready")
        out_ready = sem("c_out_ready")
        stored = sem("c_stored")
        lchain = sem("c_lchain")

        out_v = out.rearrange("s (t p) d -> s p t d", p=P)
        x2_v = x2_dram.rearrange("s (t p) d -> s p t d", p=P)

        def over_experts(eng, body):
            body(0, 0, True, False)
            with eng.Fori(0, (E - 2) // 2) as i:
                for a in range(2):
                    body(2 * i + (1 + a), 1 - a, False, False)
            for n in range(E - 1, E + 1):
                body(n, n % 2, False, n == E)

        HALF = CH * KD // 2

        def x_bank(n):
            return n if n < HALF else 4 + n % 4

        with nc.Block() as block:

            @block.sync
            def _(sp):
                def load(n, par, first, last):
                    if first:
                        load_x(range(CH // 4))
                        sp.dma_start(wr[:, :, :], Wr.rearrange("(k p) n -> p k n", p=P)).then_inc(consts_in, 16)
                        sp.dma_start(rb_sb[:, :], rb.partition_broadcast(P)).then_inc(consts_in, 16)
                        load_x(range(CH // 4, CH))
                    else:
                        sp.wait_ge(w_ready, 6 * n)
                    if first:
                        srcs = (Ws1, Ws3, Ws2)
                    else:
                        srcs = [w[bass.ds(n - 1, 1)].rearrange("e k n -> (e k) n") for w in (W1, W3, W2)]
                    for m, src in enumerate(srcs):
                        sp.dma_start(raw[:, m, :].rearrange("p (k n) -> p k n", n=src.shape[1]),
                                     src.rearrange("(k p) n -> p k n", p=P)).then_inc(raw_in, 16)

                def load_x(chunks):
                    for c in chunks:
                        sp.dma_start(y[:, c * CT:(c + 1) * CT, :], x2_v[c]).then_inc(x_in[c], 16)

                over_experts(sp, load)
                for c in range(CH):
                    sp.wait_ge(out_ready, CT * (c + 1))
                    sp.dma_start(out_v[c], y[:, c * CT:(c + 1) * CT, :]).then_inc(stored, 16)
                sp.wait_ge(stored, 16 * CH)

            @block.gpsimd
            def _(pool):
                pool.iota(topi[:, 0, :], pattern=[[1, E]], base=0, channel_multiplier=0).then_inc(consts, 1)
                pool.memset(mhalf[:, :], -0.5).then_inc(consts, 1)
                pool.wait_ge(consts, 2)
                pool.tensor_copy(lane[:, :], topi[:, 0, :]).then_inc(consts, 1)
                pool.memset(share[:, :, 0], 1.0)
                pool.wait_ge(consts_in, 32)
                pool.tensor_copy(wrs[0][:, :, :], wr[:, :, :]).then_inc(consts, 1)
                pool.wait_ge(consts, 4)
                pool.tensor_tensor(wrs[1][:, :, :], wr[:, :, :], wrs[0][:, :, :].bitcast(F32), ALU.subtract
                                   ).then_inc(consts, 1)

                def split(n, par, first, last):
                    if first:
                        return
                    pool.wait_ge(raw_in, (n + 1) * 48)
                    pool.wait_ge(y_filled[3], (n - 1) * (CH // 2))
                    pool.sem_inc(raw_taken, 1)
                    for m, w in enumerate((w1, w3, w2)):
                        pool.tensor_copy(w[par][0][:, :], raw[:, m, :]).then_inc(w_ready, 1)
                    for m, w in enumerate((w1, w3, w2)):
                        pool.wait_ge(w_ready, n * 6 + m + 1)
                        pool.tensor_tensor(w[par][1][:, :], raw[:, m, :], w[par][0][:, :].bitcast(F32), ALU.subtract
                                           ).then_inc(w_ready, 1)

                over_experts(pool, split)
                for c in range(CH):
                    pool.wait_ge(var_ready, c + 1)
                    pool.tensor_tensor(rs[:, :], ve[:, :], mhalf[:, :], ALU.pow).then_inc(rstd_ready, 1)

            def second(pe, n, c, par, half):
                k = 2 * (c % 2) + half
                pe.wait_ge(y_drained[k], n * (CH // 2) + c // 2)
                if half == 0:
                    pe.wait_ge(hl_ready, (n * CH + c + 1) * HB)
                for t in (2 * half, 2 * half + 1):
                    a = 0
                    for hb in range(HB):
                        for lhsT, rhs in three_terms(hT[0][:, c % 2, hb, t * P:(t + 1) * P],
                                                     hT[1][:, c % 2, hb, t * P:(t + 1) * P],
                                                     w2[par][0][:, hb * D:(hb + 1) * D],
                                                     w2[par][1][:, hb * D:(hb + 1) * D]):
                            mm = pe.matmul(ps[:, 4 + k, (t % 2) * D:(t % 2 + 1) * D], lhsT, rhs,
                                           start=(a == 0), stop=(a == 3 * HB - 1))
                            a += 1
                mm.then_inc(y_filled[k], 1)

            @block.tensor
            def _(pe):
                def logits(c):
                    terms = [u for k in range(KD) for u in three_terms(
                        wrs[0][:, k, :], wrs[1][:, k, :],
                        xT[0][:, k, c * 512:(c + 1) * 512], xT[1][:, k, c * 512:(c + 1) * 512])]
                    for a, (lhsT, rhs) in enumerate(terms):
                        mm = pe.matmul(ps[0:E, c, :], lhsT, rhs, start=(a == 0), stop=(a == len(terms) - 1))
                    mm.then_inc(logitsT_done, 1)

                for c in range(CH):
                    pe.wait_ge(x_in[c], 16)
                    for k in range(KD):
                        n = c * KD + k
                        if n >= HALF:
                            pe.wait_ge(xl_ready, n - 3)
                        for t in range(CT):
                            mm = pe.transpose(ps[:, x_bank(n), t * P:(t + 1) * P], y[:, c * CT + t, k * P:(k + 1) * P],
                                              ident[:, :])
                        mm.then_inc(turned, 1)
                    if c == CH // 2 - 1:
                        pe.wait_ge(xl_ready, HALF)
                        pe.wait_ge(consts, 5)
                        for early in range(CH // 2):
                            logits(early)
                pe.wait_ge(xl_ready, CH * KD)
                for c in range(CH // 2, CH):
                    logits(c)
                for t in range(NT):
                    c, a = t // CT, t % CT
                    pe.wait_ge(logitsT_read, c + 1)
                    pe.transpose(ps[:, 0, t * E:(t + 1) * E], lgT[c % 4][:, a * P:(a + 1) * P], ident[0:E, 0:E]
                                 ).then_inc(logits_done, 1)
                pe.wait_ge(logits_read, 1)

                def run(n, par, first, last):
                    pe.wait_ge(w_ready, (n + 1) * 6)
                    for c in range(CH):
                        for hb in range(HB):
                            k = hb % 2
                            pe.wait_ge(h_drained[k], (n * CH + c) * (HB // 2) + hb // 2)
                            for m, w in enumerate((w3, w1)):
                                a = 0
                                for kk in range(KD):
                                    c0 = kk * FF + hb * P
                                    for lhsT, rhs in three_terms(w[par][0][:, c0:c0 + P], w[par][1][:, c0:c0 + P],
                                                                 xT[0][:, kk, c * 512:(c + 1) * 512],
                                                                 xT[1][:, kk, c * 512:(c + 1) * 512]):
                                        mm = pe.matmul(ps[:, 2 * k + m, :], lhsT, rhs, start=(a == 0),
                                                       stop=(a == 3 * KD - 1))
                                        a += 1
                            mm.then_inc(h_filled[k], 1)
                            if k == 1 and (c or not first):
                                before = (n, c - 1, par) if c else (n - 1, CH - 1, 1 - par)
                                second(pe, *before, hb // 2)
                    if last:
                        for half in range(2):
                            second(pe, n, CH - 1, par, half)

                over_experts(pe, run)

            @block.scalar
            def _(act):
                for n in range(CH * KD):
                    act.wait_ge(turned, n + 1)
                    act.activation(xT[0][:, n % KD, (n // KD) * 512:(n // KD + 1) * 512], ps[:, x_bank(n), :], ACT.Copy
                                   ).then_inc(xh_ready, 1)
                act.wait_ge(raw_in, 48)
                for m, w in enumerate((w1, w3, w2)):
                    act.activation(w[0][0][:, :], raw[:, m, :], ACT.Copy).then_inc(first_hi, 1)
                for c in range(CH):
                    act.wait_ge(logitsT_done, c + 1)
                    if c >= 4:
                        act.wait_ge(logits_done, (c - 3) * CT)
                    act.activation(lgT[c % 4], ps[0:E, c, :], ACT.Copy, scale=RSCALE
                                   ).then_inc(logitsT_read, 1)

                def run(n, par, first, last):
                    for c in range(CH):
                        u = n * CH + c

                        def hi(hb):
                            act.wait_ge(hid_ready, u * HB + hb + 1)
                            act.activation(hT[0][:, c % 2, hb, :], hid[:, hb % 2, :], ACT.Copy).then_inc(hh_ready, 1)

                        for hb in range(HB):
                            k = hb % 2
                            act.wait_ge(h_filled[k], u * (HB // 2) + hb // 2 + 1)
                            act.activation(gate[:, k, :], ps[:, 2 * k, :], ACT.Silu).then_inc(gated, 1)
                            if hb:
                                hi(hb - 1)
                        hi(HB - 1)
                        if first and c == 3:
                            act.wait_ge(route_in, 1)
                            act.activation(pick[:, :, :], pick[:, :, :], ACT.Exp).then_inc(route_exp, 1)

                over_experts(act, run)

            @block.vector
            def _(dve):
                for n in range(CH * KD):
                    dve.wait_ge(xh_ready, n + 1)
                    cols = slice((n // KD) * 512, (n // KD + 1) * 512)
                    dve.tensor_tensor(xT[1][:, n % KD, cols], ps[:, x_bank(n), :], xT[0][:, n % KD, cols].bitcast(F32),
                                      ALU.subtract).then_inc(xl_ready, 1)
                for m, w in enumerate((w1, w3, w2)):
                    dve.wait_ge(first_hi, m + 1)
                    dve.tensor_tensor(w[0][1][:, :], raw[:, m, :], w[0][0][:, :].bitcast(F32), ALU.subtract
                                      ).then_inc(w_ready, 2)
                dve.wait_ge(logits_done, NT)
                dve.tensor_copy(logit[:, :, :].rearrange("p t e -> p (t e)"), ps[:, 0, 0:NT * E]
                                ).then_inc(logits_read, 1)
                made = [0]

                def routing(part):

                    def link(ins):
                        made[0] += 1
                        ins.then_inc(rchain, 1)
                        dve.wait_ge(rchain, made[0])

                    if part == 0:
                        dve.wait_ge(consts, 5)
                        dve.wait_ge(logits_read, 1)
                        link(dve.tensor_tensor(biased[:, :, :], logit[:, :, :],
                                               rb_sb[:, :].unsqueeze(1).broadcast_to([P, NT, E]), ALU.add))
                        for t in range(NT):
                            ins = dve.max(top[:, t, :], biased[:, t, :])
                        link(ins)
                    if part == 1:
                        for t in range(NT):
                            ins = dve.max_index(topi[:, t, :], top[:, t, :], biased[:, t, :])
                        link(ins)
                        link(dve.tensor_copy(topf[:, :, :], topi[:, :, 0:2].rearrange("p t a -> p a t")))
                        for a in range(2):
                            ins = dve.tensor_tensor(hot[:, a], lane[:, :].unsqueeze(1).broadcast_to([P, NT, E]),
                                                    topf[:, a, :].unsqueeze(2).broadcast_to([P, NT, E]), ALU.is_equal)
                        link(ins)
                    if part == 2:
                        for a in range(2):
                            link(dve.tensor_tensor(prod[:, :, :], hot[:, a], logit[:, :, :], ALU.mult))
                            link(dve.tensor_reduce(pick[:, a, :], prod[:, :, :], AX.X, ALU.add))
                        link(dve.tensor_tensor(pmax[:, :], pick[:, 0, :], pick[:, 1, :], ALU.max))
                        dve.tensor_tensor(pick[:, :, :], pick[:, :, :], pmax[:, :].unsqueeze(1).broadcast_to([P, 2, NT]),
                                          ALU.subtract).then_inc(route_in, 1)
                    if part == 4:
                        dve.wait_ge(route_exp, 1)
                        link(dve.tensor_tensor(pmax[:, :], pick[:, 0, :], pick[:, 1, :], ALU.add))
                        link(dve.reciprocal(pmax[:, :], pmax[:, :]))
                        link(dve.tensor_tensor(pick[:, :, :], pick[:, :, :],
                                               pmax[:, :].unsqueeze(1).broadcast_to([P, 2, NT]), ALU.mult))
                    if part == 5:
                        for a in range(2):
                            link(dve.tensor_tensor(hot[:, a], hot[:, a],
                                                   pick[:, a, :].unsqueeze(2).broadcast_to([P, NT, E]), ALU.mult))
                        link(dve.tensor_tensor(share[:, :, 1:1 + E], hot[:, 0], hot[:, 1], ALU.add))

                def add_up(n, c, half):
                    k = 2 * (c % 2) + half
                    dve.wait_ge(y_filled[k], n * (CH // 2) + c // 2 + 1)
                    for a in range(2):
                        t = c * CT + 2 * half + a
                        src = ps[:, 4 + k, a * D:(a + 1) * D]
                        ins = dve.scalar_tensor_tensor(y[:, t, :], src, share[:, t, bass.ds(n, 1)], y[:, t, :],
                                                       ALU.mult, ALU.add)
                    ins.then_inc(y_drained[k], 1)

                def layer_norm(c):
                    t0 = c * CT
                    for half in range(2):
                        dve.wait_ge(y_drained[2 * (c % 2) + half], E * (CH // 2) + c // 2 + 1)
                    for t in range(CT):
                        ins = dve.bn_stats(st[:, t, :], y[:, t0 + t, :])
                    ins.then_inc(lchain, 1)
                    dve.wait_ge(lchain, 2 * c + 1)
                    for t in range(CT):
                        ins = dve.bn_aggr(mv[:, t, :], st[:, t, :])
                    ins.then_inc(lchain, 1)
                    dve.wait_ge(lchain, 2 * c + 2)
                    dve.tensor_scalar(ve[:, :], mv[:, :, 1], EPS, None, ALU.add).then_inc(var_ready, 1)
                    dve.wait_ge(rstd_ready, c + 1)
                    for t in range(CT):
                        dve.tensor_scalar(y[:, t0 + t, :], y[:, t0 + t, :], mv[:, t, 0:1], rs[:, t:t + 1],
                                          ALU.subtract, ALU.mult).then_inc(out_ready, 1)

                def run(n, par, first, last):
                    for c in range(CH):
                        u = n * CH + c
                        before = (n, c - 1) if c else None if first else (n - 1, CH - 1)

                        def lo(hb):
                            dve.wait_ge(hh_ready, u * HB + hb + 1)
                            dve.tensor_tensor(hT[1][:, c % 2, hb, :], hid[:, hb % 2, :],
                                              hT[0][:, c % 2, hb, :].bitcast(F32), ALU.subtract).then_inc(hl_ready, 1)

                        for hb in range(HB):
                            k = hb % 2
                            dve.wait_ge(gated, u * HB + hb + 1)
                            if hb >= 2 or c or not first:
                                dve.wait_ge(hl_ready, u * HB + hb - 1)
                            dve.tensor_tensor(hid[:, k, :], ps[:, 2 * k + 1, :], gate[:, k, :], ALU.mult
                                              ).then_inc(hid_ready, 1)
                            dve.wait_ge(hid_ready, u * HB + hb + 1)
                            dve.sem_inc(h_drained[k], 1)
                            if hb:
                                lo(hb - 1)
                            if hb == 2 and before:
                                add_up(*before, 0)
                        lo(HB - 1)
                        if before:
                            add_up(*before, 1)
                        if last and c:
                            layer_norm(c - 1)
                        if first:
                            routing(c)
                    if last:
                        for half in range(2):
                            add_up(n, CH - 1, half)
                        layer_norm(CH - 1)

                over_experts(dve, run)


def build(nc, x, ctx_1024, aWkv, abkv, aWq, abq, aWp, abp, cos, sin, lg, lb, cg, cb, xWq, xWkv, xWo, xbo,
          Wr, rb, W1, W2, W3, Ws1, Ws2, Ws3, out, upto="abc", x1_out=None, x2_out=None):
    x1_dram = x1_out if x1_out is not None else nc.dram_tensor("x1", (S, B, D), F32, kind="Internal").ap()
    with ExitStack() as ctx:
        ident = ctx.enter_context(nc.sbuf_tensor("ident", [P, P], F32))
        identr = ctx.enter_context(nc.sbuf_tensor("identr", [P, P], F32R))
        identb = ctx.enter_context(nc.sbuf_tensor("identb", [P, P], BF16))
        made = ctx.enter_context(nc.semaphore("ident_made"))
        with nc.Block() as block:

            @block.gpsimd
            def _(pool):
                pool.memset(ident[:, :], 0.0).then_inc(made, 1)
                pool.wait_ge(made, 1)
                pool.affine_select(out=ident[:, :], in_=ident[:, :], compare_op=ALU.not_equal, fill=1.0, base=0,
                                   pattern=[[-1, P]], channel_multiplier=1).then_inc(made, 1)
                pool.wait_ge(made, 2)
                pool.tensor_copy(identr[:, :], ident[:, :]).then_inc(made, 1)
                pool.tensor_copy(identb[:, :], ident[:, :]).then_inc(made, 1)

        x2_dram = x2_out if x2_out is not None else nc.dram_tensor("x2", (S, B, D), F32, kind="Internal").ap()
        with ExitStack() as attention:
            raw = attention.enter_context(nc.sbuf_tensor("raw", [P, 4, 2048], F32))
            loaded = [[attention.enter_context(nc.semaphore(f"{name}_w_loaded{n}")) for n in range(4)] for name in "ab"]

            def load_next(sp):
                if "b" in upto:
                    load_weights(sp, weight_views(xWq, xWkv, xWo), raw, loaded[1])

            if "a" in upto:
                self_attention(nc, x, aWkv, abkv, aWq, abq, aWp, abp, x1_dram, ident, identb, raw, loaded[0], load_next)
            else:
                with nc.Block() as block:

                    @block.sync
                    def _(sp):
                        load_next(sp)

            if "b" in upto:
                cross_attention(nc, x1_dram, ctx_1024, cos, sin, lg, lb, cg, cb, xbo, x2_dram, ident, identr, raw,
                                loaded[1])
        if "c" in upto:
            experts(nc, x2_dram, Wr, rb, W1, W2, W3, Ws1, Ws2, Ws3, out, ident)


_INS = ['x', 'ctx_1024', 'L0_attn_Wkv', 'L0_attn_bkv', 'L0_attn_Wq', 'L0_attn_bq', 'L0_attn_Wp', 'L0_attn_bp',
        'L0_xattn_cos', 'L0_xattn_sin', 'L0_xattn_ln_lat_g', 'L0_xattn_ln_lat_b', 'L0_xattn_ln_ctx_g',
        'L0_xattn_ln_ctx_b', 'L0_xattn_Wq', 'L0_xattn_Wkv', 'L0_xattn_Wo', 'L0_xattn_bo', 'L0_ffn_Wr', 'L0_ffn_rb',
        'L0_ffn_W1', 'L0_ffn_W2', 'L0_ffn_W3', 'L0_ffn_Ws1', 'L0_ffn_Ws2', 'L0_ffn_Ws3']
_OUTS = [((S, B, D), 'float32')]


def kernel(**inputs):
    import numpy as _np
    import concourse.bacc as _bacc
    from concourse import mybir as _mybir
    from concourse.bass_utils import run_bass_kernel_spmd as _run

    nc = _bacc.Bacc("TRN2", target_bir_lowering=False, num_devices=1, dynamic_dma_scratch_size=1024)
    arrays, args = {}, []
    for name in _INS:
        a = _np.ascontiguousarray(inputs[name])
        arrays[f"in_{name}_dram"] = a
        args.append(nc.dram_tensor(f"in_{name}_dram", a.shape, _mybir.dt.from_np(a.dtype), kind="ExternalInput").ap())
    for i, (shape, dtype) in enumerate(_OUTS):
        dt = _mybir.dt.from_np(_np.dtype(dtype))
        args.append(nc.dram_tensor(f"out_{i}_dram", shape, dt, kind="ExternalOutput").ap())
    build(nc, *args)
    r = _run(nc, [arrays], core_ids=[0])
    return r.results[0]["out_0_dram"]
```
